# Optimizing a Trainium2 kernel written in Bass

```python
import numpy as np
import jax
import jax.numpy as jnp

def _softmax(x, axis=-1):
    return jax.nn.softmax(x, axis=axis)

def _gelu(x):
    return jax.nn.gelu(x, approximate=True)

def _silu(x):
    return jax.nn.silu(x)

def _sigmoid(x):
    return jax.nn.sigmoid(x)

def _layernorm(x, axis=-1, eps=1e-05):
    m = jnp.mean(x, axis=axis, keepdims=True)
    v = jnp.var(x, axis=axis, keepdims=True)
    return (x - m) / jnp.sqrt(v + eps)

def _scatter_add(tgt, idx, src, axis=0):
    return tgt.at[idx].add(src)

def _segment_sum(src, seg, n):
    return jax.ops.segment_sum(src, seg, n)
kernel_name = 'mk_xattn_ffn_d1_seqx_r4_429465'

def setup_inputs(seed: int=0):
    np.random.seed(seed)
    _w = jnp.asarray

    def _rec_inputs():
        import jax
        import jax.numpy as jnp
        _rk = jax.random.key(seed)
        x = 7.22e-05 + 1 * jax.random.normal(jax.random.fold_in(_rk, 1), (32, 256, 256), jnp.float32)
        _lenS = 256 - jax.random.randint(jax.random.fold_in(_rk, 7), (32,), 0, max(1, 256 // 4) + 1, jnp.int32)
        _lenS2 = 256 - jax.random.randint(jax.random.fold_in(_rk, 8), (32,), 0, max(1, 256 // 4) + 1, jnp.int32)
        _ctx_1024P = jax.random.normal(jax.random.fold_in(_rk, 11), (32, 16, 256), jnp.float32)
        _ctx_1024c = jax.random.dirichlet(jax.random.fold_in(_rk, 511), 0.3 * jnp.ones((16,), jnp.float32), (32, 256))
        _ctx_1024t = jnp.einsum('bsk,bkd->bsd', _ctx_1024c, _ctx_1024P)
        _ctx_1024t = _ctx_1024t * jax.lax.rsqrt(jnp.mean(jnp.square(_ctx_1024t)) + 1e-12) * 0.953939
        ctx_1024 = 4.13588e-05 + 0.999923 * (_ctx_1024t + 0.3 * jax.random.normal(jax.random.fold_in(_rk, 611), (32, 256, 256), jnp.float32))
        return (x, ctx_1024)
    x, ctx_1024 = _rec_inputs()

    def _L0_xattn_setup():
        import jax, jax.numpy as jnp
        import numpy as np
        D_MODEL = 256
        HEADS = 16
        D_K = D_MODEL // HEADS
        key = jax.random.key(seed)
        ks = jax.random.split(key, 11)
        B, S = (4, 512)
        scale = 1.0 / np.sqrt(D_MODEL)
        return {'q': jax.random.normal(ks[0], (B, S, D_MODEL), jnp.float32), 'k': jax.random.normal(ks[1], (B, S, D_MODEL), jnp.float32), 'v': jax.random.normal(ks[2], (B, S, D_MODEL), jnp.float32), 'wq': jax.random.normal(ks[3], (D_MODEL, D_MODEL), jnp.float32) * scale, 'bq': jax.random.normal(ks[4], (D_MODEL,), jnp.float32) * 0.01, 'wk': jax.random.normal(ks[5], (D_MODEL, D_MODEL), jnp.float32) * scale, 'bk': jax.random.normal(ks[6], (D_MODEL,), jnp.float32) * 0.01, 'wv': jax.random.normal(ks[7], (D_MODEL, D_MODEL), jnp.float32) * scale, 'bv': jax.random.normal(ks[8], (D_MODEL,), jnp.float32) * 0.01, 'wo': jax.random.normal(ks[9], (D_MODEL, D_MODEL), jnp.float32) * scale, 'bo': jax.random.normal(ks[10], (D_MODEL,), jnp.float32) * 0.01}
    _L0_xattn_all = _L0_xattn_setup()
    _L0_xattn_in = {k: v for k, v in _L0_xattn_all.items() if k in ('wq', 'bq', 'wk', 'bk', 'wv', 'bv', 'wo', 'bo')}
    del _L0_xattn_all

    def _L0_ffn_setup():
        import jax, jax.numpy as jnp
        import numpy as np
        DIM = 256
        HID = 512
        E = 8
        K = 2
        R = 16
        B_, S_ = (2, 256)

        def _lora_in(xf, W, b, A, B):
            base = jnp.einsum('td,ehd->teh', xf, W)
            low = jnp.einsum('ter,ehr->teh', jnp.einsum('td,erd->ter', xf, A), B)
            return base + low + b

        def _lora_out(g, W, b, A, B):
            base = jnp.einsum('teh,edh->ted', g, W)
            low = jnp.einsum('ter,edr->ted', jnp.einsum('teh,erh->ter', g, A), B)
            return base + low + b
        key = jax.random.key(seed)
        ks = jax.random.split(key, 14)
        n = lambda k, shape, scale: jax.random.normal(k, shape, jnp.float32) * scale
        inp = {'x': jax.random.normal(ks[0], (B_, S_, DIM), jnp.float32), 'Wg': n(ks[1], (E, DIM), DIM ** (-0.5)), 'W1': n(ks[2], (E, HID, DIM), DIM ** (-0.5)), 'b1': jnp.zeros((E, HID), jnp.float32), 'A1': n(ks[3], (E, R, DIM), DIM ** (-0.5)), 'B1': n(ks[4], (E, HID, R), 0.01), 'W2': n(ks[5], (E, DIM, HID), HID ** (-0.5)), 'b2': jnp.zeros((E, DIM), jnp.float32), 'A2': n(ks[6], (E, R, HID), HID ** (-0.5)), 'B2': n(ks[7], (E, DIM, R), 0.01), 'W3': n(ks[8], (E, HID, DIM), DIM ** (-0.5)), 'b3': jnp.zeros((E, HID), jnp.float32), 'A3': n(ks[9], (E, R, DIM), DIM ** (-0.5)), 'B3': n(ks[10], (E, HID, R), 0.01)}
        return inp
    _L0_ffn_all = _L0_ffn_setup()
    _L0_ffn_in = {k: v for k, v in _L0_ffn_all.items() if k in ('Wg', 'W1', 'b1', 'A1', 'B1', 'W2', 'b2', 'A2', 'B2', 'W3', 'b3', 'A3', 'B3')}
    del _L0_ffn_all
    return {'x': x, 'ctx_1024': ctx_1024, 'L0_xattn_wq': _L0_xattn_in['wq'], 'L0_xattn_bq': _L0_xattn_in['bq'], 'L0_xattn_wk': _L0_xattn_in['wk'], 'L0_xattn_bk': _L0_xattn_in['bk'], 'L0_xattn_wv': _L0_xattn_in['wv'], 'L0_xattn_bv': _L0_xattn_in['bv'], 'L0_xattn_wo': _L0_xattn_in['wo'], 'L0_xattn_bo': _L0_xattn_in['bo'], 'L0_ffn_Wg': _L0_ffn_in['Wg'], 'L0_ffn_W1': _L0_ffn_in['W1'], 'L0_ffn_b1': _L0_ffn_in['b1'], 'L0_ffn_A1': _L0_ffn_in['A1'], 'L0_ffn_B1': _L0_ffn_in['B1'], 'L0_ffn_W2': _L0_ffn_in['W2'], 'L0_ffn_b2': _L0_ffn_in['b2'], 'L0_ffn_A2': _L0_ffn_in['A2'], 'L0_ffn_B2': _L0_ffn_in['B2'], 'L0_ffn_W3': _L0_ffn_in['W3'], 'L0_ffn_b3': _L0_ffn_in['b3'], 'L0_ffn_A3': _L0_ffn_in['A3'], 'L0_ffn_B3': _L0_ffn_in['B3']}

def reference(x, ctx_1024, L0_xattn_wq, L0_xattn_bq, L0_xattn_wk, L0_xattn_bk, L0_xattn_wv, L0_xattn_bv, L0_xattn_wo, L0_xattn_bo, L0_ffn_Wg, L0_ffn_W1, L0_ffn_b1, L0_ffn_A1, L0_ffn_B1, L0_ffn_W2, L0_ffn_b2, L0_ffn_A2, L0_ffn_B2, L0_ffn_W3, L0_ffn_b3, L0_ffn_A3, L0_ffn_B3):
    import jax
    import jax.numpy as jnp

    def _L0_xattn_ref(q, k, v, wq, bq, wk, bk, wv, bv, wo, bo):
        import jax, jax.numpy as jnp
        import numpy as np
        D_MODEL = 256
        HEADS = 16
        D_K = D_MODEL // HEADS
        B, S, _ = q.shape
        qp = q @ wq.T + bq
        kp = k @ wk.T + bk
        vp = v @ wv.T + bv

        def split_heads(x):
            return x.reshape(B, S, HEADS, D_K).transpose(0, 2, 1, 3)
        qh, kh, vh = (split_heads(qp), split_heads(kp), split_heads(vp))
        scores = jnp.einsum('bhsd,bhtd->bhst', qh, kh) / jnp.sqrt(jnp.float32(D_K)).astype(qh.dtype)
        attn = jax.nn.softmax(scores, axis=-1)
        ctx = jnp.einsum('bhst,bhtd->bhsd', attn, vh)
        ctx = ctx.transpose(0, 2, 1, 3).reshape(B, S, D_MODEL)
        return ctx @ wo.T + bo

    def _L0_ffn_ref(x, Wg, W1, b1, A1, B1, W2, b2, A2, B2, W3, b3, A3, B3):
        import jax, jax.numpy as jnp
        import numpy as np
        DIM = 256
        HID = 512
        E = 8
        K = 2
        R = 16
        B_, S_ = (2, 256)

        def _lora_in(xf, W, b, A, B):
            base = jnp.einsum('td,ehd->teh', xf, W)
            low = jnp.einsum('ter,ehr->teh', jnp.einsum('td,erd->ter', xf, A), B)
            return base + low + b

        def _lora_out(g, W, b, A, B):
            base = jnp.einsum('teh,edh->ted', g, W)
            low = jnp.einsum('ter,edr->ted', jnp.einsum('teh,erh->ter', g, A), B)
            return base + low + b
        orig_shape = x.shape
        xf = x.reshape(-1, x.shape[-1])
        scores = jax.nn.softmax(xf @ Wg.T, axis=-1)
        expert_weights, expert_indices = jax.lax.top_k(scores, K)
        expert_weights = expert_weights / expert_weights.sum(-1, keepdims=True)
        gates = (jax.nn.one_hot(expert_indices, E, dtype=xf.dtype) * expert_weights[..., None]).sum(axis=1)
        h1 = _lora_in(xf, W1, b1, A1, B1)
        h3 = _lora_in(xf, W3, b3, A3, B3)
        g = jax.nn.silu(h1) * h3
        y_e = _lora_out(g, W2, b2, A2, B2)
        y = jnp.einsum('te,ted->td', gates, y_e)
        return y.reshape(orig_shape)
    x = x + _L0_xattn_ref(_layernorm(x, axis=-1), ctx_1024, ctx_1024, L0_xattn_wq, L0_xattn_bq, L0_xattn_wk, L0_xattn_bk, L0_xattn_wv, L0_xattn_bv, L0_xattn_wo, L0_xattn_bo)
    x = x + _L0_ffn_ref(_layernorm(x, axis=-1), L0_ffn_Wg, L0_ffn_W1, L0_ffn_b1, L0_ffn_A1, L0_ffn_B1, L0_ffn_W2, L0_ffn_b2, L0_ffn_A2, L0_ffn_B2, L0_ffn_W3, L0_ffn_b3, L0_ffn_A3, L0_ffn_B3)
    return x

_drawn_inputs = setup_inputs


def setup_inputs(seed=0):
    import zlib

    import numpy as np

    out = dict(_drawn_inputs(seed))
    spreads = {'L0_ffn_b1': (0.0, 0.1), 'L0_ffn_b2': (0.0, 0.1), 'L0_ffn_b3': (0.0, 0.1)}
    factors = {'L0_xattn_bq': 4.651,
     'L0_xattn_bk': 8.0,
     'L0_xattn_bo': 2.876,
     'L0_ffn_A1': 3.716,
     'L0_ffn_B1': 3.756,
     'L0_ffn_A2': 3.846,
     'L0_ffn_B2': 3.843,
     'L0_ffn_A3': 3.901,
     'L0_ffn_B3': 3.86}
    for name, (base, spread) in spreads.items():
        noise = np.random.default_rng([zlib.crc32(name.encode()), seed]).standard_normal(out[name].shape)
        drawn = base * np.exp(spread * noise) if base else spread * noise
        out[name] = jnp.asarray(drawn.astype(out[name].dtype))
    for name, factor in factors.items():
        out[name] = (out[name] * factor).astype(out[name].dtype)
    return out
```

```python
from contextlib import ExitStack

import concourse.bass as bass
from concourse import mybir

F32 = mybir.dt.float32
BF16 = mybir.dt.bfloat16
U32 = mybir.dt.uint32
ALU = mybir.AluOpType
ACT = mybir.ActivationFunctionType
AX_X = mybir.AxisListType.X

P = 128
D = 256
KC = D // P
HEADS = 16
DH = D // HEADS
HID = 512
MC = HID // P
EXPERTS = 8
RANK = 16
EPS = 1e-5
SCALE = DH ** -0.5

TOK = 512
TT = TOK // P
UNITS = 6

MAX_ROW = 97
STACK_ROWS = 99

LAG = 8
SLOTS = 32
E_RING = 8
STACK_DMAS = 8


def halves_matmul(pe, out, lhs, rhs, first, last):
    lhs_hi, lhs_lo = lhs
    rhs_hi, rhs_lo = rhs
    pe.matmul(out, lhs_hi, rhs_hi, start=first, stop=False)
    pe.matmul(out, lhs_lo, rhs_hi, start=False, stop=False)
    return pe.matmul(out, lhs_hi, rhs_lo, start=False, stop=last)


def prepare_weights(nc, t, dram, wq_sb, NB):
    with ExitStack() as ctx:
        sb = lambda n, s, d: ctx.enter_context(nc.sbuf_tensor(n, s, d))
        sem = lambda n: ctx.enter_context(nc.semaphore(n))
        w_in = [sb(f"w_in{k}", [P, UNITS, 512], F32) for k in range(2)]
        a_in = [sb(f"a_in{k}", [P, D + D + HID], F32) for k in range(2)]
        b_in = [sb(f"b_in{k}", [P, HID + HID + D], F32) for k in range(2)]
        w_sum = [sb(f"w_sum{k}", [P, UNITS, 512], F32) for k in range(2)]
        w_out = [sb(f"w_out{k}", [P, 2, UNITS, 512], BF16) for k in range(2)]
        proj_in = sb("proj_in", [P, 4 * KC * D], F32)
        low = [ctx.enter_context(nc.psum_tensor(f"low{k}", [P, 512], F32)) for k in range(2)]

        zeroed = sem("zeroed")
        loaded = [sem(f"prep_loaded{k}") for k in range(2)]
        proj_loaded = sem("proj_loaded")
        proj_hi = sem("proj_hi")
        low_ready = sem("low_ready")
        sum_ready = sem("sum_ready")
        hi_ready = sem("prep_hi_ready")
        lo_ready = sem("prep_lo_ready")
        stored = [sem(f"prep_stored{k}") for k in range(2)]
        LOADS = 3 + 3 + 3

        block = ctx.enter_context(nc.Block())

        @block.sync
        def _(sp):
            sp.dma_start(proj_in[:], dram["w_qkvo"]).then_inc(proj_loaded, 16)
            sp.wait_ge(zeroed, 1)
            with sp.Fori(0, EXPERTS // 2) as i:
                for k in range(2):
                    e = i * 2 + k
                    sp.wait_ge(lo_ready, e * UNITS + UNITS)
                    for n, name in enumerate(("w1", "w3", "w2")):
                        sp.dma_start(w_in[k][:, 2 * n:2 * n + 2, :], dram[name][e]).then_inc(loaded[k], 16)
                    at = 0
                    for name, width in (("a1", D), ("a3", D), ("a2", HID)):
                        sp.dma_start(a_in[k][0:RANK, at:at + width], dram[name][e]).then_inc(loaded[k], 16)
                        at += width
                    at = 0
                    for name, width in (("b1", HID), ("b3", HID), ("b2", D)):
                        sp.dma_start(b_in[k][0:RANK, at:at + width], dram[name][e]).then_inc(loaded[k], 16)
                        at += width

        @block.gpsimd
        def _(pool):
            for k in range(2):
                pool.memset(a_in[k][:], 0.0)
                ins = pool.memset(b_in[k][:], 0.0)
            ins.then_inc(zeroed, 1)
            pool.sem_inc(lo_ready, 2 * UNITS)
            pool.wait_ge(proj_hi, 1)
            pool.tensor_tensor(wq_sb["lo"][:], proj_in[:], wq_sb["hi"][:], ALU.subtract).then_inc(proj_hi, 1)
            with pool.Fori(0, EXPERTS // 2) as i:
                for k in range(2):
                    e = i * 2 + k
                    for u in range(UNITS):
                        pool.wait_ge(hi_ready, e * UNITS + u + 1)
                        pool.tensor_tensor(w_out[k][:, 1, u, :], w_sum[k][:, u, :], w_out[k][:, 0, u, :],
                                           ALU.subtract).then_inc(lo_ready, 1)

        @block.tensor
        def _(pe):
            pe.wait_ge(zeroed, 1)
            with pe.Fori(0, EXPERTS // 2) as i:
                for k in range(2):
                    e = i * 2 + k
                    pe.wait_ge(loaded[k], (i + 1) * 16 * LOADS)
                    for u in range(UNITS):
                        pe.wait_ge(sum_ready, e * UNITS + u + 1)
                        if u < 4:
                            pe.matmul(low[u % 2][:], a_in[k][:, u * P:(u + 1) * P],
                                      b_in[k][:, (u // 2) * HID:(u // 2 + 1) * HID],
                                      start=True, stop=True).then_inc(low_ready, 1)
                        else:
                            for half in range(2):
                                c = 2 * D + (2 * (u - 4) + half) * P
                                ins = pe.matmul(low[u % 2][:, half * D:(half + 1) * D], a_in[k][:, c:c + P],
                                                b_in[k][:, 2 * HID:2 * HID + D], start=True, stop=True)
                            ins.then_inc(low_ready, 1)

        @block.vector
        def _(dve):
            dve.sem_inc(sum_ready, 2)
            with dve.Fori(0, EXPERTS // 2) as i:
                for k in range(2):
                    e = i * 2 + k
                    dve.wait_ge(lo_ready, e * UNITS + UNITS)
                    for u in range(UNITS):
                        dve.wait_ge(low_ready, e * UNITS + u + 1)
                        dve.tensor_tensor(w_sum[k][:, u, :], low[u % 2][:], w_in[k][:, u, :],
                                          ALU.add).then_inc(sum_ready, 1)

        @block.scalar
        def _(act):
            act.wait_ge(proj_loaded, 16)
            act.copy(wq_sb["hi"][:], proj_in[:]).then_inc(proj_hi, 1)
            for k in range(2):
                act.sem_inc(stored[k], 16)
            with act.Fori(0, EXPERTS // 2) as i:
                for k in range(2):
                    e = i * 2 + k
                    act.wait_ge(stored[k], i * 16 + 16)
                    for u in range(UNITS):
                        act.wait_ge(sum_ready, e * UNITS + u + 3)
                        act.copy(w_out[k][:, 0, u, :], w_sum[k][:, u, :]).then_inc(hi_ready, 1)
                    act.wait_ge(lo_ready, e * UNITS + 3 * UNITS)
                    act.dma_start(dram["experts"][e], w_out[k][:]).then_inc(stored[k], 16)
            for k in range(2):
                act.wait_ge(stored[k], 16 * (EXPERTS // 2 + 1))
            act.wait_ge(proj_hi, 2)


def attention(nc, t, dram, wq_sb, NB):
    with ExitStack() as ctx:
        sb = lambda n, s, d: ctx.enter_context(nc.sbuf_tensor(n, s, d))
        pb = lambda n, s, d: ctx.enter_context(nc.psum_tensor(n, s, d))
        sem = lambda n: ctx.enter_context(nc.semaphore(n))

        x_in = [sb(f"x_in{k}", [P, TT, D], F32) for k in range(2)]
        x_res = [sb(f"x_res{k}", [P, TT, D], F32) for k in range(2)]
        xn = sb("xn", [P, TT, D], F32)
        stats = sb("stats", [P, TT, 6], F32)
        mean_var = sb("mean_var", [P, TT, 2], F32)
        rstd = sb("rstd", [P, TT], F32)
        xt_hi = sb("xt_hi", [P, KC, TOK], BF16)
        xt_lo = sb("xt_lo", [P, KC, TOK], BF16)
        ctx_in = [sb(f"ctx_in{k}", [P, KC, TOK], F32) for k in range(2)]
        ct_hi = sb("ct_hi", [P, KC, TOK], BF16)
        ct_lo = sb("ct_lo", [P, KC, TOK], BF16)
        qk = sb("qk", [P, KC, 4, TOK], BF16)
        stack = [sb(f"stack{k}", [P, HEADS, 2, TOK], BF16) for k in range(2)]
        vals = [sb(f"vals{k}", [P, TT, HEADS, 32], F32) for k in range(2)]
        expo = sb("expo", [P, E_RING, 2, D], F32)
        maxes = sb("maxes", [P, TT, HEADS], F32)
        negmax = sb("negmax", [HEADS, 2, TOK], BF16)
        sums_t = [sb(f"sums_t{k}", [P, 2, D], F32) for k in range(2)]
        inverse = sb("inverse", [P, 2, 16], F32)
        heads_n = sb("heads_n", [P, TT, HEADS, DH], F32)
        ht_hi = sb("ht_hi", [P, KC, TOK], BF16)
        ht_lo = sb("ht_lo", [P, KC, TOK], BF16)
        bias_o = sb("bias_o", [P, D], F32)
        power = sb("power", [P, TT], F32)
        hold = sb("hold", [P, 1], F32)
        var_eps = sb("var_eps", [P, TT], F32)
        x1 = [sb(f"x1_{k}", [P, TT, D], F32) for k in range(2)]
        bias_qk = sb("bias_qk", [P, 2, KC], F32)
        bias_v = sb("bias_v", [P, D], F32)
        ident = sb("ident", [P, P], F32)
        ones = sb("ones", [P, P], F32)

        st_bank = [pb(f"st_bank{k}", [P, 2, D], F32) for k in range(2)]
        s_bank = [pb(f"s_bank{k}", [P, 2, D], F32) for k in range(2)]
        pv_bank = [pb(f"pv_bank{k}", [P, 2, D], F32) for k in range(2)]
        bank = [pb(f"bank{k}", [P, 512], F32) for k in range(2)]

        loaded = sem("const_loaded")
        const = sem("const_ready")
        ident_ready = sem("ident_ready")
        x_loaded = [sem(f"x_loaded{k}") for k in range(2)]
        ctx_loaded = [sem(f"ctx_loaded{k}") for k in range(2)]
        res_loaded = [sem(f"res_loaded{k}") for k in range(2)]
        ln_step = sem("ln_step")
        xn_ready = sem("xn_ready")
        ct_hi_ready = sem("ct_hi_ready")
        ct_lo_ready = sem("ct_lo_ready")
        bank_ready = sem("bank_ready")
        bank_free = sem("bank_free")
        hi_ready = sem("hi_ready")
        unstacked = sem("unstacked")
        stacked = sem("stacked")
        st_ready = sem("st_ready")
        exp_done = sem("exp_done")
        s_ready = sem("s_ready")
        max_done = sem("max_done")
        pv_done = sem("pv_done")
        cleared = sem("cleared")
        sums_ready = sem("sums_ready")
        inverse_ready = sem("inverse_ready")
        var_ready = sem("var_ready")
        rstd_ready = sem("rstd_ready")
        res_ready = sem("res_ready")
        ht_hi_ready = sem("ht_hi_ready")
        negmax_ready = sem("negmax_ready")
        negmax_stacked = sem("negmax_stacked")
        x1_stored = [sem(f"x1_stored{k}") for k in range(2)]

        FIRST, EACH = 17, 17
        IN_0, MAX_0, IN_1 = 0, 8, 9

        def fills(q):
            if isinstance(q, int) and q == NB - 2:
                s = FIRST + EACH * q
                return dict(start=s, sums=[s, s + 1, s + 2, s + 3], max=s + 4, turn=s + 5, out=s + 7)
            if isinstance(q, int) and q == NB - 1:
                s = FIRST + EACH * (q - 1) + 9
                return dict(start=s, sums=[s, s + 1, s + 2, s + 3], turn=s + 4, out=s + 6)
            s = FIRST + EACH * q
            return dict(start=s, sums=[s, s + 1, s + 2, s + 3], proj=s + 4, max=s + 10, turn=s + 11,
                        v=s + 13, out=s + 15)

        def bank_of(q, k, step, n=None):
            at = fills(q if isinstance(q, int) else k)[step]
            return (at if n is None else at[n]) % 2

        block = ctx.enter_context(nc.Block())

        def steady(engine, first, step, last):
            first()
            with engine.Fori(0, (NB - 2) // 2) as i:
                for k in range(2):
                    step(i * 2 + k, k)
            for q in range(NB - 2, NB):
                step(q, q % 2)
            last()

        def is_last(q, back):
            return isinstance(q, int) and q >= NB - back

        @block.sync
        def _(sp):
            sp.dma_start(bias_qk[:], dram["bias_qk"]).then_inc(loaded, 16)
            sp.dma_start(bias_v[:], dram["bias_v"].partition_broadcast(P)).then_inc(loaded, 16)
            sp.dma_start(bias_o[:], dram["bias_o"].partition_broadcast(P)).then_inc(loaded, 16)

            def load(p, k):
                sp.dma_start(x_in[k][:], dram["x"][p]).then_inc(x_loaded[k], 16)
                sp.dma_start(ctx_in[k][:], dram["ctx"][p]).then_inc(ctx_loaded[k], 16)

            def stack_inputs(p, k, proj):
                sp.wait_ge(bank_free, proj + 6 + 2)
                for c in range(KC):
                    sp.dma_start(dram["qk"][k, c], qk[:, c]).then_inc(unstacked, 16)
                sp.wait_ge(unstacked, 16 * KC * (p + 1))
                for u in range(4):
                    for side, half in ((0, u // 2), (1, u % 2)):
                        sp.dma_start(stack[k][DH * u:DH * u + DH, :, side, :],
                                     dram["qk_by_row"][k, 2 * side + half]).then_inc(stacked, 16)

            def stack_max(k, fill):
                sp.wait_ge(bank_free, fill + 1 + 2)
                for n in range(2):
                    sp.dma_start(stack[k][MAX_ROW + n:MAX_ROW + n + 1, :, 0, :], negmax[:, n, :])\
                        .then_inc(negmax_stacked, 16)

            for k in range(2):
                sp.sem_inc(x1_stored[k], 16)

            def first():
                load(0, 0)
                load(1, 1)
                sp.wait_ge(const, 1)
                stack_inputs(0, 0, IN_0)
                stack_max(0, MAX_0)
                stack_inputs(1, 1, IN_1)

            def step(q, k):
                f = fills(q)
                sp.wait_ge(bank_free, f["start"] + 2)
                sp.dma_start(x_res[k][:], dram["x"][q]).then_inc(res_loaded[k], 16)
                if not is_last(q, 2):
                    sp.wait_ge(xn_ready, q + 1)
                    sp.wait_ge(ct_lo_ready, q + 1)
                    load(q + 2, k)
                if not is_last(q, 1):
                    stack_max(1 - k, f["max"])
                if not is_last(q, 2):
                    stack_inputs(q + 2, k, f["proj"])
                sp.wait_ge(bank_free, f["out"] + 2 + 2)
                sp.dma_start(dram["x1"][q], x1[k][:]).then_inc(x1_stored[k], 16)

            def last():
                for k in range(2):
                    sp.wait_ge(x1_stored[k], 16 * (NB // 2 + 1))

            steady(sp, first, step, last)

        @block.gpsimd
        def _(pool):
            pool.memset(ones[:], 1.0).then_inc(ident_ready, 1)
            pool.wait_ge(ident_ready, 1)
            pool.affine_select(out=ident[:], in_=ones[:], compare_op=ALU.is_equal, fill=0.0, base=0,
                               pattern=[[-1, P]], channel_multiplier=1).then_inc(ident_ready, 1)

            pool.memset(power[:], -0.5).then_inc(ident_ready, 1)
            pool.wait_ge(ident_ready, 3)
            pool.wait_ge(loaded, 48)

            def deviations(p):
                pool.wait_ge(var_ready, p + 1)
                pool.tensor_tensor(rstd[:], var_eps[:], power[:], ALU.pow).then_inc(rstd_ready, 1)

            def split_ctx(p, k):
                pool.wait_ge(ct_hi_ready, p + 1)
                pool.tensor_tensor(ct_lo[:], ctx_in[k][:], ct_hi[:], ALU.subtract).then_inc(ct_lo_ready, 1)

            def first():
                for p in range(2):
                    deviations(p)
                    split_ctx(p, p)

            def step(q, k):
                pool.wait_ge(res_loaded[k], (q - k) * 8 + 16)
                pool.tensor_tensor(x_res[k][:], x_res[k][:], bias_o[:].unsqueeze(1).to_broadcast([P, TT, D]),
                                   ALU.add).then_inc(res_ready, 1)
                if not is_last(q, 2):
                    deviations(q + 2)
                    split_ctx(q + 2, k)

            steady(pool, first, step, lambda: None)

        @block.tensor
        def _(pe):
            pe.wait_ge(const, 1)
            pe.wait_ge(ident_ready, 2)

            def fill(f, b):
                pe.wait_ge(bank_free, f + 1)
                return bank[b % 2]

            def weights(n, c, cols):
                at = (n * KC + c) * D
                return tuple(wq_sb[h][:, at + cols.start:at + cols.stop] for h in ("hi", "lo"))

            def project_qk(p, f, b, between=lambda g: None):
                pe.wait_ge(xn_ready, p + 1)
                for c in range(KC):
                    between(c)
                    out = fill(f + c, b + c)
                    for a in range(TT):
                        ins = pe.transpose(out[:, a * P:(a + 1) * P], xn[:, a, c * P:(c + 1) * P], ident[:])
                    ins.then_inc(bank_ready, 1)
                for n in range(2):
                    between(2 + 2 * n)
                    if n == 0:
                        pe.wait_ge(bank_free, f + 4)
                        src = (xt_hi, xt_lo)
                    else:
                        pe.wait_ge(ct_lo_ready, p + 1)
                        src = (ct_hi, ct_lo)
                    for m in range(KC):
                        g = 2 + 2 * n + m
                        if m:
                            between(g)
                        out = fill(f + g, b + g)
                        for c in range(KC):
                            ins = halves_matmul(pe, out[:], weights(n, c, slice(m * P, m * P + P)),
                                                (src[0][:, c, :], src[1][:, c, :]), c == 0, c == KC - 1)
                        ins.then_inc(bank_ready, 1)

            def project_v(f, b):
                for g in range(2):
                    out = fill(f + g, b + g)
                    for half in range(2):
                        a = 2 * g + half
                        tok = slice(a * P, a * P + P)
                        for c in range(KC):
                            ins = halves_matmul(pe, out[:, half * D:(half + 1) * D],
                                                (ct_hi[:, c, tok], ct_lo[:, c, tok]),
                                                weights(2, c, slice(0, D)), c == 0, c == KC - 1)
                    ins.then_inc(bank_ready, 1)

            def row_scores(p, k, u):
                if u == 0:
                    pe.wait_ge(stacked, (p + 1) * 16 * STACK_DMAS)
                pe.wait_ge(max_done, p * SLOTS + u + 1)
                a, h0 = u // 8, 2 * (u % 8)
                keys = slice((a // 2) * D, (a // 2) * D + D)
                for n in range(2):
                    ins = pe.matmul(s_bank[u % 2][:, n, :],
                                    stack[k][0:MAX_ROW, h0 + n, 0, a * P:(a + 1) * P],
                                    stack[k][0:MAX_ROW, h0 + n, 1, keys], start=True, stop=True)
                ins.then_inc(s_ready, 1)

            def turn_maxima(p, f, b):
                out = fill(f, b)
                pe.wait_ge(max_done, (p + 1) * SLOTS + 2)
                for a in range(TT):
                    ins = pe.transpose(out[0:HEADS, a * P:(a + 1) * P], maxes[:, a, :], ident[:])
                ins.then_inc(bank_ready, 1)

            def slot(u):
                return u // 16, (u // 4) % 4, (u // 2) % 2, u % 2

            def col_scores(q, k, u):
                if u == 0:
                    pe.wait_ge(negmax_stacked, (q + 1) * 32)
                pe.wait_ge(exp_done, q * SLOTS + u + 1)
                j, i, c, hh = slot(u)
                keys = slice(j * D + c * P, j * D + c * P + P)
                for n in range(2):
                    h = 4 * i + 2 * hh + n
                    ins = pe.matmul(st_bank[u % 2][:, n, :], stack[k][0:STACK_ROWS, h, 1, keys],
                                    stack[k][0:STACK_ROWS, h, 0, j * D:(j + 1) * D], start=True, stop=True)
                ins.then_inc(st_ready, 1)

            def values(q, k, v):
                u = 2 * v
                j, i, c, _ = slot(u)
                pe.wait_ge(exp_done, q * SLOTS + u + 4)
                g2 = 2 * j + i // 2
                if v == 0:
                    pe.wait_ge(bank_free, fills(q)["start"])
                if i % 2 == 0 and c == 0:
                    pe.wait_ge(sums_ready, 4 * q + g2 + 1)
                for g in range(4):
                    s = (u + g // 2) % E_RING
                    ins = pe.matmul(pv_bank[g2 % 2][32 * g:32 * g + 32, i % 2, :],
                                    vals[k][:, 2 * j + c, 4 * i + g, :], expo[:, s, g % 2, :],
                                    start=(c == 0), stop=(c == 1), tile_position=(0, 32 * g))
                ins.then_inc(pv_done, 1)

            def turn_sums(q, k, n):
                out = fill(fills(q)["sums"][n], bank_of(q, k, "sums", n))
                pe.wait_ge(sums_ready, 4 * q + n + 1 + 2)
                for half in range(2):
                    for i in range(2):
                        at = (2 * half + i) * P
                        ins = pe.transpose(out[:, at:at + P], sums_t[n % 2][:, i, half * P:(half + 1) * P],
                                           ident[:])
                ins.then_inc(bank_ready, 1)

            def turn_heads(q, k):
                f, b = fills(q)["turn"], bank_of(q, k, "turn")
                pe.wait_ge(bank_free, fills(q)["sums"][3] + 1 + 2)
                for c in range(KC):
                    out = fill(f + c, b + c)
                    for a in range(TT):
                        ins = pe.transpose(out[:, a * P:(a + 1) * P],
                                           heads_n[:, a, c * 8:(c + 1) * 8, :].rearrange("p h d -> p (h d)"),
                                           ident[:])
                    ins.then_inc(bank_ready, 1)

            def output(q, k):
                f, b = fills(q)["out"], bank_of(q, k, "out")
                pe.wait_ge(bank_free, fills(q)["turn"] + 2 + 2)
                for g in range(2):
                    out = fill(f + g, b + g)
                    for half in range(2):
                        tok = slice((2 * g + half) * P, (2 * g + half + 1) * P)
                        for c in range(KC):
                            ins = halves_matmul(pe, out[:, half * D:(half + 1) * D],
                                                (ht_hi[:, c, tok], ht_lo[:, c, tok]),
                                                weights(3, c, slice(0, D)), c == 0, c == KC - 1)
                    ins.then_inc(bank_ready, 1)

            def first():
                project_qk(0, IN_0, IN_0)
                project_v(IN_0 + 6, IN_0 + 6)
                for u in range(SLOTS):
                    row_scores(0, 0, u)
                turn_maxima(0, MAX_0, MAX_0)
                project_qk(1, IN_1, IN_1)
                project_v(IN_1 + 6, IN_1 + 6)

            def step(q, k):
                f = fills(q)
                for u in range(SLOTS):
                    col_scores(q, k, u)
                    if u >= LAG and not is_last(q, 1):
                        row_scores(q + 1, 1 - k, u - LAG)
                    if u % 2 == 1 and u > 1:
                        values(q, k, u // 2 - 1)
                    if u % 8 == 6 and u > 8:
                        turn_sums(q, k, u // 8 - 1)
                values(q, k, SLOTS // 2 - 1)

                def trailing(n):
                    if n == 1:
                        turn_sums(q, k, 3)
                    if not is_last(q, 1):
                        row_scores(q + 1, 1 - k, SLOTS - LAG + n)

                trailing(0)
                trailing(1)
                if not is_last(q, 2):
                    project_qk(q + 2, f["proj"], bank_of(q, k, "proj"), lambda g: trailing(2 + g))
                else:
                    for n in range(2, LAG):
                        trailing(n)
                if not is_last(q, 1):
                    turn_maxima(q + 1, f["max"], bank_of(q, k, "max"))
                turn_heads(q, k)
                if not is_last(q, 2):
                    project_v(f["v"], bank_of(q, k, "v"))
                output(q, k)

            steady(pe, first, step, lambda: None)

        @block.scalar
        def _(act):
            act.sem_inc(exp_done, 2)
            act.sem_inc(sums_ready, 2)

            act.wait_ge(loaded, 48)

            def inputs(p, f, b):
                for c in range(KC):
                    act.wait_ge(bank_ready, f + c + 1)
                    act.copy(xt_hi[:, c, :], bank[(b + c) % 2][:]).then_inc(hi_ready, 1)
                for n in range(2):
                    for m in range(KC):
                        g = 2 + 2 * n + m
                        if g == 2 and not (isinstance(p, int) and p == 0):
                            act.wait_ge(unstacked, p * 16 * KC)
                        act.wait_ge(bank_ready, f + g + 1)
                        act.activation(qk[:, m, 2 * n, :], bank[(b + g) % 2][:], ACT.Identity,
                                       bias=bias_qk[:, n, m:m + 1]).then_inc(hi_ready, 1)

            def maxima(p, f, b):
                act.wait_ge(bank_ready, f + 1)
                if not (isinstance(p, int) and p == 0):
                    act.wait_ge(negmax_stacked, p * 32)
                act.mul(negmax[:, 0, :], bank[b % 2][0:HEADS, :], -1.0).then_inc(negmax_ready, 1)

            def exponentials(q, k, u):
                act.wait_ge(st_ready, q * SLOTS + u + 1)
                act.wait_ge(pv_done, q * (SLOTS // 2) + u // 2 + 1)
                act.activation(expo[:, u % E_RING, :, :], st_bank[u % 2][:], ACT.Exp,
                               scale=SCALE).then_inc(exp_done, 1)

            def copy_sums(q, n):
                act.wait_ge(pv_done, q * (SLOTS // 2) + 4 * (n + 1) + E_RING // 2)
                act.wait_ge(bank_ready, fills(q)["sums"][n - 2] + 1 if n > 1 else fills(q)["start"])
                act.copy(sums_t[n % 2][:], pv_bank[n % 2][:]).then_inc(sums_ready, 1)

            def heads_hi(q, k):
                f, b = fills(q)["turn"], bank_of(q, k, "turn")
                for c in range(KC):
                    act.wait_ge(bank_ready, f + c + 1)
                    act.copy(ht_hi[:, c, :], bank[(b + c) % 2][:]).then_inc(ht_hi_ready, 1)

            def first():
                inputs(0, IN_0, IN_0)
                maxima(0, MAX_0, MAX_0)
                inputs(1, IN_1, IN_1)

            def step(q, k):
                f = fills(q)
                for u in range(SLOTS):
                    exponentials(q, k, u)
                    if u % 8 == 3 and u > 8:
                        copy_sums(q, u // 8 - 1)
                copy_sums(q, 3)
                if not is_last(q, 2):
                    inputs(q + 2, f["proj"], bank_of(q, k, "proj"))
                if not is_last(q, 1):
                    maxima(q + 1, f["max"], bank_of(q, k, "max"))
                heads_hi(q, k)

            steady(act, first, step, lambda: None)

        @block.vector
        def _(dve):
            dve.sem_inc(bank_free, 2)
            dve.sem_inc(max_done, 2)
            dve.sem_inc(pv_done, E_RING // 2)
            for k in range(2):
                dve.memset(stack[k][64:P, :, :, :], 0.0)
                ins = dve.memset(vals[k][:], 1.0)
            ins.then_inc(cleared, 1)
            dve.wait_ge(cleared, 1)
            for k in range(2):
                ins = dve.memset(stack[k][96:P, :, 1, :], 1.0)
            ins.then_inc(const, 1)
            dve.wait_ge(loaded, 48)

            def normalize(p, k, reads):
                dve.wait_ge(x_loaded[k], (p - k) * 8 + 16)
                for a in range(TT):
                    ins = dve.bn_stats(stats[:, a, :], x_in[k][:, a, :])
                ins.then_inc(ln_step, 1)
                dve.wait_ge(ln_step, 2 * p + 1)
                dve.memset(hold[:], 0.0)
                for a in range(TT):
                    ins = dve.bn_aggr(mean_var[:, a, :], stats[:, a, :])
                ins.then_inc(ln_step, 1)
                dve.wait_ge(ln_step, 2 * p + 2)
                dve.tensor_scalar(var_eps[:], mean_var[:, :, 1], EPS, None, ALU.add).then_inc(var_ready, 1)
                dve.wait_ge(rstd_ready, p + 1)
                if reads is not None:
                    dve.wait_ge(bank_ready, reads)
                for a in range(TT):
                    ins = dve.tensor_scalar(xn[:, a, :], x_in[k][:, a, :], mean_var[:, a, 0:1],
                                            rstd[:, a:a + 1], ALU.subtract, ALU.mult)
                ins.then_inc(xn_ready, 1)

            def split_ctx(p, k, reads):
                dve.wait_ge(ctx_loaded[k], (p - k) * 8 + 16)
                if reads is not None:
                    dve.wait_ge(bank_ready, reads)
                    dve.wait_ge(ct_lo_ready, p)
                dve.tensor_copy(ct_hi[:], ctx_in[k][:]).then_inc(ct_hi_ready, 1)

            def split_qk(p, f, b, between=lambda g: None):
                for c in range(KC):
                    between(c)
                    dve.wait_ge(hi_ready, 6 * p + c + 1)
                    dve.tensor_tensor(xt_lo[:, c, :], bank[(b + c) % 2][:], xt_hi[:, c, :],
                                      ALU.subtract).then_inc(bank_free, 1)
                for n in range(2):
                    for m in range(KC):
                        g = 2 + 2 * n + m
                        between(g)
                        dve.wait_ge(hi_ready, 6 * p + g + 1)
                        dve.scalar_tensor_tensor(out=qk[:, m, 2 * n + 1, :], in0=bank[(b + g) % 2][:],
                                                 scalar=bias_qk[:, n, m:m + 1], in1=qk[:, m, 2 * n, :],
                                                 op0=ALU.add, op1=ALU.subtract).then_inc(bank_free, 1)

            def keep_v(k, f, b):
                for g in range(2):
                    dve.wait_ge(bank_ready, f + 1 + g)
                    for half in range(2):
                        ins = dve.tensor_tensor(
                            vals[k][:, 2 * g + half, :, 0:DH],
                            bank[(b + g) % 2][:, half * D:(half + 1) * D].rearrange("p (h d) -> p h d", d=DH),
                            bias_v[:].rearrange("p (h d) -> p h d", d=DH), ALU.add)
                    ins.then_inc(bank_free, 1)

            def row_max(p, u, reads=None):
                dve.wait_ge(s_ready, p * SLOTS + u + 1)
                if u == 0 and reads is not None:
                    dve.wait_ge(bank_ready, reads)
                a, h0 = u // 8, 2 * (u % 8)
                dve.tensor_reduce(maxes[:, a, h0:h0 + 2], s_bank[u % 2][:], AX_X, ALU.max)\
                    .then_inc(max_done, 1)

            def maxima(p, f, b):
                dve.wait_ge(negmax_ready, p + 1)
                dve.scalar_tensor_tensor(out=negmax[:, 1, :], in0=bank[b % 2][0:HEADS, :], scalar=-1.0,
                                         in1=negmax[:, 0, :], op0=ALU.mult, op1=ALU.subtract)\
                    .then_inc(bank_free, 1)

            def divide(q, k, n):
                f, b = fills(q)["sums"][n], bank_of(q, k, "sums", n)
                dve.wait_ge(bank_ready, f + 1)
                dve.reciprocal(inverse[:, n % 2], bank[b][:, DH::32]).then_inc(inverse_ready, 1)
                dve.wait_ge(inverse_ready, 4 * q + n + 1)
                j, h = n // 2, 8 * (n % 2)
                dve.tensor_tensor(heads_n[:, 2 * j:2 * j + 2, h:h + 8, :],
                                  bank[b][:].rearrange("p (a h d) -> p a h d", a=2, d=32)[:, :, :, 0:DH],
                                  inverse[:, n % 2].rearrange("p (a h) -> p a h", a=2).unsqueeze(3)
                                  .to_broadcast([P, 2, 8, DH]), ALU.mult).then_inc(bank_free, 1)

            def heads_lo(q, k):
                b = bank_of(q, k, "turn")
                for c in range(KC):
                    dve.wait_ge(ht_hi_ready, KC * q + c + 1)
                    dve.tensor_tensor(ht_lo[:, c, :], bank[(b + c) % 2][:], ht_hi[:, c, :],
                                      ALU.subtract).then_inc(bank_free, 1)

            def output(q, k):
                f, b = fills(q)["out"], bank_of(q, k, "out")
                dve.wait_ge(res_ready, q + 1)
                dve.wait_ge(x1_stored[k], (q - k) * 8 + 16)
                for g in range(2):
                    dve.wait_ge(bank_ready, f + g + 1)
                    dve.tensor_tensor(x1[k][:, 2 * g:2 * g + 2, :],
                                      bank[(b + g) % 2][:].rearrange("p (a d) -> p a d", d=D),
                                      x_res[k][:, 2 * g:2 * g + 2, :], ALU.add).then_inc(bank_free, 1)

            def first():
                normalize(0, 0, None)
                split_ctx(0, 0, None)
                split_qk(0, IN_0, IN_0)
                keep_v(0, IN_0 + 6, IN_0 + 6)
                normalize(1, 1, IN_0 + 2)
                split_ctx(1, 1, IN_0 + 8)
                for u in range(SLOTS):
                    row_max(0, u)
                maxima(0, MAX_0, MAX_0)
                split_qk(1, IN_1, IN_1)
                keep_v(1, IN_1 + 6, IN_1 + 6)

            def step(q, k):
                f = fills(q)
                for u in range(SLOTS):
                    if u >= LAG and not is_last(q, 1):
                        row_max(q + 1, u - LAG, f["start"])
                    if u == 12 and not is_last(q, 2):
                        normalize(q + 2, k, f["start"])
                        split_ctx(q + 2, k, f["start"])
                    if u % 8 == 7 and u > 8:
                        divide(q, k, u // 8 - 1)

                def trailing(n):
                    if not is_last(q, 1):
                        row_max(q + 1, SLOTS - LAG + n)
                    if n == 1:
                        divide(q, k, 3)

                trailing(0)
                trailing(1)
                if not is_last(q, 2):
                    split_qk(q + 2, f["proj"], bank_of(q, k, "proj"), lambda g: trailing(2 + g))
                else:
                    for n in range(2, LAG):
                        trailing(n)
                if not is_last(q, 1):
                    maxima(q + 1, f["max"], bank_of(q, k, "max"))
                heads_lo(q, k)
                if not is_last(q, 2):
                    keep_v(k, f["v"], bank_of(q, k, "v"))
                output(q, k)

            steady(dve, first, step, lambda: None)


def experts(nc, t, dram, NB):
    with ExitStack() as ctx:
        sb = lambda n, s, d: ctx.enter_context(nc.sbuf_tensor(n, s, d))
        pb = lambda n, s, d: ctx.enter_context(nc.psum_tensor(n, s, d))
        sem = lambda n: ctx.enter_context(nc.semaphore(n))

        w = sb("w", [P, EXPERTS, 2, UNITS * 512], BF16)
        gate_w = sb("gate_w", [P, KC, EXPERTS], F32)
        gate_hi = sb("gate_hi", [P, KC, EXPERTS], BF16)
        gate_lo = sb("gate_lo", [P, KC, EXPERTS], BF16)
        b1 = sb("b1", [P, EXPERTS, MC], F32)
        b3 = sb("b3", [P, EXPERTS, MC], F32)
        b2 = sb("b2", [P, EXPERTS, D], F32)
        x1 = sb("x1", [P, TT, D], F32)
        xn = sb("f_xn", [P, TT, D], F32)
        stats = sb("f_stats", [P, TT, 6], F32)
        mean_var = sb("f_mean_var", [P, TT, 2], F32)
        rstd = sb("f_rstd", [P, TT], F32)
        xt_hi = sb("f_xt_hi", [P, KC, TOK], BF16)
        xt_lo = sb("f_xt_lo", [P, KC, TOK], BF16)
        logits = sb("logits", [P, TT, EXPERTS], F32)
        score_max = sb("score_max", [P, TT], F32)
        scores = sb("scores", [P, TT, EXPERTS], F32)
        top = sb("top", [P, TT, 8], F32)
        top_at = sb("top_at", [P, TT, 8], U32)
        top_f = sb("top_f", [P, TT, 2], F32)
        top_sum = sb("top_sum", [P, TT], F32)
        top_inv = sb("top_inv", [P, TT], F32)
        weight = sb("weight", [P, TT, 2], F32)
        part = sb("part", [P, 2, TT, EXPERTS], F32)
        gates = sb("gates", [P, TT, EXPERTS], F32)
        number = sb("number", [P, EXPERTS], F32)
        acc = [sb(f"acc{k}", [P, TT, D], F32) for k in range(2)]
        silu = sb("silu", [P, 2, TOK], F32)
        act_f = sb("act_f", [P, 2, TOK], F32)
        act_hi = sb("act_hi", [P, 2, MC, TOK], BF16)
        act_lo = sb("act_lo", [P, 2, MC, TOK], BF16)
        power = sb("f_power", [P, TT], F32)
        hold = sb("f_hold", [P, 1], F32)
        var_eps = sb("f_var_eps", [P, TT], F32)
        ident = sb("f_ident", [P, P], F32)
        ones = sb("f_ones", [P, P], F32)

        y_bank = [pb(f"y_bank{a}", [P, 512], F32) for a in range(TT)]
        h1_bank = [pb(f"h1_bank{k}", [P, TOK], F32) for k in range(2)]
        h3_bank = [pb(f"h3_bank{k}", [P, TOK], F32) for k in range(2)]

        w_loaded = [sem(f"w_loaded{e}") for e in range(EXPERTS)]
        const_loaded = sem("f_const_loaded")
        const = sem("f_const")
        x1_loaded = sem("x1_loaded")
        step_done = sem("f_step")
        var_ready = sem("f_var_ready")
        rstd_ready = sem("f_rstd_ready")
        xn_ready = sem("f_xn_ready")
        xt_ready = sem("f_xt_ready")
        xt_hi_ready = sem("f_xt_hi_ready")
        xt_lo_ready = sem("f_xt_lo_ready")
        logits_ready = sem("logits_ready")
        gate_step = sem("gate_step")
        exp_ready = sem("f_exp_ready")
        h_ready = sem("h_ready")
        silu_ready = sem("silu_ready")
        g_ready = sem("g_ready")
        g_hi_ready = sem("g_hi_ready")
        g_lo_ready = sem("g_lo_ready")
        y_ready = sem("y_ready")
        y_added = sem("y_added")
        stored = [sem(f"y_stored{k}") for k in range(2)]

        block = ctx.enter_context(nc.Block())
        HT = EXPERTS * MC
        YT = EXPERTS * TT
        GATE_STEPS = 9 + EXPERTS

        @block.sync
        def _(sp):
            sp.dma_start(gate_w[:], dram["wg"]).then_inc(const_loaded, 16)
            sp.dma_start(b1[:], dram["bias1"]).then_inc(const_loaded, 16)
            sp.dma_start(b3[:], dram["bias3"]).then_inc(const_loaded, 16)
            sp.dma_start(b2[:], dram["bias2"].partition_broadcast(P)).then_inc(const_loaded, 16)
            for e in range(EXPERTS):
                sp.dma_start(w[:, e], dram["experts"][e].rearrange("p h u n -> p h (u n)")).then_inc(w_loaded[e], 16)
            for k in range(2):
                sp.sem_inc(stored[k], 16)
            with sp.Fori(0, NB // 2) as i:
                for k in range(2):
                    b = i * 2 + k
                    sp.wait_ge(y_added, b * YT + 1)
                    sp.dma_start(x1[:], dram["x1"][b]).then_inc(x1_loaded, 16)
                    sp.wait_ge(y_added, (b + 1) * YT + 1)
                    sp.dma_start(dram["y"][b], acc[k][:]).then_inc(stored[k], 16)
            for k in range(2):
                sp.wait_ge(stored[k], 16 * (NB // 2 + 1))

        @block.gpsimd
        def _(pool):
            pool.memset(ones[:], 1.0).then_inc(const, 1)
            pool.wait_ge(const, 1)
            pool.affine_select(out=ident[:], in_=ones[:], compare_op=ALU.is_equal, fill=0.0, base=0,
                               pattern=[[-1, P]], channel_multiplier=1).then_inc(const, 1)
            pool.iota(number[:], pattern=[[1, EXPERTS]], base=0, channel_multiplier=0,
                      allow_small_or_imprecise_dtypes=True).then_inc(const, 1)
            pool.wait_ge(const_loaded, 64)
            pool.tensor_copy(gate_hi[:], gate_w[:]).then_inc(const, 1)
            pool.wait_ge(const, 4)
            pool.tensor_tensor(gate_lo[:], gate_w[:], gate_hi[:], ALU.subtract).then_inc(const, 1)
            pool.memset(power[:], -0.5).then_inc(const, 1)
            pool.wait_ge(const, 6)
            pool.sem_inc(g_lo_ready, 2)
            with pool.Fori(0, NB) as b:
                pool.wait_ge(var_ready, b + 1)
                pool.tensor_tensor(rstd[:], var_eps[:], power[:], ALU.pow).then_inc(rstd_ready, 1)
                for e in range(EXPERTS):
                    for m in range(MC):
                        n = b * HT + e * MC + m
                        pool.wait_ge(g_hi_ready, n + 1)
                        pool.tensor_tensor(act_lo[:, e % 2, m, :], act_f[:, m % 2, :], act_hi[:, e % 2, m, :],
                                           ALU.subtract).then_inc(g_lo_ready, 1)

        @block.tensor
        def _(pe):
            pe.wait_ge(const, 5)
            with pe.Fori(0, NB) as b:
                pe.wait_ge(xn_ready, b + 1)
                pe.wait_ge(y_added, b * YT + 1)
                for c in range(KC):
                    for a in range(TT):
                        ins = pe.transpose(y_bank[c][:, a * P:(a + 1) * P], xn[:, a, c * P:(c + 1) * P], ident[:])
                    ins.then_inc(xt_ready, 1)
                pe.wait_ge(xt_lo_ready, KC * (b + 1))
                for a in range(TT):
                    for c in range(KC):
                        lhs = [x[:, c, a * P:(a + 1) * P] for x in (xt_hi, xt_lo)]
                        ins = halves_matmul(pe, y_bank[2][:, a * EXPERTS:(a + 1) * EXPERTS], lhs,
                                            (gate_hi[:, c, :], gate_lo[:, c, :]), c == 0, c == KC - 1)
                ins.then_inc(logits_ready, 1)

                def hidden(e):
                    for m in range(MC):
                        n = b * HT + e * MC + m
                        pe.wait_ge(g_ready, n + 1)
                        for kind, out in ((0, h1_bank), (1, h3_bank)):
                            for c in range(KC):
                                at = (2 * kind + c) * 512 + m * P
                                ins = halves_matmul(pe, out[m % 2][:],
                                                    (w[:, e, 0, at:at + P], w[:, e, 1, at:at + P]),
                                                    (xt_hi[:, c, :], xt_lo[:, c, :]), c == 0, c == KC - 1)
                        ins.then_inc(h_ready, 1)

                def outputs(e):
                    pe.wait_ge(g_lo_ready, b * HT + (e + 1) * MC + 2)
                    for a in range(TT):
                        pe.wait_ge(y_added, b * YT + e * TT - TT + a + 2 if e else b * YT + 1)
                        if e == 0:
                            pe.wait_ge(exp_ready, b + 1)
                        tok = slice(a * P, (a + 1) * P)
                        for m in range(MC):
                            at = 4 * 512 + m * D
                            ins = halves_matmul(pe, y_bank[a][:, 0:D],
                                                (act_hi[:, e % 2, m, tok], act_lo[:, e % 2, m, tok]),
                                                (w[:, e, 0, at:at + D], w[:, e, 1, at:at + D]), m == 0, m == MC - 1)
                        ins.then_inc(y_ready, 1)

                for e in range(EXPERTS):
                    pe.wait_ge(w_loaded[e], 16)
                    hidden(e)
                    if e:
                        outputs(e - 1)
                outputs(EXPERTS - 1)

        @block.scalar
        def _(act):
            act.sem_inc(g_hi_ready, 0) if False else None
            with act.Fori(0, NB) as b:
                for c in range(KC):
                    act.wait_ge(xt_ready, KC * b + c + 1)
                    act.copy(xt_hi[:, c, :], y_bank[c][:]).then_inc(xt_hi_ready, 1)
                act.wait_ge(gate_step, GATE_STEPS * b + 2)
                act.activation(scores[:], logits[:], ACT.Exp).then_inc(exp_ready, 1)
                for e in range(EXPERTS):
                    for m in range(MC):
                        n = b * HT + e * MC + m
                        act.wait_ge(h_ready, n + 1)
                        act.activation(silu[:, m % 2, :], h1_bank[m % 2][:], ACT.Silu,
                                       bias=b1[:, e, m:m + 1]).then_inc(silu_ready, 1)
                        act.wait_ge(g_ready, n + 3)
                        act.copy(act_hi[:, e % 2, m, :], act_f[:, m % 2, :]).then_inc(g_hi_ready, 1)

        @block.vector
        def _(dve):
            dve.sem_inc(g_ready, 2)
            dve.sem_inc(y_added, 1)
            dve.wait_ge(const_loaded, 64)
            dve.wait_ge(const, 5)
            with dve.Fori(0, NB // 2) as i2:
                for k in range(2):
                    b = i2 * 2 + k
                    dve.wait_ge(x1_loaded, 16 * b + 16)
                    for a in range(TT):
                        ins = dve.bn_stats(stats[:, a, :], x1[:, a, :])
                    ins.then_inc(step_done, 1)
                    dve.wait_ge(step_done, 2 * b + 1)
                    dve.memset(hold[:], 0.0)
                    for a in range(TT):
                        ins = dve.bn_aggr(mean_var[:, a, :], stats[:, a, :])
                    ins.then_inc(step_done, 1)
                    dve.wait_ge(step_done, 2 * b + 2)
                    dve.tensor_scalar(var_eps[:], mean_var[:, :, 1], EPS, None, ALU.add).then_inc(var_ready, 1)
                    dve.wait_ge(rstd_ready, b + 1)
                    for a in range(TT):
                        ins = dve.tensor_scalar(xn[:, a, :], x1[:, a, :], mean_var[:, a, 0:1],
                                                rstd[:, a:a + 1], ALU.subtract, ALU.mult)
                    ins.then_inc(xn_ready, 1)
                    for c in range(KC):
                        dve.wait_ge(xt_hi_ready, KC * b + c + 1)
                        dve.tensor_tensor(xt_lo[:, c, :], y_bank[c][:], xt_hi[:, c, :], ALU.subtract)\
                            .then_inc(xt_lo_ready, 1)

                    def done(ins, n):
                        ins.then_inc(gate_step, 1)
                        dve.wait_ge(gate_step, GATE_STEPS * b + n)

                    dve.wait_ge(logits_ready, b + 1)
                    done(dve.tensor_reduce(score_max[:], y_bank[2][:, 0:TT * EXPERTS].rearrange(
                        "p (a e) -> p a e", e=EXPERTS), AX_X, ALU.max), 1)
                    done(dve.tensor_tensor(logits[:], y_bank[2][:, 0:TT * EXPERTS].rearrange(
                        "p (a e) -> p a e", e=EXPERTS), score_max[:].unsqueeze(2).to_broadcast([P, TT, EXPERTS]),
                        ALU.subtract), 2)
                    dve.wait_ge(exp_ready, b + 1)
                    dve.memset(hold[:], 0.0)
                    for a in range(TT):
                        ins = dve.max(top[:, a, :], scores[:, a, :])
                    done(ins, 3)
                    dve.memset(hold[:], 0.0)
                    for a in range(TT):
                        ins = dve.max_index(top_at[:, a, :], top[:, a, :], scores[:, a, :])
                    done(ins, 4)
                    dve.tensor_copy(top_f[:], top_at[:, :, 0:2])
                    done(dve.tensor_tensor(top_sum[:], top[:, :, 0], top[:, :, 1], ALU.add), 5)
                    done(dve.reciprocal(top_inv[:], top_sum[:]), 6)
                    done(dve.tensor_tensor(weight[:], top[:, :, 0:2],
                                           top_inv[:].unsqueeze(2).to_broadcast([P, TT, 2]), ALU.mult), 7)
                    for a in range(TT):
                        for n in range(2):
                            ins = dve.tensor_scalar(part[:, n, a, :], number[:], top_f[:, a, n:n + 1],
                                                    weight[:, a, n:n + 1], ALU.is_equal, ALU.mult)
                    done(ins, 8)
                    done(dve.tensor_tensor(gates[:], part[:, 0], part[:, 1], ALU.add), 9)
                    dve.wait_ge(stored[k], i2 * 16 + 16)
                    for e in range(EXPERTS):
                        for a in range(TT):
                            ins = dve.scalar_tensor_tensor(out=acc[k][:, a, :], in0=b2[:, e, :],
                                                           scalar=gates[:, a, e:e + 1],
                                                           in1=x1[:, a, :] if e == 0 else acc[k][:, a, :],
                                                           op0=ALU.mult, op1=ALU.add)
                        done(ins, 10 + e)

                    def product(e, m):
                        n = b * HT + e * MC + m
                        dve.wait_ge(silu_ready, n + 1)
                        dve.wait_ge(g_lo_ready, n + 1)
                        dve.scalar_tensor_tensor(out=act_f[:, m % 2, :], in0=h3_bank[m % 2][:],
                                                 scalar=b3[:, e, m:m + 1], in1=silu[:, m % 2, :],
                                                 op0=ALU.add, op1=ALU.mult).then_inc(g_ready, 1)

                    def add(e):
                        for a in range(TT):
                            if e:
                                dve.wait_ge(y_added, b * YT + (e - 1) * TT + a + 2)
                            dve.wait_ge(y_ready, b * YT + e * TT + a + 1)
                            dve.scalar_tensor_tensor(out=acc[k][:, a, :], in0=y_bank[a][:, 0:D],
                                                     scalar=gates[:, a, e:e + 1], in1=acc[k][:, a, :],
                                                     op0=ALU.mult, op1=ALU.add).then_inc(y_added, 1)

                    for e in range(EXPERTS):
                        for m in range(MC):
                            product(e, m)
                        if e:
                            add(e - 1)
                    add(EXPERTS - 1)


def build(nc, ins, out):
    NB = 16
    tokens = lambda a: a.rearrange("b s d -> (b s) d").rearrange("(q a p) d -> q p a d", a=TT, p=P)
    scratch = lambda n, s, d: nc.dram_tensor(n, s, d, kind="Internal").ap()
    dram = dict(ins)
    dram["x"] = tokens(ins["x"])
    dram["y"] = tokens(out)
    dram["x1"] = scratch("x1_scratch", [NB, P, TT, D], F32)
    qk = scratch("qk_scratch", [2, 4, D, TOK], BF16)
    dram["qk"] = qk.rearrange("b s (c p) n -> b c p s n", p=P)
    dram["qk_by_row"] = qk.rearrange("b s (h j) n -> b s j h n", j=DH)
    dram["experts"] = scratch("experts_scratch", [EXPERTS, P, 2, UNITS, 512], BF16)
    with ExitStack() as ctx:
        width = 4 * KC * D
        wq_sb = {h: ctx.enter_context(nc.sbuf_tensor(f"proj_{h}", [P, width], BF16)) for h in ("hi", "lo")}
        prepare_weights(nc, None, dram, wq_sb, NB)
        attention(nc, None, dram, wq_sb, NB)
    experts(nc, None, dram, NB)


def lay_out(inputs):
    import numpy as np

    def arr(name):
        return np.asarray(inputs[name])

    def rows(w):
        w = np.swapaxes(w, -1, -2)
        w = w.reshape(w.shape[:-2] + (w.shape[-2] // P, P, w.shape[-1]))
        return np.ascontiguousarray(np.swapaxes(w, -2, -3))

    a = {"x": arr("x")}
    a["ctx"] = np.ascontiguousarray(arr("ctx_1024").reshape(16, TOK, KC, P).transpose(0, 3, 2, 1))
    a["w_qkvo"] = np.concatenate([rows(arr(f"L0_xattn_w{n}")).reshape(P, KC * D) for n in "qkvo"], axis=1)
    a["bias_qk"] = np.ascontiguousarray(
        np.stack([arr("L0_xattn_bq"), arr("L0_xattn_bk")]).reshape(2, KC, P).transpose(2, 0, 1))
    a["bias_v"] = arr("L0_xattn_bv")
    a["bias_o"] = arr("L0_xattn_bo")
    a["wg"] = rows(arr("L0_ffn_Wg"))
    for n in "132":
        a[f"w{n}"] = rows(arr(f"L0_ffn_W{n}")).reshape(EXPERTS, P, 2, 512)
        a[f"a{n}"] = arr(f"L0_ffn_A{n}")
        a[f"b{n}"] = np.ascontiguousarray(np.swapaxes(arr(f"L0_ffn_B{n}"), 1, 2))
    for n in "13":
        a[f"bias{n}"] = np.ascontiguousarray(arr(f"L0_ffn_b{n}").reshape(EXPERTS, MC, P).transpose(2, 0, 1))
    a["bias2"] = arr("L0_ffn_b2")
    return a


def kernel(**inputs):
    import concourse.bacc as bacc
    from concourse.bass_utils import run_bass_kernel_spmd

    nc = bacc.Bacc("TRN2", target_bir_lowering=False, num_devices=1)
    arrays = lay_out(inputs)
    ins = {n: nc.dram_tensor(f"in_{n}", a.shape, mybir.dt.from_np(a.dtype), kind="ExternalInput").ap()
           for n, a in arrays.items()}
    shape = tuple(inputs["x"].shape)
    out = nc.dram_tensor("out_y", shape, F32, kind="ExternalOutput").ap()
    build(nc, ins, out)
    r = run_bass_kernel_spmd(nc, [{f"in_{n}": a for n, a in arrays.items()}], core_ids=[0])
    return r.results[0]["out_y"]
```

```python
from contextlib import ExitStack

import concourse.bass as bass
from concourse import mybir

F32 = mybir.dt.float32
BF16 = mybir.dt.bfloat16
U32 = mybir.dt.uint32
I32 = mybir.dt.int32
ALU = mybir.AluOpType
ACT = mybir.ActivationFunctionType
AX_X = mybir.AxisListType.X

P = 128
D = 256
KC = D // P
HEADS = 16
DH = D // HEADS
HID = 512
MC = HID // P
EXPERTS = 8
RANK = 16
EPS = 1e-5
SCALE = DH ** -0.5

TOK = 512
TT = TOK // P
TOKENS = 8192
REGION = TOKENS + TOK
ROW = D + 4
MAX_TILES = 2 * TOKENS // TOK + EXPERTS
UNITS = 6

MAX_ROW = 97
STACK_ROWS = 99

LAG = 8
SLOTS = 32
E_RING = 8
STACK_DMAS = 8


def halves_matmul(pe, out, lhs, rhs, first, last):
    lhs_hi, lhs_lo = lhs
    rhs_hi, rhs_lo = rhs
    pe.matmul(out, lhs_hi, rhs_hi, start=first, stop=False)
    pe.matmul(out, lhs_lo, rhs_hi, start=False, stop=False)
    return pe.matmul(out, lhs_hi, rhs_lo, start=False, stop=last)


def prepare_weights(nc, t, dram, wq_sb, NB):
    with ExitStack() as ctx:
        sb = lambda n, s, d: ctx.enter_context(nc.sbuf_tensor(n, s, d))
        sem = lambda n: ctx.enter_context(nc.semaphore(n))
        w_in = [sb(f"w_in{k}", [P, UNITS, 512], F32) for k in range(2)]
        a_in = [sb(f"a_in{k}", [P, D + D + HID], F32) for k in range(2)]
        b_in = [sb(f"b_in{k}", [P, HID + HID + D], F32) for k in range(2)]
        w_sum = [sb(f"w_sum{k}", [P, UNITS, 512], F32) for k in range(2)]
        w_out = [sb(f"w_out{k}", [P, 2, UNITS, 512], BF16) for k in range(2)]
        proj_in = sb("proj_in", [P, 4 * KC * D], F32)
        low = [ctx.enter_context(nc.psum_tensor(f"low{k}", [P, 512], F32)) for k in range(2)]

        zeroed = sem("zeroed")
        loaded = [sem(f"prep_loaded{k}") for k in range(2)]
        proj_loaded = sem("proj_loaded")
        proj_hi = sem("proj_hi")
        low_ready = sem("low_ready")
        sum_ready = sem("sum_ready")
        hi_ready = sem("prep_hi_ready")
        lo_ready = sem("prep_lo_ready")
        stored = [sem(f"prep_stored{k}") for k in range(2)]
        LOADS = 3 + 3 + 3

        block = ctx.enter_context(nc.Block())

        @block.sync
        def _(sp):
            sp.dma_start(proj_in[:], dram["w_qkvo"]).then_inc(proj_loaded, 16)
            sp.wait_ge(zeroed, 1)
            with sp.Fori(0, EXPERTS // 2) as i:
                for k in range(2):
                    e = i * 2 + k
                    sp.wait_ge(lo_ready, e * UNITS + UNITS)
                    for n, name in enumerate(("w1", "w3", "w2")):
                        sp.dma_start(w_in[k][:, 2 * n:2 * n + 2, :], dram[name][e]).then_inc(loaded[k], 16)
                    at = 0
                    for name, width in (("a1", D), ("a3", D), ("a2", HID)):
                        sp.dma_start(a_in[k][0:RANK, at:at + width], dram[name][e]).then_inc(loaded[k], 16)
                        at += width
                    at = 0
                    for name, width in (("b1", HID), ("b3", HID), ("b2", D)):
                        sp.dma_start(b_in[k][0:RANK, at:at + width], dram[name][e]).then_inc(loaded[k], 16)
                        at += width

        @block.gpsimd
        def _(pool):
            for k in range(2):
                pool.memset(a_in[k][:], 0.0)
                ins = pool.memset(b_in[k][:], 0.0)
            ins.then_inc(zeroed, 1)
            pool.sem_inc(lo_ready, 2 * UNITS)
            pool.wait_ge(proj_hi, 1)
            pool.tensor_tensor(wq_sb["lo"][:], proj_in[:], wq_sb["hi"][:], ALU.subtract).then_inc(proj_hi, 1)
            with pool.Fori(0, EXPERTS // 2) as i:
                for k in range(2):
                    e = i * 2 + k
                    for u in range(UNITS):
                        pool.wait_ge(hi_ready, e * UNITS + u + 1)
                        pool.tensor_tensor(w_out[k][:, 1, u, :], w_sum[k][:, u, :], w_out[k][:, 0, u, :],
                                           ALU.subtract).then_inc(lo_ready, 1)

        @block.tensor
        def _(pe):
            pe.wait_ge(zeroed, 1)
            with pe.Fori(0, EXPERTS // 2) as i:
                for k in range(2):
                    e = i * 2 + k
                    pe.wait_ge(loaded[k], (i + 1) * 16 * LOADS)
                    for u in range(UNITS):
                        pe.wait_ge(sum_ready, e * UNITS + u + 1)
                        if u < 4:
                            pe.matmul(low[u % 2][:], a_in[k][:, u * P:(u + 1) * P],
                                      b_in[k][:, (u // 2) * HID:(u // 2 + 1) * HID],
                                      start=True, stop=True).then_inc(low_ready, 1)
                        else:
                            for half in range(2):
                                c = 2 * D + (2 * (u - 4) + half) * P
                                ins = pe.matmul(low[u % 2][:, half * D:(half + 1) * D], a_in[k][:, c:c + P],
                                                b_in[k][:, 2 * HID:2 * HID + D], start=True, stop=True)
                            ins.then_inc(low_ready, 1)

        @block.vector
        def _(dve):
            dve.sem_inc(sum_ready, 2)
            with dve.Fori(0, EXPERTS // 2) as i:
                for k in range(2):
                    e = i * 2 + k
                    dve.wait_ge(lo_ready, e * UNITS + UNITS)
                    for u in range(UNITS):
                        dve.wait_ge(low_ready, e * UNITS + u + 1)
                        dve.tensor_tensor(w_sum[k][:, u, :], low[u % 2][:], w_in[k][:, u, :],
                                          ALU.add).then_inc(sum_ready, 1)

        @block.scalar
        def _(act):
            act.wait_ge(proj_loaded, 16)
            act.copy(wq_sb["hi"][:], proj_in[:]).then_inc(proj_hi, 1)
            for k in range(2):
                act.sem_inc(stored[k], 16)
            with act.Fori(0, EXPERTS // 2) as i:
                for k in range(2):
                    e = i * 2 + k
                    act.wait_ge(stored[k], i * 16 + 16)
                    for u in range(UNITS):
                        act.wait_ge(sum_ready, e * UNITS + u + 3)
                        act.copy(w_out[k][:, 0, u, :], w_sum[k][:, u, :]).then_inc(hi_ready, 1)
                    act.wait_ge(lo_ready, e * UNITS + 3 * UNITS)
                    act.dma_start(dram["experts"][e], w_out[k][:]).then_inc(stored[k], 16)
            for k in range(2):
                act.wait_ge(stored[k], 16 * (EXPERTS // 2 + 1))
            act.wait_ge(proj_hi, 2)


def attention(nc, t, dram, wq_sb, NB):
    with ExitStack() as ctx:
        sb = lambda n, s, d: ctx.enter_context(nc.sbuf_tensor(n, s, d))
        pb = lambda n, s, d: ctx.enter_context(nc.psum_tensor(n, s, d))
        sem = lambda n: ctx.enter_context(nc.semaphore(n))

        x_in = [sb(f"x_in{k}", [P, TT, D], F32) for k in range(2)]
        x_res = [sb(f"x_res{k}", [P, TT, D], F32) for k in range(2)]
        xn = sb("xn", [P, TT, D], F32)
        stats = sb("stats", [P, TT, 6], F32)
        mean_var = sb("mean_var", [P, TT, 2], F32)
        rstd = sb("rstd", [P, TT], F32)
        xt_hi = sb("xt_hi", [P, KC, TOK], BF16)
        xt_lo = sb("xt_lo", [P, KC, TOK], BF16)
        ctx_in = [sb(f"ctx_in{k}", [P, KC, TOK], F32) for k in range(2)]
        ct_hi = sb("ct_hi", [P, KC, TOK], BF16)
        ct_lo = sb("ct_lo", [P, KC, TOK], BF16)
        qk = sb("qk", [P, KC, 4, TOK], BF16)
        stack = [sb(f"stack{k}", [P, HEADS, 2, TOK], BF16) for k in range(2)]
        vals = [sb(f"vals{k}", [P, TT, HEADS, 32], F32) for k in range(2)]
        expo = sb("expo", [P, E_RING, 2, D], F32)
        maxes = sb("maxes", [P, TT, HEADS], F32)
        negmax = sb("negmax", [HEADS, 2, TOK], BF16)
        sums_t = [sb(f"sums_t{k}", [P, 2, D], F32) for k in range(2)]
        inverse = sb("inverse", [P, 2, 16], F32)
        heads_n = sb("heads_n", [P, TT, HEADS, DH], F32)
        ht_hi = sb("ht_hi", [P, KC, TOK], BF16)
        ht_lo = sb("ht_lo", [P, KC, TOK], BF16)
        bias_o = sb("bias_o", [P, D], F32)
        power = sb("power", [P, TT], F32)
        hold = sb("hold", [P, 1], F32)
        var_eps = sb("var_eps", [P, TT], F32)
        x1 = [sb(f"x1_{k}", [P, TT, D], F32) for k in range(2)]
        bias_qk = sb("bias_qk", [P, 2, KC], F32)
        bias_v = sb("bias_v", [P, D], F32)
        ident = sb("ident", [P, P], F32)
        ones = sb("ones", [P, P], F32)

        st_bank = [pb(f"st_bank{k}", [P, 2, D], F32) for k in range(2)]
        s_bank = [pb(f"s_bank{k}", [P, 2, D], F32) for k in range(2)]
        pv_bank = [pb(f"pv_bank{k}", [P, 2, D], F32) for k in range(2)]
        bank = [pb(f"bank{k}", [P, 512], F32) for k in range(2)]

        loaded = sem("const_loaded")
        const = sem("const_ready")
        ident_ready = sem("ident_ready")
        x_loaded = [sem(f"x_loaded{k}") for k in range(2)]
        ctx_loaded = [sem(f"ctx_loaded{k}") for k in range(2)]
        res_loaded = [sem(f"res_loaded{k}") for k in range(2)]
        ln_step = sem("ln_step")
        xn_ready = sem("xn_ready")
        ct_hi_ready = sem("ct_hi_ready")
        ct_lo_ready = sem("ct_lo_ready")
        bank_ready = sem("bank_ready")
        bank_free = sem("bank_free")
        hi_ready = sem("hi_ready")
        unstacked = sem("unstacked")
        stacked = sem("stacked")
        st_ready = sem("st_ready")
        exp_done = sem("exp_done")
        s_ready = sem("s_ready")
        max_done = sem("max_done")
        pv_done = sem("pv_done")
        cleared = sem("cleared")
        sums_ready = sem("sums_ready")
        inverse_ready = sem("inverse_ready")
        var_ready = sem("var_ready")
        rstd_ready = sem("rstd_ready")
        res_ready = sem("res_ready")
        ht_hi_ready = sem("ht_hi_ready")
        negmax_ready = sem("negmax_ready")
        negmax_stacked = sem("negmax_stacked")
        x1_stored = [sem(f"x1_stored{k}") for k in range(2)]

        FIRST, EACH = 17, 17
        IN_0, MAX_0, IN_1 = 0, 8, 9

        def fills(q):
            if isinstance(q, int) and q == NB - 2:
                s = FIRST + EACH * q
                return dict(start=s, sums=[s, s + 1, s + 2, s + 3], max=s + 4, turn=s + 5, out=s + 7)
            if isinstance(q, int) and q == NB - 1:
                s = FIRST + EACH * (q - 1) + 9
                return dict(start=s, sums=[s, s + 1, s + 2, s + 3], turn=s + 4, out=s + 6)
            s = FIRST + EACH * q
            return dict(start=s, sums=[s, s + 1, s + 2, s + 3], proj=s + 4, max=s + 10, turn=s + 11,
                        v=s + 13, out=s + 15)

        def bank_of(q, k, step, n=None):
            at = fills(q if isinstance(q, int) else k)[step]
            return (at if n is None else at[n]) % 2

        block = ctx.enter_context(nc.Block())

        def steady(engine, first, step, last):
            first()
            with engine.Fori(0, (NB - 2) // 2) as i:
                for k in range(2):
                    step(i * 2 + k, k)
            for q in range(NB - 2, NB):
                step(q, q % 2)
            last()

        def is_last(q, back):
            return isinstance(q, int) and q >= NB - back

        @block.sync
        def _(sp):
            sp.dma_start(bias_qk[:], dram["bias_qk"]).then_inc(loaded, 16)
            sp.dma_start(bias_v[:], dram["bias_v"].partition_broadcast(P)).then_inc(loaded, 16)
            sp.dma_start(bias_o[:], dram["bias_o"].partition_broadcast(P)).then_inc(loaded, 16)

            def load(p, k):
                sp.dma_start(x_in[k][:], dram["x"][p]).then_inc(x_loaded[k], 16)
                sp.dma_start(ctx_in[k][:], dram["ctx"][p]).then_inc(ctx_loaded[k], 16)

            def stack_inputs(p, k, proj):
                sp.wait_ge(bank_free, proj + 6 + 2)
                for c in range(KC):
                    sp.dma_start(dram["qk"][k, c], qk[:, c]).then_inc(unstacked, 16)
                sp.wait_ge(unstacked, 16 * KC * (p + 1))
                for u in range(4):
                    for side, half in ((0, u // 2), (1, u % 2)):
                        sp.dma_start(stack[k][DH * u:DH * u + DH, :, side, :],
                                     dram["qk_by_row"][k, 2 * side + half]).then_inc(stacked, 16)

            def stack_max(k, fill):
                sp.wait_ge(bank_free, fill + 1 + 2)
                for n in range(2):
                    sp.dma_start(stack[k][MAX_ROW + n:MAX_ROW + n + 1, :, 0, :], negmax[:, n, :])\
                        .then_inc(negmax_stacked, 16)

            for k in range(2):
                sp.sem_inc(x1_stored[k], 16)

            def first():
                load(0, 0)
                load(1, 1)
                sp.wait_ge(const, 1)
                stack_inputs(0, 0, IN_0)
                stack_max(0, MAX_0)
                stack_inputs(1, 1, IN_1)

            def step(q, k):
                f = fills(q)
                sp.wait_ge(bank_free, f["start"] + 2)
                sp.dma_start(x_res[k][:], dram["x"][q]).then_inc(res_loaded[k], 16)
                if not is_last(q, 2):
                    sp.wait_ge(xn_ready, q + 1)
                    sp.wait_ge(ct_lo_ready, q + 1)
                    load(q + 2, k)
                if not is_last(q, 1):
                    stack_max(1 - k, f["max"])
                if not is_last(q, 2):
                    stack_inputs(q + 2, k, f["proj"])
                sp.wait_ge(bank_free, f["out"] + 2 + 2)
                sp.dma_start(dram["x1"][q], x1[k][:]).then_inc(x1_stored[k], 16)

            def last():
                for k in range(2):
                    sp.wait_ge(x1_stored[k], 16 * (NB // 2 + 1))

            steady(sp, first, step, last)

        @block.gpsimd
        def _(pool):
            pool.memset(ones[:], 1.0).then_inc(ident_ready, 1)
            pool.wait_ge(ident_ready, 1)
            pool.affine_select(out=ident[:], in_=ones[:], compare_op=ALU.is_equal, fill=0.0, base=0,
                               pattern=[[-1, P]], channel_multiplier=1).then_inc(ident_ready, 1)

            pool.memset(power[:], -0.5).then_inc(ident_ready, 1)
            pool.wait_ge(ident_ready, 3)
            pool.wait_ge(loaded, 48)

            def deviations(p):
                pool.wait_ge(var_ready, p + 1)
                pool.tensor_tensor(rstd[:], var_eps[:], power[:], ALU.pow).then_inc(rstd_ready, 1)

            def split_ctx(p, k):
                pool.wait_ge(ct_hi_ready, p + 1)
                pool.tensor_tensor(ct_lo[:], ctx_in[k][:], ct_hi[:], ALU.subtract).then_inc(ct_lo_ready, 1)

            def first():
                for p in range(2):
                    deviations(p)
                    split_ctx(p, p)

            def step(q, k):
                pool.wait_ge(res_loaded[k], (q - k) * 8 + 16)
                pool.tensor_tensor(x_res[k][:], x_res[k][:], bias_o[:].unsqueeze(1).to_broadcast([P, TT, D]),
                                   ALU.add).then_inc(res_ready, 1)
                if not is_last(q, 2):
                    deviations(q + 2)
                    split_ctx(q + 2, k)

            steady(pool, first, step, lambda: None)

        @block.tensor
        def _(pe):
            pe.wait_ge(const, 1)
            pe.wait_ge(ident_ready, 2)

            def fill(f, b):
                pe.wait_ge(bank_free, f + 1)
                return bank[b % 2]

            def weights(n, c, cols):
                at = (n * KC + c) * D
                return tuple(wq_sb[h][:, at + cols.start:at + cols.stop] for h in ("hi", "lo"))

            def project_qk(p, f, b, between=lambda g: None):
                pe.wait_ge(xn_ready, p + 1)
                for c in range(KC):
                    between(c)
                    out = fill(f + c, b + c)
                    for a in range(TT):
                        ins = pe.transpose(out[:, a * P:(a + 1) * P], xn[:, a, c * P:(c + 1) * P], ident[:])
                    ins.then_inc(bank_ready, 1)
                for n in range(2):
                    between(2 + 2 * n)
                    if n == 0:
                        pe.wait_ge(bank_free, f + 4)
                        src = (xt_hi, xt_lo)
                    else:
                        pe.wait_ge(ct_lo_ready, p + 1)
                        src = (ct_hi, ct_lo)
                    for m in range(KC):
                        g = 2 + 2 * n + m
                        if m:
                            between(g)
                        out = fill(f + g, b + g)
                        for c in range(KC):
                            ins = halves_matmul(pe, out[:], weights(n, c, slice(m * P, m * P + P)),
                                                (src[0][:, c, :], src[1][:, c, :]), c == 0, c == KC - 1)
                        ins.then_inc(bank_ready, 1)

            def project_v(f, b):
                for g in range(2):
                    out = fill(f + g, b + g)
                    for half in range(2):
                        a = 2 * g + half
                        tok = slice(a * P, a * P + P)
                        for c in range(KC):
                            ins = halves_matmul(pe, out[:, half * D:(half + 1) * D],
                                                (ct_hi[:, c, tok], ct_lo[:, c, tok]),
                                                weights(2, c, slice(0, D)), c == 0, c == KC - 1)
                    ins.then_inc(bank_ready, 1)

            def row_scores(p, k, u):
                if u == 0:
                    pe.wait_ge(stacked, (p + 1) * 16 * STACK_DMAS)
                pe.wait_ge(max_done, p * SLOTS + u + 1)
                a, h0 = u // 8, 2 * (u % 8)
                keys = slice((a // 2) * D, (a // 2) * D + D)
                for n in range(2):
                    ins = pe.matmul(s_bank[u % 2][:, n, :],
                                    stack[k][0:MAX_ROW, h0 + n, 0, a * P:(a + 1) * P],
                                    stack[k][0:MAX_ROW, h0 + n, 1, keys], start=True, stop=True)
                ins.then_inc(s_ready, 1)

            def turn_maxima(p, f, b):
                out = fill(f, b)
                pe.wait_ge(max_done, (p + 1) * SLOTS + 2)
                for a in range(TT):
                    ins = pe.transpose(out[0:HEADS, a * P:(a + 1) * P], maxes[:, a, :], ident[:])
                ins.then_inc(bank_ready, 1)

            def slot(u):
                return u // 16, (u // 4) % 4, (u // 2) % 2, u % 2

            def col_scores(q, k, u):
                if u == 0:
                    pe.wait_ge(negmax_stacked, (q + 1) * 32)
                pe.wait_ge(exp_done, q * SLOTS + u + 1)
                j, i, c, hh = slot(u)
                keys = slice(j * D + c * P, j * D + c * P + P)
                for n in range(2):
                    h = 4 * i + 2 * hh + n
                    ins = pe.matmul(st_bank[u % 2][:, n, :], stack[k][0:STACK_ROWS, h, 1, keys],
                                    stack[k][0:STACK_ROWS, h, 0, j * D:(j + 1) * D], start=True, stop=True)
                ins.then_inc(st_ready, 1)

            def values(q, k, v):
                u = 2 * v
                j, i, c, _ = slot(u)
                pe.wait_ge(exp_done, q * SLOTS + u + 4)
                g2 = 2 * j + i // 2
                if v == 0:
                    pe.wait_ge(bank_free, fills(q)["start"])
                if i % 2 == 0 and c == 0:
                    pe.wait_ge(sums_ready, 4 * q + g2 + 1)
                for g in range(4):
                    s = (u + g // 2) % E_RING
                    ins = pe.matmul(pv_bank[g2 % 2][32 * g:32 * g + 32, i % 2, :],
                                    vals[k][:, 2 * j + c, 4 * i + g, :], expo[:, s, g % 2, :],
                                    start=(c == 0), stop=(c == 1), tile_position=(0, 32 * g))
                ins.then_inc(pv_done, 1)

            def turn_sums(q, k, n):
                out = fill(fills(q)["sums"][n], bank_of(q, k, "sums", n))
                pe.wait_ge(sums_ready, 4 * q + n + 1 + 2)
                for half in range(2):
                    for i in range(2):
                        at = (2 * half + i) * P
                        ins = pe.transpose(out[:, at:at + P], sums_t[n % 2][:, i, half * P:(half + 1) * P],
                                           ident[:])
                ins.then_inc(bank_ready, 1)

            def turn_heads(q, k):
                f, b = fills(q)["turn"], bank_of(q, k, "turn")
                pe.wait_ge(bank_free, fills(q)["sums"][3] + 1 + 2)
                for c in range(KC):
                    out = fill(f + c, b + c)
                    for a in range(TT):
                        ins = pe.transpose(out[:, a * P:(a + 1) * P],
                                           heads_n[:, a, c * 8:(c + 1) * 8, :].rearrange("p h d -> p (h d)"),
                                           ident[:])
                    ins.then_inc(bank_ready, 1)

            def output(q, k):
                f, b = fills(q)["out"], bank_of(q, k, "out")
                pe.wait_ge(bank_free, fills(q)["turn"] + 2 + 2)
                for g in range(2):
                    out = fill(f + g, b + g)
                    for half in range(2):
                        tok = slice((2 * g + half) * P, (2 * g + half + 1) * P)
                        for c in range(KC):
                            ins = halves_matmul(pe, out[:, half * D:(half + 1) * D],
                                                (ht_hi[:, c, tok], ht_lo[:, c, tok]),
                                                weights(3, c, slice(0, D)), c == 0, c == KC - 1)
                    ins.then_inc(bank_ready, 1)

            def first():
                project_qk(0, IN_0, IN_0)
                project_v(IN_0 + 6, IN_0 + 6)
                for u in range(SLOTS):
                    row_scores(0, 0, u)
                turn_maxima(0, MAX_0, MAX_0)
                project_qk(1, IN_1, IN_1)
                project_v(IN_1 + 6, IN_1 + 6)

            def step(q, k):
                f = fills(q)
                for u in range(SLOTS):
                    col_scores(q, k, u)
                    if u >= LAG and not is_last(q, 1):
                        row_scores(q + 1, 1 - k, u - LAG)
                    if u % 2 == 1 and u > 1:
                        values(q, k, u // 2 - 1)
                    if u % 8 == 6 and u > 8:
                        turn_sums(q, k, u // 8 - 1)
                values(q, k, SLOTS // 2 - 1)

                def trailing(n):
                    if n == 1:
                        turn_sums(q, k, 3)
                    if not is_last(q, 1):
                        row_scores(q + 1, 1 - k, SLOTS - LAG + n)

                trailing(0)
                trailing(1)
                if not is_last(q, 2):
                    project_qk(q + 2, f["proj"], bank_of(q, k, "proj"), lambda g: trailing(2 + g))
                else:
                    for n in range(2, LAG):
                        trailing(n)
                if not is_last(q, 1):
                    turn_maxima(q + 1, f["max"], bank_of(q, k, "max"))
                turn_heads(q, k)
                if not is_last(q, 2):
                    project_v(f["v"], bank_of(q, k, "v"))
                output(q, k)

            steady(pe, first, step, lambda: None)

        @block.scalar
        def _(act):
            act.sem_inc(exp_done, 2)
            act.sem_inc(sums_ready, 2)

            act.wait_ge(loaded, 48)

            def inputs(p, f, b):
                for c in range(KC):
                    act.wait_ge(bank_ready, f + c + 1)
                    act.copy(xt_hi[:, c, :], bank[(b + c) % 2][:]).then_inc(hi_ready, 1)
                for n in range(2):
                    for m in range(KC):
                        g = 2 + 2 * n + m
                        if g == 2 and not (isinstance(p, int) and p == 0):
                            act.wait_ge(unstacked, p * 16 * KC)
                        act.wait_ge(bank_ready, f + g + 1)
                        act.activation(qk[:, m, 2 * n, :], bank[(b + g) % 2][:], ACT.Identity,
                                       bias=bias_qk[:, n, m:m + 1]).then_inc(hi_ready, 1)

            def maxima(p, f, b):
                act.wait_ge(bank_ready, f + 1)
                if not (isinstance(p, int) and p == 0):
                    act.wait_ge(negmax_stacked, p * 32)
                act.mul(negmax[:, 0, :], bank[b % 2][0:HEADS, :], -1.0).then_inc(negmax_ready, 1)

            def exponentials(q, k, u):
                act.wait_ge(st_ready, q * SLOTS + u + 1)
                act.wait_ge(pv_done, q * (SLOTS // 2) + u // 2 + 1)
                act.activation(expo[:, u % E_RING, :, :], st_bank[u % 2][:], ACT.Exp,
                               scale=SCALE).then_inc(exp_done, 1)

            def copy_sums(q, n):
                act.wait_ge(pv_done, q * (SLOTS // 2) + 4 * (n + 1) + E_RING // 2)
                act.wait_ge(bank_ready, fills(q)["sums"][n - 2] + 1 if n > 1 else fills(q)["start"])
                act.copy(sums_t[n % 2][:], pv_bank[n % 2][:]).then_inc(sums_ready, 1)

            def heads_hi(q, k):
                f, b = fills(q)["turn"], bank_of(q, k, "turn")
                for c in range(KC):
                    act.wait_ge(bank_ready, f + c + 1)
                    act.copy(ht_hi[:, c, :], bank[(b + c) % 2][:]).then_inc(ht_hi_ready, 1)

            def first():
                inputs(0, IN_0, IN_0)
                maxima(0, MAX_0, MAX_0)
                inputs(1, IN_1, IN_1)

            def step(q, k):
                f = fills(q)
                for u in range(SLOTS):
                    exponentials(q, k, u)
                    if u % 8 == 3 and u > 8:
                        copy_sums(q, u // 8 - 1)
                copy_sums(q, 3)
                if not is_last(q, 2):
                    inputs(q + 2, f["proj"], bank_of(q, k, "proj"))
                if not is_last(q, 1):
                    maxima(q + 1, f["max"], bank_of(q, k, "max"))
                heads_hi(q, k)

            steady(act, first, step, lambda: None)

        @block.vector
        def _(dve):
            dve.sem_inc(bank_free, 2)
            dve.sem_inc(max_done, 2)
            dve.sem_inc(pv_done, E_RING // 2)
            for k in range(2):
                dve.memset(stack[k][64:P, :, :, :], 0.0)
                ins = dve.memset(vals[k][:], 1.0)
            ins.then_inc(cleared, 1)
            dve.wait_ge(cleared, 1)
            for k in range(2):
                ins = dve.memset(stack[k][96:P, :, 1, :], 1.0)
            ins.then_inc(const, 1)
            dve.wait_ge(loaded, 48)

            def normalize(p, k, reads):
                dve.wait_ge(x_loaded[k], (p - k) * 8 + 16)
                for a in range(TT):
                    ins = dve.bn_stats(stats[:, a, :], x_in[k][:, a, :])
                ins.then_inc(ln_step, 1)
                dve.wait_ge(ln_step, 2 * p + 1)
                dve.memset(hold[:], 0.0)
                for a in range(TT):
                    ins = dve.bn_aggr(mean_var[:, a, :], stats[:, a, :])
                ins.then_inc(ln_step, 1)
                dve.wait_ge(ln_step, 2 * p + 2)
                dve.tensor_scalar(var_eps[:], mean_var[:, :, 1], EPS, None, ALU.add).then_inc(var_ready, 1)
                dve.wait_ge(rstd_ready, p + 1)
                if reads is not None:
                    dve.wait_ge(bank_ready, reads)
                for a in range(TT):
                    ins = dve.tensor_scalar(xn[:, a, :], x_in[k][:, a, :], mean_var[:, a, 0:1],
                                            rstd[:, a:a + 1], ALU.subtract, ALU.mult)
                ins.then_inc(xn_ready, 1)

            def split_ctx(p, k, reads):
                dve.wait_ge(ctx_loaded[k], (p - k) * 8 + 16)
                if reads is not None:
                    dve.wait_ge(bank_ready, reads)
                    dve.wait_ge(ct_lo_ready, p)
                dve.tensor_copy(ct_hi[:], ctx_in[k][:]).then_inc(ct_hi_ready, 1)

            def split_qk(p, f, b, between=lambda g: None):
                for c in range(KC):
                    between(c)
                    dve.wait_ge(hi_ready, 6 * p + c + 1)
                    dve.tensor_tensor(xt_lo[:, c, :], bank[(b + c) % 2][:], xt_hi[:, c, :],
                                      ALU.subtract).then_inc(bank_free, 1)
                for n in range(2):
                    for m in range(KC):
                        g = 2 + 2 * n + m
                        between(g)
                        dve.wait_ge(hi_ready, 6 * p + g + 1)
                        dve.scalar_tensor_tensor(out=qk[:, m, 2 * n + 1, :], in0=bank[(b + g) % 2][:],
                                                 scalar=bias_qk[:, n, m:m + 1], in1=qk[:, m, 2 * n, :],
                                                 op0=ALU.add, op1=ALU.subtract).then_inc(bank_free, 1)

            def keep_v(k, f, b):
                for g in range(2):
                    dve.wait_ge(bank_ready, f + 1 + g)
                    for half in range(2):
                        ins = dve.tensor_tensor(
                            vals[k][:, 2 * g + half, :, 0:DH],
                            bank[(b + g) % 2][:, half * D:(half + 1) * D].rearrange("p (h d) -> p h d", d=DH),
                            bias_v[:].rearrange("p (h d) -> p h d", d=DH), ALU.add)
                    ins.then_inc(bank_free, 1)

            def row_max(p, u, reads=None):
                dve.wait_ge(s_ready, p * SLOTS + u + 1)
                if u == 0 and reads is not None:
                    dve.wait_ge(bank_ready, reads)
                a, h0 = u // 8, 2 * (u % 8)
                dve.tensor_reduce(maxes[:, a, h0:h0 + 2], s_bank[u % 2][:], AX_X, ALU.max)\
                    .then_inc(max_done, 1)

            def maxima(p, f, b):
                dve.wait_ge(negmax_ready, p + 1)
                dve.scalar_tensor_tensor(out=negmax[:, 1, :], in0=bank[b % 2][0:HEADS, :], scalar=-1.0,
                                         in1=negmax[:, 0, :], op0=ALU.mult, op1=ALU.subtract)\
                    .then_inc(bank_free, 1)

            def divide(q, k, n):
                f, b = fills(q)["sums"][n], bank_of(q, k, "sums", n)
                dve.wait_ge(bank_ready, f + 1)
                dve.reciprocal(inverse[:, n % 2], bank[b][:, DH::32]).then_inc(inverse_ready, 1)
                dve.wait_ge(inverse_ready, 4 * q + n + 1)
                j, h = n // 2, 8 * (n % 2)
                dve.tensor_tensor(heads_n[:, 2 * j:2 * j + 2, h:h + 8, :],
                                  bank[b][:].rearrange("p (a h d) -> p a h d", a=2, d=32)[:, :, :, 0:DH],
                                  inverse[:, n % 2].rearrange("p (a h) -> p a h", a=2).unsqueeze(3)
                                  .to_broadcast([P, 2, 8, DH]), ALU.mult).then_inc(bank_free, 1)

            def heads_lo(q, k):
                b = bank_of(q, k, "turn")
                for c in range(KC):
                    dve.wait_ge(ht_hi_ready, KC * q + c + 1)
                    dve.tensor_tensor(ht_lo[:, c, :], bank[(b + c) % 2][:], ht_hi[:, c, :],
                                      ALU.subtract).then_inc(bank_free, 1)

            def output(q, k):
                f, b = fills(q)["out"], bank_of(q, k, "out")
                dve.wait_ge(res_ready, q + 1)
                dve.wait_ge(x1_stored[k], (q - k) * 8 + 16)
                for g in range(2):
                    dve.wait_ge(bank_ready, f + g + 1)
                    dve.tensor_tensor(x1[k][:, 2 * g:2 * g + 2, :],
                                      bank[(b + g) % 2][:].rearrange("p (a d) -> p a d", d=D),
                                      x_res[k][:, 2 * g:2 * g + 2, :], ALU.add).then_inc(bank_free, 1)

            def first():
                normalize(0, 0, None)
                split_ctx(0, 0, None)
                split_qk(0, IN_0, IN_0)
                keep_v(0, IN_0 + 6, IN_0 + 6)
                normalize(1, 1, IN_0 + 2)
                split_ctx(1, 1, IN_0 + 8)
                for u in range(SLOTS):
                    row_max(0, u)
                maxima(0, MAX_0, MAX_0)
                split_qk(1, IN_1, IN_1)
                keep_v(1, IN_1 + 6, IN_1 + 6)

            def step(q, k):
                f = fills(q)
                for u in range(SLOTS):
                    if u >= LAG and not is_last(q, 1):
                        row_max(q + 1, u - LAG, f["start"])
                    if u == 12 and not is_last(q, 2):
                        normalize(q + 2, k, f["start"])
                        split_ctx(q + 2, k, f["start"])
                    if u % 8 == 7 and u > 8:
                        divide(q, k, u // 8 - 1)

                def trailing(n):
                    if not is_last(q, 1):
                        row_max(q + 1, SLOTS - LAG + n)
                    if n == 1:
                        divide(q, k, 3)

                trailing(0)
                trailing(1)
                if not is_last(q, 2):
                    split_qk(q + 2, f["proj"], bank_of(q, k, "proj"), lambda g: trailing(2 + g))
                else:
                    for n in range(2, LAG):
                        trailing(n)
                if not is_last(q, 1):
                    maxima(q + 1, f["max"], bank_of(q, k, "max"))
                heads_lo(q, k)
                if not is_last(q, 2):
                    keep_v(k, f["v"], bank_of(q, k, "v"))
                output(q, k)

            steady(dve, first, step, lambda: None)


def route(nc, dram, tables, NB):
    with ExitStack() as ctx:
        sb = lambda n, s, d: ctx.enter_context(nc.sbuf_tensor(n, s, d))
        pb = lambda n, s, d: ctx.enter_context(nc.psum_tensor(n, s, d))
        sem = lambda n: ctx.enter_context(nc.semaphore(n))

        gate_w = sb("gate_w", [P, KC, EXPERTS], F32)
        gate_hi = sb("gate_hi", [P, KC, EXPERTS], BF16)
        gate_lo = sb("gate_lo", [P, KC, EXPERTS], BF16)
        x1 = [sb(f"r_x1_{k}", [P, TT, D], F32) for k in range(2)]
        row = [sb(f"row{k}", [P, TT, ROW], F32) for k in range(2)]
        stats = sb("r_stats", [P, TT, 6], F32)
        mean_var = sb("r_mean_var", [P, TT, 2], F32)
        var_eps = sb("r_var_eps", [P, TT], F32)
        rstd = sb("r_rstd", [P, TT], F32)
        power = sb("r_power", [P, TT], F32)
        hold = sb("r_hold", [P, 1], F32)
        hold_pool = sb("r_hold_pool", [P, 4], F32)
        xt_hi = sb("r_xt_hi", [P, KC, TOK], BF16)
        xt_lo = sb("r_xt_lo", [P, KC, TOK], BF16)
        logits = sb("logits", [P, TT, EXPERTS], F32)
        score_max = sb("score_max", [P, TT], F32)
        scores = sb("scores", [P, TT, EXPERTS], F32)
        top = sb("top", [P, TT, 8], F32)
        top_at = sb("top_at", [P, TT, 8], U32)
        top_f = sb("top_f", [P, TT, 2], F32)
        top_sum = sb("top_sum", [P, TT], F32)
        top_inv = sb("top_inv", [P, TT], F32)
        weight = sb("weight", [P, TT, 2], F32)
        token = sb("token", [P, TT], F32)
        picks = sb("picks", [P, TT, 2, EXPERTS], F32)
        mask = sb("mask", [P, TT, EXPERTS], BF16)
        place = sb("place", [P, TT, EXPERTS], F32)
        taken = sb("taken", [P, EXPERTS], F32)
        picked = sb("picked", [P, TT, 2, EXPERTS], F32)
        slot_f = sb("slot_f", [P, TT, 2], F32)
        slot = [sb(f"slot{k}", [P, TT * 2], U32) for k in range(2)]
        number = sb("number", [P, EXPERTS + 1], F32)
        base = sb("base", [P, EXPERTS], F32)
        ident = sb("r_ident", [P, P], F32)
        ones = sb("r_ones", [P, P], F32)
        ones_b = sb("ones_b", [P, P], BF16)
        before = sb("before", [P, P], BF16)
        padding = sb("padding", [P, TT, ROW], F32)
        PARTS = TOKENS // TOK
        steps = sb("tile_steps", [P, EXPERTS, PARTS - 1], F32)
        over = sb("over", [P, EXPERTS, PARTS - 1], F32)
        count = sb("count", [P, EXPERTS], F32)
        tiles = sb("tiles", [P, EXPERTS], F32)
        earlier = sb("earlier", [P, EXPERTS + 1, EXPERTS], F32)
        start_f = sb("start_f", [P, EXPERTS + 1], F32)

        x_bank = [pb(f"x_bank{c}", [P, TOK], F32) for c in range(KC)]
        gate_bank = pb("gate_bank", [P, 512], F32)
        rank_bank = pb("rank_bank", [P, 512], F32)

        const_loaded = sem("r_const_loaded")
        const = sem("r_const")
        x1_loaded = [sem(f"r_x1_loaded{k}") for k in range(2)]
        step_done = sem("r_step")
        var_ready = sem("r_var_ready")
        rstd_ready = sem("r_rstd_ready")
        xn_ready = sem("r_xn_ready")
        xt_ready = sem("r_xt_ready")
        xt_hi_ready = sem("r_xt_hi_ready")
        xt_lo_ready = sem("r_xt_lo_ready")
        logits_ready = sem("logits_ready")
        gate_step = sem("gate_step")
        exp_ready = sem("r_exp_ready")
        rank_ready = sem("rank_ready")
        slots_ready = sem("slots_ready")
        row_free = sem("row_free")
        scattered = [sem(f"scattered{k}") for k in range(2)]
        cleared = sem("r_cleared")
        table_step = sem("table_step")
        table_ready = sem("table_ready")
        padded = sem("padded")
        STEPS = 14
        CONST = 11

        block = ctx.enter_context(nc.Block())

        @block.sync
        def _(sp):
            sp.dma_start(gate_w[:], dram["wg"]).then_inc(const_loaded, 16)
            with sp.Fori(0, NB // 2) as i:
                for k in range(2):
                    b = i * 2 + k
                    sp.wait_ge(xn_ready, b + 1)
                    sp.dma_start(x1[k][:], dram["x1"][b]).then_inc(x1_loaded[k], 16)
            sp.wait_ge(const, CONST)
            sp.dma_start(dram["y"][TOKENS:TOKENS + TOK].rearrange("(a p) d -> p a d", p=P),
                         padding[:, :, 0:D]).then_inc(cleared, 16)
            sp.wait_ge(table_ready, 2)
            for k in range(2):
                sp.wait_ge(scattered[k], 16 * 2 * TT * (NB // 2))
            with sp.Fori(0, EXPERTS) as e:
                end = sp.value_load(tables["row_end"][0:1, bass.ds(e, 1)], min_val=0,
                                    max_val=EXPERTS * REGION - TOK)
                sp.dma_start(dram["rows"][bass.ds(end, TOK)].rearrange("(a p) d -> p a d", p=P),
                             padding[:]).then_inc(padded, 16)
            sp.wait_ge(padded, 16 * EXPERTS)
            sp.wait_ge(cleared, 16)

        @block.gpsimd
        def _(pool):
            pool.memset(ones[:], 1.0).then_inc(const, 1)
            pool.memset(ones_b[:], 1.0).then_inc(const, 1)
            pool.memset(padding[:], 0.0).then_inc(const, 1)
            pool.wait_ge(const, 3)
            pool.affine_select(out=ident[:], in_=ones[:], compare_op=ALU.is_equal, fill=0.0, base=0,
                               pattern=[[-1, P]], channel_multiplier=1).then_inc(const, 1)
            pool.affine_select(out=before[:], in_=ones_b[:], compare_op=ALU.is_gt, fill=0.0, base=0,
                               pattern=[[1, P]], channel_multiplier=-1).then_inc(const, 1)
            pool.iota(number[:], pattern=[[1, EXPERTS + 1]], base=0, channel_multiplier=0,
                      allow_small_or_imprecise_dtypes=True).then_inc(const, 1)
            pool.iota(base[:], pattern=[[REGION, EXPERTS]], base=0, channel_multiplier=0,
                      allow_small_or_imprecise_dtypes=True)
            pool.iota(token[:], pattern=[[P, TT]], base=0, channel_multiplier=1,
                      allow_small_or_imprecise_dtypes=True)
            pool.iota(steps[:], pattern=[[0, EXPERTS], [TOK, PARTS - 1]], base=TOK, channel_multiplier=0,
                      allow_small_or_imprecise_dtypes=True)
            pool.iota(padding[:, :, ROW - 1], pattern=[[P, TT]], base=TOKENS, channel_multiplier=1,
                      allow_small_or_imprecise_dtypes=True).then_inc(const, 1)
            pool.wait_ge(const, 7)
            pool.tensor_copy(taken[:], base[:]).then_inc(const, 1)
            pool.wait_ge(const_loaded, 16)
            pool.tensor_copy(gate_hi[:], gate_w[:]).then_inc(const, 1)
            pool.wait_ge(const, 9)
            pool.tensor_tensor(gate_lo[:], gate_w[:], gate_hi[:], ALU.subtract).then_inc(const, 1)
            pool.memset(power[:], -0.5).then_inc(const, 1)
            pool.wait_ge(const, CONST)
            with pool.Fori(0, NB // 2) as i:
                for k in range(2):
                    b = i * 2 + k
                    pool.wait_ge(var_ready, b + 1)
                    pool.tensor_tensor(rstd[:], var_eps[:], power[:], ALU.pow).then_inc(rstd_ready, 1)
                    pool.wait_ge(slots_ready, b + 1)
                    pool.tensor_tensor(hold_pool[:, k:k + 1], ones[:, 0:1], ones[:, 0:1], ALU.subtract)
                    for a in range(TT):
                        for n in range(2):
                            pool.indirect_dma_start(
                                out=dram["rows"],
                                out_offset=bass.IndirectOffsetOnAxis(ap=slot[k][:, 2 * a + n:2 * a + n + 1], axis=0),
                                in_=row[k][:, a, :], in_offset=None).then_inc(scattered[k], 16)
                    pool.wait_ge(scattered[k], (i + 1) * (2 * TT * 16))
                    pool.tensor_tensor(hold_pool[:, 2 + k:3 + k], ones[:, 0:1], ones[:, 0:1], ALU.subtract)\
                        .then_inc(row_free, 1)

        @block.tensor
        def _(pe):
            pe.wait_ge(const, CONST)
            with pe.Fori(0, NB // 2) as i:
                for k in range(2):
                    b = i * 2 + k
                    pe.wait_ge(xn_ready, b + 3)
                    for c in range(KC):
                        for a in range(TT):
                            ins = pe.transpose(x_bank[c][:, a * P:(a + 1) * P],
                                               row[k][:, a, c * P:(c + 1) * P], ident[:])
                        ins.then_inc(xt_ready, 1)
                    pe.wait_ge(xt_lo_ready, KC * (b + 1))
                    for a in range(TT):
                        for c in range(KC):
                            lhs = [x[:, c, a * P:(a + 1) * P] for x in (xt_hi, xt_lo)]
                            ins = halves_matmul(pe, gate_bank[:, a * EXPERTS:(a + 1) * EXPERTS], lhs,
                                                (gate_hi[:, c, :], gate_lo[:, c, :]), c == 0, c == KC - 1)
                    ins.then_inc(logits_ready, 1)
                    pe.wait_ge(gate_step, STEPS * b + 9)
                    for a in range(TT + 1):
                        for c in range(min(a + 1, TT)):
                            ins = pe.matmul(rank_bank[:, a * EXPERTS:(a + 1) * EXPERTS],
                                            before[:] if c == a else ones_b[:], mask[:, c, :],
                                            start=c == 0, stop=c == min(a, TT - 1))
                    ins.then_inc(rank_ready, 1)

        @block.scalar
        def _(act):
            with act.Fori(0, NB) as b:
                for c in range(KC):
                    act.wait_ge(xt_ready, KC * b + c + 1)
                    act.copy(xt_hi[:, c, :], x_bank[c][:]).then_inc(xt_hi_ready, 1)
                act.wait_ge(gate_step, STEPS * b + 2)
                act.activation(scores[:], logits[:], ACT.Exp).then_inc(exp_ready, 1)

        @block.vector
        def _(dve):
            dve.sem_inc(xn_ready, 2)
            dve.sem_inc(row_free, 2)
            dve.wait_ge(const, CONST)
            with dve.Fori(0, NB // 2) as i:
                for k in range(2):
                    b = i * 2 + k
                    dve.wait_ge(x1_loaded[k], 16 * i + 16)
                    for a in range(TT):
                        ins = dve.bn_stats(stats[:, a, :], x1[k][:, a, :])
                    ins.then_inc(step_done, 1)
                    dve.wait_ge(step_done, 2 * b + 1)
                    dve.memset(hold[:], 0.0)
                    for a in range(TT):
                        ins = dve.bn_aggr(mean_var[:, a, :], stats[:, a, :])
                    ins.then_inc(step_done, 1)
                    dve.wait_ge(step_done, 2 * b + 2)
                    dve.tensor_scalar(var_eps[:], mean_var[:, :, 1], EPS, None, ALU.add).then_inc(var_ready, 1)
                    dve.wait_ge(rstd_ready, b + 1)
                    dve.wait_ge(row_free, b + 1)
                    for a in range(TT):
                        ins = dve.tensor_scalar(row[k][:, a, 0:D], x1[k][:, a, :], mean_var[:, a, 0:1],
                                                rstd[:, a:a + 1], ALU.subtract, ALU.mult)
                    ins.then_inc(xn_ready, 1)
                    for c in range(KC):
                        dve.wait_ge(xt_hi_ready, KC * b + c + 1)
                        dve.tensor_tensor(xt_lo[:, c, :], x_bank[c][:], xt_hi[:, c, :], ALU.subtract)\
                            .then_inc(xt_lo_ready, 1)

                    def done(ins, n):
                        ins.then_inc(gate_step, 1)
                        dve.wait_ge(gate_step, STEPS * b + n)

                    def wide(x):
                        return x.unsqueeze(3).to_broadcast([P, TT, 2, EXPERTS])

                    dve.wait_ge(logits_ready, b + 1)
                    done(dve.tensor_reduce(score_max[:], gate_bank[:, 0:TT * EXPERTS].rearrange(
                        "p (a e) -> p a e", e=EXPERTS), AX_X, ALU.max), 1)
                    done(dve.tensor_tensor(logits[:], gate_bank[:, 0:TT * EXPERTS].rearrange(
                        "p (a e) -> p a e", e=EXPERTS), score_max[:].unsqueeze(2).to_broadcast([P, TT, EXPERTS]),
                        ALU.subtract), 2)
                    dve.wait_ge(exp_ready, b + 1)
                    dve.memset(hold[:], 0.0)
                    for a in range(TT):
                        ins = dve.max(top[:, a, :], scores[:, a, :])
                    done(ins, 3)
                    dve.memset(hold[:], 0.0)
                    for a in range(TT):
                        ins = dve.max_index(top_at[:, a, :], top[:, a, :], scores[:, a, :])
                    done(ins, 4)
                    dve.tensor_copy(top_f[:], top_at[:, :, 0:2])
                    done(dve.tensor_tensor(top_sum[:], top[:, :, 0], top[:, :, 1], ALU.add), 5)
                    done(dve.reciprocal(top_inv[:], top_sum[:]), 6)
                    dve.tensor_tensor(weight[:], top[:, :, 0:2],
                                      top_inv[:].unsqueeze(2).to_broadcast([P, TT, 2]), ALU.mult)
                    done(dve.tensor_tensor(
                        picks[:], number[:, 0:EXPERTS].unsqueeze(1).unsqueeze(1).to_broadcast([P, TT, 2, EXPERTS]),
                        wide(top_f[:]), ALU.is_equal), 7)
                    dve.tensor_copy(row[k][:, :, D], weight[:, :, 1])
                    dve.tensor_tensor(row[k][:, :, D + 1], weight[:, :, 0], weight[:, :, 1], ALU.subtract)
                    dve.tensor_copy(row[k][:, :, D + 2], top_f[:, :, 0])
                    done(dve.tensor_copy(row[k][:, :, D + 3], token[:]), 8)
                    done(dve.tensor_tensor(mask[:], picks[:, :, 0, :], picks[:, :, 1, :], ALU.add), 9)
                    dve.tensor_scalar(token[:], token[:], float(TOK), None, ALU.add)
                    dve.wait_ge(rank_ready, b + 1)
                    done(dve.tensor_tensor(
                        place[:], rank_bank[:, 0:TT * EXPERTS].rearrange("p (a e) -> p a e", e=EXPERTS),
                        taken[:].unsqueeze(1).to_broadcast([P, TT, EXPERTS]), ALU.add), 10)
                    done(dve.tensor_tensor(taken[:], rank_bank[:, TT * EXPERTS:(TT + 1) * EXPERTS], taken[:],
                                           ALU.add), 11)
                    done(dve.tensor_tensor(picked[:], picks[:], place[:].unsqueeze(2).to_broadcast(
                        [P, TT, 2, EXPERTS]), ALU.mult), 12)
                    done(dve.tensor_reduce(slot_f[:], picked[:], AX_X, ALU.add), 13)
                    done(dve.tensor_copy(slot[k][:], slot_f[:].rearrange("p a n -> p (a n)")), 14)
                    dve.sem_inc(slots_ready, 1)

            def table(ins, n):
                ins.then_inc(table_step, 1)
                dve.wait_ge(table_step, n)

            table(dve.tensor_tensor(count[:], taken[:], base[:], ALU.subtract), 1)
            table(dve.tensor_tensor(over[:], count[:].unsqueeze(2).to_broadcast([P, EXPERTS, PARTS - 1]),
                                    steps[:], ALU.is_gt), 2)
            table(dve.tensor_reduce(tiles[:], over[:], AX_X, ALU.add), 3)
            table(dve.tensor_scalar(tiles[:], tiles[:], 1.0, None, ALU.add), 4)
            shape = [P, EXPERTS + 1, EXPERTS]
            table(dve.tensor_tensor(earlier[:], number[:].unsqueeze(2).to_broadcast(shape),
                                    number[:, 0:EXPERTS].unsqueeze(1).to_broadcast(shape), ALU.is_gt), 5)
            table(dve.tensor_tensor(earlier[:], earlier[:], tiles[:].unsqueeze(1).to_broadcast(shape),
                                    ALU.mult), 6)
            table(dve.tensor_reduce(start_f[:], earlier[:], AX_X, ALU.add), 7)
            dve.tensor_copy(tables["tile_start"][:], start_f[:]).then_inc(table_ready, 1)
            dve.tensor_copy(tables["row_end"][:, 0:EXPERTS], taken[:]).then_inc(table_ready, 1)


def experts(nc, dram, tables):
    with ExitStack() as ctx:
        sb = lambda n, s, d: ctx.enter_context(nc.sbuf_tensor(n, s, d))
        pb = lambda n, s, d: ctx.enter_context(nc.psum_tensor(n, s, d))
        sem = lambda n: ctx.enter_context(nc.semaphore(n))

        w = [sb(f"w{k}", [P, 2, UNITS * 512], BF16) for k in range(2)]
        b13 = [sb(f"b13_{k}", [P, 2, MC], F32) for k in range(2)]
        b2 = [sb(f"b2_{k}", [P, D], F32) for k in range(2)]
        rows = sb("rows", [P, TT, ROW], F32)
        meta = sb("meta", [P, TT, ROW - D], F32)
        xt_hi = sb("f_xt_hi", [P, KC, TOK], BF16)
        xt_lo = sb("f_xt_lo", [P, KC, TOK], BF16)
        silu = sb("silu", [P, 2, TOK], F32)
        act_f = sb("act_f", [P, 2, TOK], F32)
        act_hi = sb("act_hi", [P, MC, TOK], BF16)
        act_lo = sb("act_lo", [P, MC, TOK], BF16)
        y_sum = sb("y_sum", [P, TT, D], F32)
        y_out = sb("y_out", [P, TT, D], F32)
        first_pick = sb("first_pick", [P, TT], F32)
        gate = sb("gate", [P, TT], F32)
        token = sb("f_token", [P, TT], U32)
        number = sb("f_number", [P, EXPERTS], F32)
        hold = sb("f_hold", [P, TT + 1], F32)
        ident = sb("f_ident", [P, P], F32)
        ones = sb("f_ones", [P, P], F32)

        y_bank = [pb(f"y_bank{a}", [P, 512], F32) for a in range(TT)]
        h1_bank = [pb(f"h1_bank{k}", [P, TOK], F32) for k in range(2)]
        h3_bank = [pb(f"h3_bank{k}", [P, TOK], F32) for k in range(2)]
        x_bank = [h1_bank[0], h3_bank[0]]

        const = sem("f_const")
        w_loaded = [sem(f"w_loaded{k}") for k in range(2)]
        expert_done = sem("expert_done")
        rows_loaded = sem("rows_loaded")
        rows_free = sem("rows_free")
        xt_ready = sem("f_xt_ready")
        xt_hi_ready = sem("f_xt_hi_ready")
        xt_lo_ready = sem("f_xt_lo_ready")
        h_ready = sem("h_ready")
        silu_ready = sem("silu_ready")
        g_ready = sem("g_ready")
        g_hi_ready = sem("g_hi_ready")
        g_lo_ready = sem("g_lo_ready")
        gate_ready = sem("gate_ready")
        y_ready = sem("y_ready")
        y_read = sem("y_read")
        y_scaled = sem("y_scaled")
        y_scattered = sem("y_scattered")
        tile_out = sem("tile_out")
        GATE_STEPS = 4
        LOADS = 3

        block = ctx.enter_context(nc.Block())

        def bounds(engine, e):
            return [engine.value_load(tables["tile_start"][0:1, bass.ds(e + n, 1)], min_val=0, max_val=MAX_TILES)
                    for n in range(2)]

        def every_tile(engine, start, tile, end=None):
            with engine.Fori(0, EXPERTS // 2) as i:
                for k in range(2):
                    e = i * 2 + k
                    first, last = bounds(engine, e)
                    start(e, i, k)
                    with engine.Fori(first, last) as T:
                        tile(T, e, i, k, first)
                    if end:
                        end(last)

        def nothing(e, i, k):
            pass

        @block.sync
        def _(sp):
            def load_weights(e, i, k):
                sp.wait_ge(expert_done, e + 1)
                sp.dma_start(w[k][:], dram["experts"][e].rearrange("p h u n -> p h (u n)")).then_inc(w_loaded[k], 16)
                sp.dma_start(b13[k][:], dram["bias13"][e]).then_inc(w_loaded[k], 16)
                sp.dma_start(b2[k][:], dram["bias2"][e].partition_broadcast(P)).then_inc(w_loaded[k], 16)

            def load_rows(T, e, i, k, first):
                sp.wait_ge(rows_free, T + 1)
                at = nc.s_assert_within(
                    sp.snap(e * REGION + (T - first) * TOK), 0, EXPERTS * REGION - TOK,
                    skip_runtime_bounds_check_because="an expert's tiles lie within its region")
                sp.dma_start(rows[:], dram["rows"][bass.ds(at, TOK)].rearrange("(a p) d -> p a d", p=P))\
                    .then_inc(rows_loaded, 16)

            every_tile(sp, load_weights, load_rows)
            total = sp.value_load(tables["tile_start"][0:1, EXPERTS:EXPERTS + 1], min_val=EXPERTS, max_val=MAX_TILES)
            sp.wait_ge(rows_free, total + 1)
            sp.dma_start(rows[:], dram["rows"][0:TOK].rearrange("(a p) d -> p a d", p=P)).then_inc(rows_loaded, 16)

        @block.gpsimd
        def _(pool):
            pool.memset(ones[:], 1.0).then_inc(const, 1)
            pool.wait_ge(const, 1)
            pool.affine_select(out=ident[:], in_=ones[:], compare_op=ALU.is_equal, fill=0.0, base=0,
                               pattern=[[-1, P]], channel_multiplier=1).then_inc(const, 1)
            pool.iota(number[:], pattern=[[1, EXPERTS]], base=0, channel_multiplier=0,
                      allow_small_or_imprecise_dtypes=True).then_inc(const, 1)
            pool.sem_inc(g_lo_ready, 2)

            def tile(T, e, i, k, first):
                for m in range(MC):
                    pool.wait_ge(g_hi_ready, T * MC + m + 1)
                    pool.tensor_tensor(act_lo[:, m, :], act_f[:, m % 2, :], act_hi[:, m, :],
                                       ALU.subtract).then_inc(g_lo_ready, 1)
                for a in range(TT):
                    pool.wait_ge(y_scaled, T * TT + a + 1)
                    pool.tensor_tensor(hold[:, a:a + 1], ones[:, 0:1], ones[:, 0:1], ALU.subtract)
                    pool.indirect_dma_start(
                        out=dram["y"], out_offset=bass.IndirectOffsetOnAxis(ap=token[:, a:a + 1], axis=0),
                        in_=y_out[:, a, :], in_offset=None, compute_op=ALU.add).then_inc(y_scattered, 16)
                pool.wait_ge(y_scattered, T * (16 * TT) + 16 * TT)
                pool.tensor_tensor(hold[:, TT:TT + 1], ones[:, 0:1], ones[:, 0:1], ALU.subtract)\
                    .then_inc(tile_out, 1)

            every_tile(pool, nothing, tile)

        @block.tensor
        def _(pe):
            def turn(T):
                pe.wait_ge(rows_loaded, T * 16 + 16)
                for c in range(KC):
                    for a in range(TT):
                        ins = pe.transpose(x_bank[c][:, a * P:(a + 1) * P], rows[:, a, c * P:(c + 1) * P], ident[:])
                    ins.then_inc(xt_ready, 1)

            def tile(T, e, i, k, first):
                pe.wait_ge(w_loaded[k], (i + 1) * (16 * LOADS))
                pe.wait_ge(xt_lo_ready, T * KC + KC)
                for m in range(MC):
                    pe.wait_ge(g_ready, T * MC + m + 1)
                    for kind, out in ((0, h1_bank), (1, h3_bank)):
                        for c in range(KC):
                            at = (2 * kind + c) * 512 + m * P
                            ins = halves_matmul(pe, out[m % 2][:], (w[k][:, 0, at:at + P], w[k][:, 1, at:at + P]),
                                                (xt_hi[:, c, :], xt_lo[:, c, :]), c == 0, c == KC - 1)
                    ins.then_inc(h_ready, 1)
                pe.wait_ge(g_ready, T * MC + 5)
                turn(T + 1)
                for m in range(MC):
                    pe.wait_ge(g_lo_ready, T * MC + m + 3)
                    for a in range(TT):
                        if m == 0:
                            pe.wait_ge(y_read, T * TT + a + 1)
                        tok = slice(a * P, (a + 1) * P)
                        at = 4 * 512 + m * D
                        ins = halves_matmul(pe, y_bank[a][:, 0:D], (act_hi[:, m, tok], act_lo[:, m, tok]),
                                            (w[k][:, 0, at:at + D], w[k][:, 1, at:at + D]), m == 0, m == MC - 1)
                        if m == MC - 1:
                            ins.then_inc(y_ready, 1)

            pe.wait_ge(const, 3)
            turn(0)
            every_tile(pe, nothing, tile)

        @block.scalar
        def _(act):
            def high(T):
                for c in range(KC):
                    act.wait_ge(xt_ready, T * KC + c + 1)
                    act.copy(xt_hi[:, c, :], x_bank[c][:]).then_inc(xt_hi_ready, 1)

            def tile(T, e, i, k, first):
                for m in range(MC):
                    act.wait_ge(h_ready, T * MC + m + 1)
                    act.activation(silu[:, m % 2, :], h1_bank[m % 2][:], ACT.Silu,
                                   bias=b13[k][:, 0, m:m + 1]).then_inc(silu_ready, 1)
                    act.wait_ge(g_ready, T * MC + m + 3)
                    act.copy(act_hi[:, m, :], act_f[:, m % 2, :]).then_inc(g_hi_ready, 1)
                high(T + 1)
                act.wait_ge(gate_ready, T * GATE_STEPS + GATE_STEPS)
                for a in range(TT):
                    act.wait_ge(y_read, T * TT + TT + a + 1)
                    act.activation(y_out[:, a, :], y_sum[:, a, :], ACT.Copy,
                                   scale=gate[:, a:a + 1]).then_inc(y_scaled, 1)

            high(0)
            every_tile(act, nothing, tile)

        @block.vector
        def _(dve):
            def low(T):
                for c in range(KC):
                    dve.wait_ge(xt_hi_ready, T * KC + c + 1)
                    dve.tensor_tensor(xt_lo[:, c, :], x_bank[c][:], xt_hi[:, c, :], ALU.subtract)\
                        .then_inc(xt_lo_ready, 1)
                dve.tensor_copy(meta[:], rows[:, :, D:ROW]).then_inc(rows_free, 1)

            def tile(T, e, i, k, first):
                for m in range(MC):
                    dve.wait_ge(silu_ready, T * MC + m + 1)
                    dve.wait_ge(g_lo_ready, T * MC + m + 1)
                    dve.scalar_tensor_tensor(out=act_f[:, m % 2, :], in0=h3_bank[m % 2][:],
                                             scalar=b13[k][:, 1, m:m + 1], in1=silu[:, m % 2, :],
                                             op0=ALU.add, op1=ALU.mult).then_inc(g_ready, 1)
                dve.wait_ge(rows_free, T + 2)
                dve.wait_ge(tile_out, T + 1)
                dve.tensor_copy(token[:], meta[:, :, 3]).then_inc(gate_ready, 1)
                dve.tensor_scalar(first_pick[:], meta[:, :, 2], number[:, bass.ds(e, 1)], None,
                                  ALU.is_equal).then_inc(gate_ready, 1)
                dve.wait_ge(gate_ready, T * GATE_STEPS + 2)
                dve.tensor_tensor(first_pick[:], first_pick[:], meta[:, :, 1], ALU.mult).then_inc(gate_ready, 1)
                dve.wait_ge(gate_ready, T * GATE_STEPS + 3)
                dve.tensor_tensor(gate[:], first_pick[:], meta[:, :, 0], ALU.add).then_inc(gate_ready, 1)
                dve.wait_ge(gate_ready, T * GATE_STEPS + 4)
                low(T + 1)
                for a in range(TT):
                    dve.wait_ge(y_ready, T * TT + a + 1)
                    dve.tensor_tensor(y_sum[:, a, :], y_bank[a][:, 0:D], b2[k][:], ALU.add).then_inc(y_read, 1)

            def end(last):
                dve.wait_ge(y_read, last * TT + TT)
                dve.sem_inc(expert_done, 1)

            dve.sem_inc(expert_done, 2)
            dve.sem_inc(rows_free, 1)
            dve.sem_inc(tile_out, 1)
            dve.sem_inc(g_ready, 2)
            dve.sem_inc(y_read, TT)
            dve.wait_ge(const, 3)
            low(0)
            every_tile(dve, nothing, tile, end)


def build(nc, ins, out):
    NB = 16
    tokens = lambda a: a.rearrange("b s d -> (b s) d").rearrange("(q a p) d -> q p a d", a=TT, p=P)
    scratch = lambda n, s, d: nc.dram_tensor(n, s, d, kind="Internal").ap()
    dram = dict(ins)
    dram["x"] = tokens(ins["x"])
    dram["x1"] = tokens(out[0:TOKENS].rearrange("(b s) d -> b s d", b=2 * NB))
    dram["y"] = out
    dram["rows"] = scratch("expert_rows", [EXPERTS * REGION, ROW], F32)
    qk = scratch("qk_scratch", [2, 4, D, TOK], BF16)
    dram["qk"] = qk.rearrange("b s (c p) n -> b c p s n", p=P)
    dram["qk_by_row"] = qk.rearrange("b s (h j) n -> b s j h n", j=DH)
    dram["experts"] = scratch("experts_scratch", [EXPERTS, P, 2, UNITS, 512], BF16)
    with ExitStack() as ctx:
        width = 4 * KC * D
        wq_sb = {h: ctx.enter_context(nc.sbuf_tensor(f"proj_{h}", [P, width], BF16)) for h in ("hi", "lo")}
        prepare_weights(nc, None, dram, wq_sb, NB)
        attention(nc, None, dram, wq_sb, NB)
    with ExitStack() as ctx:
        tables = {n: ctx.enter_context(nc.sbuf_tensor(n, [P, EXPERTS + 1], I32))
                  for n in ("row_end", "tile_start")}
        route(nc, dram, tables, NB)
        experts(nc, dram, tables)


def lay_out(inputs):
    import numpy as np

    def arr(name):
        return np.asarray(inputs[name])

    def rows(w):
        w = np.swapaxes(w, -1, -2)
        w = w.reshape(w.shape[:-2] + (w.shape[-2] // P, P, w.shape[-1]))
        return np.ascontiguousarray(np.swapaxes(w, -2, -3))

    a = {"x": arr("x")}
    a["ctx"] = np.ascontiguousarray(arr("ctx_1024").reshape(16, TOK, KC, P).transpose(0, 3, 2, 1))
    a["w_qkvo"] = np.concatenate([rows(arr(f"L0_xattn_w{n}")).reshape(P, KC * D) for n in "qkvo"], axis=1)
    a["bias_qk"] = np.ascontiguousarray(
        np.stack([arr("L0_xattn_bq"), arr("L0_xattn_bk")]).reshape(2, KC, P).transpose(2, 0, 1))
    a["bias_v"] = arr("L0_xattn_bv")
    a["bias_o"] = arr("L0_xattn_bo")
    a["wg"] = rows(arr("L0_ffn_Wg"))
    for n in "132":
        a[f"w{n}"] = rows(arr(f"L0_ffn_W{n}")).reshape(EXPERTS, P, 2, 512)
        a[f"a{n}"] = arr(f"L0_ffn_A{n}")
        a[f"b{n}"] = np.ascontiguousarray(np.swapaxes(arr(f"L0_ffn_B{n}"), 1, 2))
    a["bias13"] = np.ascontiguousarray(
        np.stack([arr("L0_ffn_b1"), arr("L0_ffn_b3")]).reshape(2, EXPERTS, MC, P).transpose(1, 3, 0, 2))
    a["bias2"] = arr("L0_ffn_b2")
    return a


def kernel(**inputs):
    import concourse.bacc as bacc
    from concourse.bass_utils import run_bass_kernel_spmd

    nc = bacc.Bacc("TRN2", target_bir_lowering=False, num_devices=1)
    arrays = lay_out(inputs)
    ins = {n: nc.dram_tensor(f"in_{n}", a.shape, mybir.dt.from_np(a.dtype), kind="ExternalInput").ap()
           for n, a in arrays.items()}
    shape = tuple(inputs["x"].shape)
    out = nc.dram_tensor("out_y", [TOKENS + TOK, D], F32, kind="ExternalOutput").ap()
    build(nc, ins, out)
    r = run_bass_kernel_spmd(nc, [{f"in_{n}": a for n, a in arrays.items()}], core_ids=[0])
    return r.results[0]["out_y"][:TOKENS].reshape(shape)
```

```python
from contextlib import ExitStack

import concourse.bass as bass
from concourse import mybir

F32 = mybir.dt.float32
BF16 = mybir.dt.bfloat16
U32 = mybir.dt.uint32
I32 = mybir.dt.int32
ALU = mybir.AluOpType
ACT = mybir.ActivationFunctionType
AX_X = mybir.AxisListType.X

P = 128
D = 256
KC = D // P
HEADS = 16
DH = D // HEADS
HID = 512
MC = HID // P
EXPERTS = 8
RANK = 16
EPS = 1e-5
SCALE = DH ** -0.5

TOK = 512
TT = TOK // P
TOKENS = 8192
REGION = TOKENS + TOK
ROW = D + 4
MAX_TILES = 2 * TOKENS // TOK + EXPERTS
UNITS = 6

MAX_ROW = 97
STACK_ROWS = 99

LAG = 8
SPREAD = ((2,), (3,), (4,), (5,), (6,), (7,))
SLOTS = 32
E_RING = 8
STACK_DMAS = 8


def halves_matmul(pe, out, lhs, rhs, first, last):
    lhs_hi, lhs_lo = lhs
    rhs_hi, rhs_lo = rhs
    pe.matmul(out, lhs_hi, rhs_hi, start=first, stop=False)
    pe.matmul(out, lhs_lo, rhs_hi, start=False, stop=False)
    return pe.matmul(out, lhs_hi, rhs_lo, start=False, stop=last)


def split_projections(nc, dram, wq_sb):
    with ExitStack() as ctx:
        proj_in = ctx.enter_context(nc.sbuf_tensor("proj_in", [P, 4, KC * D], F32))
        proj_loaded = [ctx.enter_context(nc.semaphore(f"proj_loaded{n}")) for n in range(4)]
        proj_hi = ctx.enter_context(nc.semaphore("proj_hi"))
        proj_lo = ctx.enter_context(nc.semaphore("proj_lo"))
        block = ctx.enter_context(nc.Block())
        part = lambda n: slice(n * KC * D, (n + 1) * KC * D)

        @block.sync
        def _(sp):
            for n in range(4):
                sp.dma_start(proj_in[:, n, :], dram["w_qkvo"][:, part(n)]).then_inc(proj_loaded[n], 16)
            sp.wait_ge(proj_lo, 4)

        @block.scalar
        def _(act):
            for n in range(4):
                act.wait_ge(proj_loaded[n], 16)
                act.copy(wq_sb["hi"][:, part(n)], proj_in[:, n, :]).then_inc(proj_hi, 1)

        @block.vector
        def _(dve):
            for n in range(4):
                dve.wait_ge(proj_hi, n + 1)
                dve.tensor_tensor(wq_sb["lo"][:, part(n)], proj_in[:, n, :], wq_sb["hi"][:, part(n)],
                                  ALU.subtract).then_inc(proj_lo, 1)


def attention(nc, dram, wq_sb, NB):
    with ExitStack() as ctx:
        sb = lambda n, s, d: ctx.enter_context(nc.sbuf_tensor(n, s, d))
        pb = lambda n, s, d: ctx.enter_context(nc.psum_tensor(n, s, d))
        sem = lambda n: ctx.enter_context(nc.semaphore(n))

        x_in = [sb(f"x_in{k}", [P, TT, D], F32) for k in range(2)]
        x_res = [sb(f"x_res{k}", [P, TT, D], F32) for k in range(2)]
        xn = sb("xn", [P, TT, D], F32)
        stats = sb("stats", [P, TT, 6], F32)
        mean_var = sb("mean_var", [P, TT, 2], F32)
        rstd = sb("rstd", [P, TT], F32)
        xt_hi = sb("xt_hi", [P, KC, TOK], BF16)
        xt_lo = sb("xt_lo", [P, KC, TOK], BF16)
        ctx_in = [sb(f"ctx_in{k}", [P, KC, TOK], F32) for k in range(2)]
        ct_hi = sb("ct_hi", [P, KC, TOK], BF16)
        ct_lo = sb("ct_lo", [P, KC, TOK], BF16)
        qk = sb("qk", [P, KC, 4, TOK], BF16)
        stack = [sb(f"stack{k}", [P, HEADS, 2, TOK], BF16) for k in range(2)]
        vals = [sb(f"vals{k}", [P, TT, HEADS, 32], F32) for k in range(2)]
        expo = sb("expo", [P, E_RING, 2, D], F32)
        maxes = sb("maxes", [P, TT, HEADS], F32)
        negmax = sb("negmax", [HEADS, 2, TOK], BF16)
        sums_t = [sb(f"sums_t{k}", [P, 2, D], F32) for k in range(2)]
        inverse = sb("inverse", [P, 2, 16], F32)
        heads_n = sb("heads_n", [P, TT, HEADS, DH], F32)
        ht_hi = sb("ht_hi", [P, KC, TOK], BF16)
        ht_lo = sb("ht_lo", [P, KC, TOK], BF16)
        bias_o = sb("bias_o", [P, D], F32)
        power = sb("power", [P, TT], F32)
        hold = sb("hold", [P, 1], F32)
        var_eps = sb("var_eps", [P, TT], F32)
        x1 = [sb(f"x1_{k}", [P, TT, D], F32) for k in range(2)]
        bias_qk = sb("bias_qk", [P, 2, KC], F32)
        bias_v = sb("bias_v", [P, D], F32)
        ident = sb("ident", [P, P], F32)
        ones = sb("ones", [P, P], F32)

        st_bank = [pb(f"st_bank{k}", [P, 2, D], F32) for k in range(2)]
        s_bank = [pb(f"s_bank{k}", [P, 2, D], F32) for k in range(2)]
        pv_bank = [pb(f"pv_bank{k}", [P, 2, D], F32) for k in range(2)]
        bank = [pb(f"bank{k}", [P, 512], F32) for k in range(2)]

        loaded = sem("const_loaded")
        stack_const = [sem(f"stack_const{k}") for k in range(2)]
        vals_ones = sem("vals_ones")
        ident_ready = sem("ident_ready")
        x_loaded = [sem(f"x_loaded{k}") for k in range(2)]
        ctx_loaded = [sem(f"ctx_loaded{k}") for k in range(2)]
        res_loaded = [sem(f"res_loaded{k}") for k in range(2)]
        ln_step = sem("ln_step")
        xn_ready = sem("xn_ready")
        ct_hi_ready = sem("ct_hi_ready")
        ct_lo_ready = sem("ct_lo_ready")
        bank_ready = sem("bank_ready")
        bank_free = sem("bank_free")
        hi_ready = sem("hi_ready")
        unstacked = sem("unstacked")
        stacked = sem("stacked")
        st_ready = sem("st_ready")
        exp_done = sem("exp_done")
        s_ready = sem("s_ready")
        max_done = sem("max_done")
        pv_done = sem("pv_done")
        sums_ready = sem("sums_ready")
        inverse_ready = sem("inverse_ready")
        var_ready = sem("var_ready")
        rstd_ready = sem("rstd_ready")
        res_ready = sem("res_ready")
        ht_hi_ready = sem("ht_hi_ready")
        negmax_ready = sem("negmax_ready")
        negmax_stacked = sem("negmax_stacked")
        x1_stored = [sem(f"x1_stored{k}") for k in range(2)]

        FIRST, EACH = 17, 17
        IN_0, IN_1, MAX_0 = 0, 8, 16

        def fills(q):
            if isinstance(q, int) and q == NB - 2:
                s = FIRST + EACH * q
                return dict(start=s, sums=[s, s + 1, s + 2, s + 3], max=s + 4, turn=s + 5, out=s + 7)
            if isinstance(q, int) and q == NB - 1:
                s = FIRST + EACH * (q - 1) + 9
                return dict(start=s, sums=[s, s + 1, s + 2, s + 3], turn=s + 4, out=s + 6)
            s = FIRST + EACH * q
            return dict(start=s, sums=[s, s + 1, s + 2, s + 3], proj=s + 4, max=s + 10, turn=s + 11,
                        v=s + 13, out=s + 15)

        def bank_of(q, k, step, n=None):
            at = fills(q if isinstance(q, int) else k)[step]
            return (at if n is None else at[n]) % 2

        PEELED = 4
        block = ctx.enter_context(nc.Block())

        def steady(engine, first, step, last):
            first()
            with engine.Fori(0, (NB - PEELED) // 2) as i:
                for k in range(2):
                    step(i * 2 + k, k)
            for q in range(NB - PEELED, NB):
                step(q, q % 2)
            last()

        def is_last(q, back):
            return isinstance(q, int) and q >= NB - back

        CONSTANT = ((slice(64, P), 0, 0.0), (slice(64, 96), 1, 0.0), (slice(96, P), 1, 1.0))

        @block.sync
        def _(sp):
            def load(p, k):
                sp.dma_start(x_in[k][:], dram["x"][p]).then_inc(x_loaded[k], 16)
                sp.dma_start(ctx_in[k][:], dram["ctx"][p]).then_inc(ctx_loaded[k], 16)

            def unstack(p, k, proj, side):
                sp.wait_ge(bank_free, proj + (4 if side else 6) + 2)
                for c in range(KC):
                    sp.dma_start(dram["qk"][k, c][:, 2 * side:2 * side + 2],
                                 qk[:, c, 2 * side:2 * side + 2]).then_inc(unstacked, 16)

            def restack(p, k, side):
                sp.wait_ge(unstacked, p * (2 * KC * 16) + (1 if side else 2) * KC * 16)
                for u in range(4):
                    half = (u // 2, u % 2)[side]
                    sp.dma_start(stack[k][DH * u:DH * u + DH, :, side, :],
                                 dram["qk_by_row"][k, 2 * side + half]).then_inc(stacked, 16)

            def stack_inputs(p, k, proj):
                for side in (1, 0):
                    unstack(p, k, proj, side)
                    restack(p, k, side)

            def stack_max(k, fill):
                sp.wait_ge(bank_free, fill + 1 + 2)
                for n in range(2):
                    sp.dma_start(stack[k][MAX_ROW + n:MAX_ROW + n + 1, :, 0, :], negmax[:, n, :])\
                        .then_inc(negmax_stacked, 16)

            for k in range(2):
                sp.sem_inc(x1_stored[k], 16)

            def first():
                load(0, 0)
                sp.dma_start(bias_qk[:], dram["bias_qk"]).then_inc(loaded, 16)
                sp.dma_start(bias_v[:], dram["bias_v"].partition_broadcast(P)).then_inc(loaded, 16)
                sp.dma_start(bias_o[:], dram["bias_o"].partition_broadcast(P)).then_inc(loaded, 16)
                load(1, 1)
                stack_inputs(0, 0, IN_0)
                sp.wait_ge(ct_lo_ready, 1)
                load(2, 0)
                stack_inputs(1, 1, IN_1)
                sp.wait_ge(stack_const[0], 3)
                stack_max(0, MAX_0)
                sp.wait_ge(stack_const[1], 3)

            def step(q, k):
                f = fills(q)
                sp.wait_ge(bank_free, f["start"] + 2)
                sp.dma_start(x_res[k][:], dram["x"][q]).then_inc(res_loaded[k], 16)
                if not is_last(q, 3):
                    load(q + 3, 1 - k)
                if not is_last(q, 2):
                    unstack(q + 2, k, f["proj"], 1)
                    restack(q + 2, k, 1)
                    unstack(q + 2, k, f["proj"], 0)
                if not is_last(q, 1):
                    stack_max(1 - k, f["max"])
                if not is_last(q, 2):
                    restack(q + 2, k, 0)
                sp.wait_ge(bank_free, f["out"] + 2 + 2)
                sp.dma_start(dram["x1"][q], x1[k][:]).then_inc(x1_stored[k], 16)

            def last():
                for k in range(2):
                    sp.wait_ge(x1_stored[k], 16 * (NB // 2 + 1))

            steady(sp, first, step, last)

        @block.gpsimd
        def _(pool):
            pool.memset(ones[:], 1.0).then_inc(ident_ready, 1)
            pool.wait_ge(ident_ready, 1)
            pool.affine_select(out=ident[:], in_=ones[:], compare_op=ALU.is_equal, fill=0.0, base=0,
                               pattern=[[-1, P]], channel_multiplier=1).then_inc(ident_ready, 1)

            pool.memset(power[:], -0.5).then_inc(ident_ready, 1)
            pool.wait_ge(ident_ready, 3)

            def deviations(p):
                pool.wait_ge(var_ready, p + 1)
                pool.tensor_tensor(rstd[:], var_eps[:], power[:], ALU.pow).then_inc(rstd_ready, 1)

            def split_ctx(p, k):
                pool.wait_ge(ct_hi_ready, p + 1)
                pool.tensor_tensor(ct_lo[:], ctx_in[k][:], ct_hi[:], ALU.subtract).then_inc(ct_lo_ready, 1)

            def first():
                deviations(0)
                split_ctx(0, 0)
                for k in range(2):
                    pool.memset(vals[k][:], 1.0).then_inc(vals_ones, 1)
                pool.wait_ge(vals_ones, 2)
                for n, (rows, side, value) in enumerate(CONSTANT):
                    pool.memset(stack[0][rows, :, side, :], value).then_inc(stack_const[0], 1)
                    pool.wait_ge(stack_const[0], n + 1)
                    if n == 0:
                        deviations(1)
                        split_ctx(1, 1)
                        pool.wait_ge(ct_lo_ready, 2)
                pool.wait_ge(loaded, 48)

            def step(q, k):
                if not is_last(q, 2):
                    deviations(q + 2)
                    split_ctx(q + 2, k)
                pool.wait_ge(res_loaded[k], (q - k) * 8 + 16)
                pool.tensor_tensor(x_res[k][:], x_res[k][:], bias_o[:].unsqueeze(1).to_broadcast([P, TT, D]),
                                   ALU.add).then_inc(res_ready, 1)

            steady(pool, first, step, lambda: None)

        @block.tensor
        def _(pe):
            pe.wait_ge(ident_ready, 2)

            def fill(f, b):
                pe.wait_ge(bank_free, f + 1)
                return bank[b % 2]

            def weights(n, c, cols):
                at = (n * KC + c) * D
                return tuple(wq_sb[h][:, at + cols.start:at + cols.stop] for h in ("hi", "lo"))

            def project_qk(p, f, b, between=lambda g: None):
                pe.wait_ge(xn_ready, p + 1)
                for c in range(KC):
                    between(c)
                    out = fill(f + c, b + c)
                    for a in range(TT):
                        ins = pe.transpose(out[:, a * P:(a + 1) * P], xn[:, a, c * P:(c + 1) * P], ident[:])
                    ins.then_inc(bank_ready, 1)
                for j, n in enumerate((1, 0)):
                    between(2 + 2 * j)
                    if n == 0:
                        pe.wait_ge(bank_free, f + 4)
                        src = (xt_hi, xt_lo)
                    else:
                        pe.wait_ge(ct_lo_ready, p + 1)
                        src = (ct_hi, ct_lo)
                    for m in range(KC):
                        g = 2 + 2 * j + m
                        if m:
                            between(g)
                        out = fill(f + g, b + g)
                        for c in range(KC):
                            ins = halves_matmul(pe, out[:], weights(n, c, slice(m * P, m * P + P)),
                                                (src[0][:, c, :], src[1][:, c, :]), c == 0, c == KC - 1)
                        ins.then_inc(bank_ready, 1)

            def project_v(f, b):
                for g in range(2):
                    out = fill(f + g, b + g)
                    for half in range(2):
                        a = 2 * g + half
                        tok = slice(a * P, a * P + P)
                        for c in range(KC):
                            ins = halves_matmul(pe, out[:, half * D:(half + 1) * D],
                                                (ct_hi[:, c, tok], ct_lo[:, c, tok]),
                                                weights(2, c, slice(0, D)), c == 0, c == KC - 1)
                    ins.then_inc(bank_ready, 1)

            def row_scores(p, k, u):
                if u == 0:
                    pe.wait_ge(stacked, (p + 1) * 16 * STACK_DMAS)
                pe.wait_ge(max_done, p * SLOTS + u + 1)
                a, h0 = u // 8, 2 * (u % 8)
                keys = slice((a // 2) * D, (a // 2) * D + D)
                for n in range(2):
                    ins = pe.matmul(s_bank[u % 2][:, n, :],
                                    stack[k][0:MAX_ROW, h0 + n, 0, a * P:(a + 1) * P],
                                    stack[k][0:MAX_ROW, h0 + n, 1, keys], start=True, stop=True)
                ins.then_inc(s_ready, 1)

            def turn_maxima(p, f, b):
                out = fill(f, b)
                pe.wait_ge(max_done, (p + 1) * SLOTS + 2)
                for a in range(TT):
                    ins = pe.transpose(out[0:HEADS, a * P:(a + 1) * P], maxes[:, a, :], ident[:])
                ins.then_inc(bank_ready, 1)

            def slot(u):
                return u // 16, (u // 4) % 4, (u // 2) % 2, u % 2

            def col_scores(q, k, u):
                if u == 0:
                    pe.wait_ge(negmax_stacked, (q + 1) * 32)
                pe.wait_ge(exp_done, q * SLOTS + u + 1)
                j, i, c, hh = slot(u)
                keys = slice(j * D + c * P, j * D + c * P + P)
                for n in range(2):
                    h = 4 * i + 2 * hh + n
                    ins = pe.matmul(st_bank[u % 2][:, n, :], stack[k][0:STACK_ROWS, h, 1, keys],
                                    stack[k][0:STACK_ROWS, h, 0, j * D:(j + 1) * D], start=True, stop=True)
                ins.then_inc(st_ready, 1)

            def values(q, k, v):
                u = 2 * v
                j, i, c, _ = slot(u)
                pe.wait_ge(exp_done, q * SLOTS + u + 4)
                g2 = 2 * j + i // 2
                if v == 0:
                    pe.wait_ge(bank_free, fills(q)["start"])
                if i % 2 == 0 and c == 0:
                    pe.wait_ge(sums_ready, 4 * q + g2 + 1)
                for g in range(4):
                    s = (u + g // 2) % E_RING
                    ins = pe.matmul(pv_bank[g2 % 2][32 * g:32 * g + 32, i % 2, :],
                                    vals[k][:, 2 * j + c, 4 * i + g, :], expo[:, s, g % 2, :],
                                    start=(c == 0), stop=(c == 1), tile_position=(0, 32 * g))
                ins.then_inc(pv_done, 1)

            def turn_sums(q, k, n):
                out = fill(fills(q)["sums"][n], bank_of(q, k, "sums", n))
                pe.wait_ge(sums_ready, 4 * q + n + 1 + 2)
                for half in range(2):
                    for i in range(2):
                        at = (2 * half + i) * P
                        ins = pe.transpose(out[:, at:at + P], sums_t[n % 2][:, i, half * P:(half + 1) * P],
                                           ident[:])
                ins.then_inc(bank_ready, 1)

            def turn_heads(q, k):
                f, b = fills(q)["turn"], bank_of(q, k, "turn")
                pe.wait_ge(bank_free, fills(q)["sums"][3] + 1 + 2)
                for c in range(KC):
                    out = fill(f + c, b + c)
                    for a in range(TT):
                        ins = pe.transpose(out[:, a * P:(a + 1) * P],
                                           heads_n[:, a, c * 8:(c + 1) * 8, :].rearrange("p h d -> p (h d)"),
                                           ident[:])
                    ins.then_inc(bank_ready, 1)

            def output(q, k):
                f, b = fills(q)["out"], bank_of(q, k, "out")
                pe.wait_ge(bank_free, fills(q)["turn"] + 2 + 2)
                for g in range(2):
                    out = fill(f + g, b + g)
                    for half in range(2):
                        tok = slice((2 * g + half) * P, (2 * g + half + 1) * P)
                        for c in range(KC):
                            ins = halves_matmul(pe, out[:, half * D:(half + 1) * D],
                                                (ht_hi[:, c, tok], ht_lo[:, c, tok]),
                                                weights(3, c, slice(0, D)), c == 0, c == KC - 1)
                    ins.then_inc(bank_ready, 1)

            def first():
                project_qk(0, IN_0, IN_0)
                project_v(IN_0 + 6, IN_0 + 6)
                project_qk(1, IN_1, IN_1)
                project_v(IN_1 + 6, IN_1 + 6)
                pe.wait_ge(stack_const[0], 3)
                for u in range(SLOTS):
                    row_scores(0, 0, u)
                turn_maxima(0, MAX_0, MAX_0)
                pe.wait_ge(stack_const[1], 3)

            def step(q, k):
                f = fills(q)
                for u in range(SLOTS):
                    col_scores(q, k, u)
                    if u >= LAG and not is_last(q, 1):
                        row_scores(q + 1, 1 - k, u - LAG)
                    if u % 2 == 1 and u > 1:
                        values(q, k, u // 2 - 1)
                    if u % 8 == 6 and u > 8:
                        turn_sums(q, k, u // 8 - 1)
                values(q, k, SLOTS // 2 - 1)

                def trailing(n):
                    if not is_last(q, 1):
                        row_scores(q + 1, 1 - k, SLOTS - LAG + n)
                    if n == 1:
                        turn_sums(q, k, 3)

                for n in range(SPREAD[0][0]):
                    trailing(n)
                if not is_last(q, 2):
                    project_qk(q + 2, f["proj"], bank_of(q, k, "proj"), lambda g: [trailing(n) for n in SPREAD[g]])
                else:
                    for n in range(SPREAD[0][0], LAG):
                        trailing(n)
                if not is_last(q, 1):
                    turn_maxima(q + 1, f["max"], bank_of(q, k, "max"))
                turn_heads(q, k)
                if not is_last(q, 2):
                    project_v(f["v"], bank_of(q, k, "v"))
                output(q, k)

            steady(pe, first, step, lambda: None)

        @block.scalar
        def _(act):
            act.sem_inc(exp_done, 2)
            act.sem_inc(sums_ready, 2)

            act.wait_ge(loaded, 48)

            def inputs(p, f, b):
                for c in range(KC):
                    act.wait_ge(bank_ready, f + c + 1)
                    act.copy(xt_hi[:, c, :], bank[(b + c) % 2][:]).then_inc(hi_ready, 1)
                for j, n in enumerate((1, 0)):
                    for m in range(KC):
                        g = 2 + 2 * j + m
                        if g == 2 and not (isinstance(p, int) and p == 0):
                            act.wait_ge(unstacked, p * (2 * KC * 16))
                        act.wait_ge(bank_ready, f + g + 1)
                        act.activation(qk[:, m, 2 * n, :], bank[(b + g) % 2][:], ACT.Identity,
                                       bias=bias_qk[:, n, m:m + 1]).then_inc(hi_ready, 1)

            def maxima(p, f, b):
                act.wait_ge(bank_ready, f + 1)
                if not (isinstance(p, int) and p == 0):
                    act.wait_ge(negmax_stacked, p * 32)
                act.mul(negmax[:, 0, :], bank[b % 2][0:HEADS, :], -1.0).then_inc(negmax_ready, 1)

            def exponentials(q, k, u):
                act.wait_ge(st_ready, q * SLOTS + u + 1)
                act.wait_ge(pv_done, q * (SLOTS // 2) + u // 2 + 1)
                act.activation(expo[:, u % E_RING, :, :], st_bank[u % 2][:], ACT.Exp,
                               scale=SCALE).then_inc(exp_done, 1)

            def copy_sums(q, n):
                act.wait_ge(pv_done, q * (SLOTS // 2) + 4 * (n + 1) + E_RING // 2)
                act.wait_ge(bank_ready, fills(q)["sums"][n - 2] + 1 if n > 1 else fills(q)["start"])
                act.copy(sums_t[n % 2][:], pv_bank[n % 2][:]).then_inc(sums_ready, 1)

            def heads_hi(q, k):
                f, b = fills(q)["turn"], bank_of(q, k, "turn")
                for c in range(KC):
                    act.wait_ge(bank_ready, f + c + 1)
                    act.copy(ht_hi[:, c, :], bank[(b + c) % 2][:]).then_inc(ht_hi_ready, 1)

            def first():
                inputs(0, IN_0, IN_0)
                inputs(1, IN_1, IN_1)
                act.wait_ge(ident_ready, 1)
                for rows, side, value in CONSTANT:
                    shape = [rows.stop - rows.start, HEADS, TOK]
                    act.mul(stack[1][rows, :, side, :], ones[rows, 0:1].unsqueeze(2).to_broadcast(shape), value)\
                        .then_inc(stack_const[1], 1)
                maxima(0, MAX_0, MAX_0)

            def step(q, k):
                f = fills(q)
                for u in range(SLOTS):
                    exponentials(q, k, u)
                    if u % 8 == 3 and u > 8:
                        copy_sums(q, u // 8 - 1)
                copy_sums(q, 3)
                if not is_last(q, 2):
                    inputs(q + 2, f["proj"], bank_of(q, k, "proj"))
                if not is_last(q, 1):
                    maxima(q + 1, f["max"], bank_of(q, k, "max"))
                heads_hi(q, k)

            steady(act, first, step, lambda: None)

        @block.vector
        def _(dve):
            dve.sem_inc(bank_free, 2)
            dve.sem_inc(max_done, 2)
            dve.sem_inc(pv_done, E_RING // 2)

            def normalize(p, k, reads):
                dve.wait_ge(x_loaded[k], (p - k) * 8 + 16)
                for a in range(TT):
                    ins = dve.bn_stats(stats[:, a, :], x_in[k][:, a, :])
                ins.then_inc(ln_step, 1)
                dve.wait_ge(ln_step, 2 * p + 1)
                dve.memset(hold[:], 0.0)
                for a in range(TT):
                    ins = dve.bn_aggr(mean_var[:, a, :], stats[:, a, :])
                ins.then_inc(ln_step, 1)
                dve.wait_ge(ln_step, 2 * p + 2)
                dve.tensor_scalar(var_eps[:], mean_var[:, :, 1], EPS, None, ALU.add).then_inc(var_ready, 1)
                dve.wait_ge(rstd_ready, p + 1)
                if reads is not None:
                    dve.wait_ge(bank_ready, reads)
                for a in range(TT):
                    ins = dve.tensor_scalar(xn[:, a, :], x_in[k][:, a, :], mean_var[:, a, 0:1],
                                            rstd[:, a:a + 1], ALU.subtract, ALU.mult)
                ins.then_inc(xn_ready, 1)

            def split_ctx(p, k, reads):
                dve.wait_ge(ctx_loaded[k], (p - k) * 8 + 16)
                if reads is not None:
                    dve.wait_ge(bank_ready, reads)
                    dve.wait_ge(ct_lo_ready, p)
                dve.tensor_copy(ct_hi[:], ctx_in[k][:]).then_inc(ct_hi_ready, 1)

            def split_qk(p, f, b, between=lambda g: None):
                for c in range(KC):
                    between(c)
                    dve.wait_ge(hi_ready, 6 * p + c + 1)
                    dve.tensor_tensor(xt_lo[:, c, :], bank[(b + c) % 2][:], xt_hi[:, c, :],
                                      ALU.subtract).then_inc(bank_free, 1)
                for j, n in enumerate((1, 0)):
                    for m in range(KC):
                        g = 2 + 2 * j + m
                        between(g)
                        dve.wait_ge(hi_ready, 6 * p + g + 1)
                        dve.scalar_tensor_tensor(out=qk[:, m, 2 * n + 1, :], in0=bank[(b + g) % 2][:],
                                                 scalar=bias_qk[:, n, m:m + 1], in1=qk[:, m, 2 * n, :],
                                                 op0=ALU.add, op1=ALU.subtract).then_inc(bank_free, 1)

            def keep_v(k, f, b):
                for g in range(2):
                    dve.wait_ge(bank_ready, f + 1 + g)
                    for half in range(2):
                        ins = dve.tensor_tensor(
                            vals[k][:, 2 * g + half, :, 0:DH],
                            bank[(b + g) % 2][:, half * D:(half + 1) * D].rearrange("p (h d) -> p h d", d=DH),
                            bias_v[:].rearrange("p (h d) -> p h d", d=DH), ALU.add)
                    ins.then_inc(bank_free, 1)

            def row_max(p, u, reads=None):
                dve.wait_ge(s_ready, p * SLOTS + u + 1)
                if u == 0 and reads is not None:
                    dve.wait_ge(bank_ready, reads)
                a, h0 = u // 8, 2 * (u % 8)
                dve.tensor_reduce(maxes[:, a, h0:h0 + 2], s_bank[u % 2][:], AX_X, ALU.max)\
                    .then_inc(max_done, 1)

            def maxima(p, f, b):
                dve.wait_ge(negmax_ready, p + 1)
                dve.scalar_tensor_tensor(out=negmax[:, 1, :], in0=bank[b % 2][0:HEADS, :], scalar=-1.0,
                                         in1=negmax[:, 0, :], op0=ALU.mult, op1=ALU.subtract)\
                    .then_inc(bank_free, 1)

            def divide(q, k, n):
                f, b = fills(q)["sums"][n], bank_of(q, k, "sums", n)
                dve.wait_ge(bank_ready, f + 1)
                dve.reciprocal(inverse[:, n % 2], bank[b][:, DH::32]).then_inc(inverse_ready, 1)
                dve.wait_ge(inverse_ready, 4 * q + n + 1)
                j, h = n // 2, 8 * (n % 2)
                dve.tensor_tensor(heads_n[:, 2 * j:2 * j + 2, h:h + 8, :],
                                  bank[b][:].rearrange("p (a h d) -> p a h d", a=2, d=32)[:, :, :, 0:DH],
                                  inverse[:, n % 2].rearrange("p (a h) -> p a h", a=2).unsqueeze(3)
                                  .to_broadcast([P, 2, 8, DH]), ALU.mult).then_inc(bank_free, 1)

            def heads_lo(q, k):
                b = bank_of(q, k, "turn")
                for c in range(KC):
                    dve.wait_ge(ht_hi_ready, KC * q + c + 1)
                    dve.tensor_tensor(ht_lo[:, c, :], bank[(b + c) % 2][:], ht_hi[:, c, :],
                                      ALU.subtract).then_inc(bank_free, 1)

            def output(q, k):
                f, b = fills(q)["out"], bank_of(q, k, "out")
                dve.wait_ge(res_ready, q + 1)
                dve.wait_ge(x1_stored[k], (q - k) * 8 + 16)
                for g in range(2):
                    dve.wait_ge(bank_ready, f + g + 1)
                    dve.tensor_tensor(x1[k][:, 2 * g:2 * g + 2, :],
                                      bank[(b + g) % 2][:].rearrange("p (a d) -> p a d", d=D),
                                      x_res[k][:, 2 * g:2 * g + 2, :], ALU.add).then_inc(bank_free, 1)

            def first():
                normalize(0, 0, None)
                split_ctx(0, 0, None)
                dve.wait_ge(loaded, 48)
                split_qk(0, IN_0, IN_0)
                dve.wait_ge(vals_ones, 2)
                keep_v(0, IN_0 + 6, IN_0 + 6)
                normalize(1, 1, IN_0 + 2)
                split_ctx(1, 1, IN_0 + 8)
                split_qk(1, IN_1, IN_1)
                keep_v(1, IN_1 + 6, IN_1 + 6)
                for u in range(SLOTS):
                    row_max(0, u)
                maxima(0, MAX_0, MAX_0)

            def step(q, k):
                f = fills(q)
                for u in range(SLOTS):
                    if u >= LAG and not is_last(q, 1):
                        row_max(q + 1, u - LAG, f["start"])
                    if u == 0 and not is_last(q, 2):
                        normalize(q + 2, k, f["start"])
                        split_ctx(q + 2, k, f["start"])
                    if u % 8 == 7 and u > 8:
                        divide(q, k, u // 8 - 1)

                def trailing(n):
                    if not is_last(q, 1):
                        row_max(q + 1, SLOTS - LAG + n)
                    if n == 1:
                        divide(q, k, 3)

                for n in range(SPREAD[0][0]):
                    trailing(n)
                if not is_last(q, 2):
                    split_qk(q + 2, f["proj"], bank_of(q, k, "proj"), lambda g: [trailing(n) for n in SPREAD[g]])
                else:
                    for n in range(SPREAD[0][0], LAG):
                        trailing(n)
                if not is_last(q, 1):
                    maxima(q + 1, f["max"], bank_of(q, k, "max"))
                heads_lo(q, k)
                if not is_last(q, 2):
                    keep_v(k, f["v"], bank_of(q, k, "v"))
                output(q, k)

            steady(dve, first, step, lambda: None)


HALF = UNITS // 2
LORA = (2 * HALF + 5) * P


def lora_products(k):
    def cols(at, n):
        return slice(at, at + n)

    if k == 0:
        return [[(cols(0, P), cols(3 * P, HID), cols(0, HID))],
                [(cols(P, P), cols(3 * P, HID), cols(0, HID))],
                [(cols(2 * P, P), cols(3 * P + HID, HID), cols(0, HID))]]
    second = 5 * P + HID
    return [[(cols(0, P), cols(5 * P, HID), cols(0, HID))]] + [
        [(cols((1 + 2 * u + h) * P, P), cols(second, D), cols(h * D, D)) for h in range(2)] for u in range(2)]


def route(nc, dram, tables, NB):
    with ExitStack() as ctx:
        sb = lambda n, s, d: ctx.enter_context(nc.sbuf_tensor(n, s, d))
        pb = lambda n, s, d: ctx.enter_context(nc.psum_tensor(n, s, d))
        sem = lambda n: ctx.enter_context(nc.semaphore(n))

        gate_w = sb("gate_w", [P, KC, EXPERTS], F32)
        gate_hi = sb("gate_hi", [P, KC, EXPERTS], BF16)
        gate_lo = sb("gate_lo", [P, KC, EXPERTS], BF16)
        x1 = [sb(f"r_x1_{k}", [P, TT, D], F32) for k in range(2)]
        row = [sb(f"row{k}", [P, TT, ROW], F32) for k in range(2)]
        stats = sb("r_stats", [P, TT, 6], F32)
        mean_var = sb("r_mean_var", [P, TT, 2], F32)
        var_eps = sb("r_var_eps", [P, TT], F32)
        rstd = sb("r_rstd", [P, TT], F32)
        power = sb("r_power", [P, TT], F32)
        hold = sb("r_hold", [P, 1], F32)
        hold_pool = sb("r_hold_pool", [P, 4], F32)
        xt_hi = sb("r_xt_hi", [P, KC, TOK], BF16)
        xt_lo = sb("r_xt_lo", [P, KC, TOK], BF16)
        logits = sb("logits", [P, TT, EXPERTS], F32)
        score_max = sb("score_max", [P, TT], F32)
        scores = sb("scores", [P, TT, EXPERTS], F32)
        top = sb("top", [P, TT, 8], F32)
        top_at = sb("top_at", [P, TT, 8], U32)
        top_f = sb("top_f", [P, TT, 2], F32)
        top_sum = sb("top_sum", [P, TT], F32)
        top_inv = sb("top_inv", [P, TT], F32)
        weight = sb("weight", [P, TT, 2], F32)
        token = sb("token", [P, TT], F32)
        picks = sb("picks", [P, TT, 2, EXPERTS], F32)
        mask = sb("mask", [P, TT, EXPERTS], BF16)
        place = sb("place", [P, TT, EXPERTS], F32)
        taken = sb("taken", [P, EXPERTS + 1], F32)
        picked = sb("picked", [P, TT, 2, EXPERTS], F32)
        slot_f = sb("slot_f", [P, TT, 2], F32)
        slot = [sb(f"slot{k}", [P, TT * 2], U32) for k in range(2)]
        number = sb("number", [P, EXPERTS + 1], F32)
        base = sb("base", [P, EXPERTS + 1], F32)
        ident = sb("r_ident", [P, P], F32)
        ones = sb("r_ones", [P, P], F32)
        ones_b = sb("ones_b", [P, P], BF16)
        before = sb("before", [P, P], BF16)
        padding = tables["padding"]
        PARTS = TOKENS // TOK
        steps = sb("tile_steps", [P, EXPERTS, PARTS - 1], F32)
        over = sb("over", [P, EXPERTS, PARTS - 1], F32)
        count = sb("count", [P, EXPERTS], F32)
        tiles = sb("tiles", [P, EXPERTS], F32)
        earlier = sb("earlier", [P, EXPERTS + 1, EXPERTS], F32)
        start_f = sb("start_f", [P, EXPERTS + 1], F32)
        skip = sb("skip", [P, EXPERTS], F32)
        tile_number = sb("tile_number", [P, MAX_TILES + 1], F32)
        begun = sb("begun", [P, MAX_TILES + 1, EXPERTS], F32)
        tile_row = sb("tile_row_f", [P, MAX_TILES + 1], F32)

        w_in = [sb(f"w_in{k}", [P, HALF, 512], F32) for k in range(2)]
        lora_in = [sb(f"lora_in{k}", [P, LORA], F32) for k in range(2)]
        w_sum = sb("w_sum", [P, HALF, 512], F32)
        w_out = [sb(f"w_out{k}", [P, 2, HALF, 512], BF16) for k in range(2)]

        low_bank = [pb(f"low_bank{u}", [P, 512], F32) for u in range(HALF)]
        x_bank = [pb(f"x_bank{c}", [P, TOK], F32) for c in range(KC)]
        gate_bank = pb("gate_bank", [P, 512], F32)
        rank_bank = pb("rank_bank", [P, 512], F32)

        const_loaded = sem("r_const_loaded")
        const = sem("r_const")
        x1_loaded = [sem(f"r_x1_loaded{k}") for k in range(2)]
        step_done = sem("r_step")
        var_ready = sem("r_var_ready")
        rstd_ready = sem("r_rstd_ready")
        xn_ready = sem("r_xn_ready")
        xt_ready = sem("r_xt_ready")
        xt_hi_ready = sem("r_xt_hi_ready")
        xt_lo_ready = sem("r_xt_lo_ready")
        logits_ready = sem("logits_ready")
        gate_step = sem("gate_step")
        exp_ready = sem("r_exp_ready")
        rank_ready = sem("rank_ready")
        slots_ready = sem("slots_ready")
        row_free = sem("row_free")
        scattered = [sem(f"scattered{k}") for k in range(2)]
        zeroed = sem("zeroed")
        w_loaded = [sem(f"prep_loaded{k}") for k in range(2)]
        low_ready = sem("low_ready")
        sum_ready = sem("sum_ready")
        w_hi_ready = sem("w_hi_ready")
        w_lo_ready = sem("w_lo_ready")
        w_stored = [sem(f"w_stored{k}") for k in range(2)]
        cleared = sem("r_cleared")
        table_step = sem("table_step")
        table_ready = sem("table_ready")
        STEPS = 13
        CONST = 11

        block = ctx.enter_context(nc.Block())

        def steady(step):
            def run(engine):
                step(0, 0, 0)
                with engine.Fori(0, (NB - 2) // 2) as j:
                    step(j * 2 + 1, j, 1)
                    step(j * 2 + 2, j + 1, 0)
                step(NB - 1, NB // 2 - 1, 1)
            return run

        def has(b, ahead):
            return not isinstance(b, int) or b + ahead < NB

        @block.sync
        def _(sp):
            sp.dma_start(gate_w[:], dram["wg"]).then_inc(const_loaded, 16)

            def load(b, i, k):
                sp.wait_ge(xn_ready, b + 1)
                sp.dma_start(x1[k][:], dram["x1"][b]).then_inc(x1_loaded[k], 16)

            def step(b, i, k):
                if has(b, 1):
                    load(b + 1, i + k, 1 - k)
                sp.wait_ge(w_lo_ready, b * HALF + HALF)
                sp.dma_start(w_in[k][:], dram["w_units"][i][:, HALF * k:HALF * k + HALF, :])\
                    .then_inc(w_loaded[k], 16)
                sp.dma_start(lora_in[k][0:RANK, :], dram["lora"][i, k]).then_inc(w_loaded[k], 16)

            load(0, 0, 0)
            sp.wait_ge(zeroed, 1)
            steady(step)(sp)
            sp.wait_ge(const, CONST)
            sp.dma_start(dram["y"][TOKENS:TOKENS + TOK].rearrange("(a p) d -> p a d", p=P),
                         padding[:, :, 0:D]).then_inc(cleared, 16)
            for k in range(2):
                sp.wait_ge(scattered[k], 16 * 2 * TT * (NB // 2))
            sp.wait_ge(cleared, 16)

        @block.gpsimd
        def _(pool):
            for k in range(2):
                ins = pool.memset(lora_in[k][:], 0.0)
            ins.then_inc(zeroed, 1)
            pool.memset(ones[:], 1.0).then_inc(const, 1)
            pool.memset(ones_b[:], 1.0).then_inc(const, 1)
            pool.memset(padding[:], 0.0).then_inc(const, 1)
            pool.wait_ge(const, 3)
            pool.affine_select(out=ident[:], in_=ones[:], compare_op=ALU.is_equal, fill=0.0, base=0,
                               pattern=[[-1, P]], channel_multiplier=1).then_inc(const, 1)
            pool.affine_select(out=before[:], in_=ones_b[:], compare_op=ALU.is_gt, fill=0.0, base=0,
                               pattern=[[1, P]], channel_multiplier=-1).then_inc(const, 1)
            pool.iota(number[:], pattern=[[1, EXPERTS + 1]], base=0, channel_multiplier=0,
                      allow_small_or_imprecise_dtypes=True).then_inc(const, 1)
            pool.iota(base[:], pattern=[[REGION, EXPERTS + 1]], base=0, channel_multiplier=0,
                      allow_small_or_imprecise_dtypes=True)
            pool.iota(token[:], pattern=[[P, TT]], base=0, channel_multiplier=1,
                      allow_small_or_imprecise_dtypes=True)
            pool.iota(tile_number[:], pattern=[[1, MAX_TILES + 1]], base=0, channel_multiplier=0,
                      allow_small_or_imprecise_dtypes=True)
            pool.iota(steps[:], pattern=[[0, EXPERTS], [TOK, PARTS - 1]], base=TOK, channel_multiplier=0,
                      allow_small_or_imprecise_dtypes=True)
            pool.iota(padding[:, :, ROW - 1], pattern=[[P, TT]], base=TOKENS, channel_multiplier=1,
                      allow_small_or_imprecise_dtypes=True).then_inc(const, 1)
            pool.wait_ge(const, 7)
            pool.tensor_copy(taken[:], base[:]).then_inc(const, 1)
            pool.wait_ge(const_loaded, 16)
            pool.tensor_copy(gate_hi[:], gate_w[:]).then_inc(const, 1)
            pool.wait_ge(const, 9)
            pool.tensor_tensor(gate_lo[:], gate_w[:], gate_hi[:], ALU.subtract).then_inc(const, 1)
            pool.memset(power[:], -0.5).then_inc(const, 1)
            pool.wait_ge(const, CONST)

            def invert(b):
                pool.wait_ge(var_ready, b + 1)
                pool.tensor_tensor(rstd[:], var_eps[:], power[:], ALU.pow).then_inc(rstd_ready, 1)

            def step(b, i, k):
                if has(b, 1):
                    invert(b + 1)
                pool.wait_ge(slots_ready, b + 1)
                pool.tensor_tensor(hold_pool[:, k:k + 1], ones[:, 0:1], ones[:, 0:1], ALU.subtract)
                for a in range(TT):
                    for n in range(2):
                        if a == 0 and n == 1 and not (isinstance(b, int) and b == 0):
                            pool.wait_ge(scattered[1 - k], (i + k) * (2 * TT * 16))
                            pool.tensor_tensor(hold_pool[:, 2 + k:3 + k], ones[:, 0:1], ones[:, 0:1],
                                               ALU.subtract).then_inc(row_free, 1)
                        pool.indirect_dma_start(
                            out=dram["rows"],
                            out_offset=bass.IndirectOffsetOnAxis(ap=slot[k][:, 2 * a + n:2 * a + n + 1], axis=0),
                            in_=row[k][:, a, :], in_offset=None).then_inc(scattered[k], 16)

            invert(0)
            steady(step)(pool)

        @block.tensor
        def _(pe):
            pe.wait_ge(const, CONST)

            def turn(b, k):
                pe.wait_ge(xn_ready, b + 3)
                for c in range(KC):
                    for a in range(TT):
                        ins = pe.transpose(x_bank[c][:, a * P:(a + 1) * P],
                                           row[k][:, a, c * P:(c + 1) * P], ident[:])
                    ins.then_inc(xt_ready, 1)

            def gate(b):
                pe.wait_ge(xt_lo_ready, b * KC + KC)
                for a in range(TT):
                    for c in range(KC):
                        lhs = [x[:, c, a * P:(a + 1) * P] for x in (xt_hi, xt_lo)]
                        ins = halves_matmul(pe, gate_bank[:, a * EXPERTS:(a + 1) * EXPERTS], lhs,
                                            (gate_hi[:, c, :], gate_lo[:, c, :]), c == 0, c == KC - 1)
                ins.then_inc(logits_ready, 1)

            def rank(b):
                pe.wait_ge(gate_step, b * STEPS + 7)
                for a in range(TT + 1):
                    for c in range(min(a + 1, TT)):
                        ins = pe.matmul(rank_bank[:, a * EXPERTS:(a + 1) * EXPERTS],
                                        before[:] if c == a else ones_b[:], mask[:, c, :],
                                        start=c == 0, stop=c == min(a, TT - 1))
                ins.then_inc(rank_ready, 1)

            def updates(b, i, k):
                pe.wait_ge(w_loaded[k], i * 32 + 32)
                for u in range(HALF):
                    pe.wait_ge(sum_ready, b * HALF + u + 1)
                    for lhs, rhs, out in lora_products(k)[u]:
                        ins = pe.matmul(low_bank[u][:, out], lora_in[k][:, lhs], lora_in[k][:, rhs],
                                        start=True, stop=True)
                    ins.then_inc(low_ready, 1)

            def step(b, i, k):
                rank(b)
                if has(b, 1):
                    turn(b + 1, 1 - k)
                    gate(b + 1)
                    updates(b + 1, i + k, 1 - k)

            turn(0, 0)
            gate(0)
            updates(0, 0, 0)
            steady(step)(pe)

        @block.scalar
        def _(act):
            def high(b):
                for c in range(KC):
                    act.wait_ge(xt_ready, b * KC + c + 1)
                    act.copy(xt_hi[:, c, :], x_bank[c][:]).then_inc(xt_hi_ready, 1)

            def exponentials(b):
                act.wait_ge(gate_step, b * STEPS + 2)
                act.activation(scores[:], logits[:], ACT.Exp).then_inc(exp_ready, 1)

            def step(b, i, k):
                act.wait_ge(w_stored[k], i * 16 + 16)
                for u in range(HALF):
                    if u == HALF - 1 and has(b, 1):
                        high(b + 1)
                    act.wait_ge(sum_ready, b * HALF + HALF + u + 1)
                    act.copy(w_out[k][:, 0, u, :], w_sum[:, u, :]).then_inc(w_hi_ready, 1)
                if has(b, 1):
                    exponentials(b + 1)
                act.wait_ge(w_lo_ready, b * HALF + 3 * HALF)
                act.dma_start(dram["experts"][i][:, :, HALF * k:HALF * k + HALF, :], w_out[k][:])\
                    .then_inc(w_stored[k], 16)

            for k in range(2):
                act.sem_inc(w_stored[k], 16)
            high(0)
            exponentials(0)
            steady(step)(act)
            for k in range(2):
                act.wait_ge(w_stored[k], 16 * (NB // 2 + 1))

        @block.vector
        def _(dve):
            dve.sem_inc(xn_ready, 2)
            dve.sem_inc(row_free, 2)
            dve.sem_inc(sum_ready, HALF)
            dve.sem_inc(w_lo_ready, 2 * HALF)
            dve.wait_ge(const, CONST)

            def moments(b, i, k):
                dve.wait_ge(x1_loaded[k], i * 16 + 16)
                for a in range(TT):
                    ins = dve.bn_stats(stats[:, a, :], x1[k][:, a, :])
                ins.then_inc(step_done, 1)
                dve.wait_ge(step_done, b * 2 + 1)
                dve.memset(hold[:], 0.0)
                for a in range(TT):
                    ins = dve.bn_aggr(mean_var[:, a, :], stats[:, a, :])
                ins.then_inc(step_done, 1)
                dve.wait_ge(step_done, b * 2 + 2)
                dve.tensor_scalar(var_eps[:], mean_var[:, :, 1], EPS, None, ALU.add).then_inc(var_ready, 1)

            def norm(b, k):
                dve.wait_ge(rstd_ready, b + 1)
                dve.wait_ge(row_free, b + 1)
                for a in range(TT):
                    ins = dve.tensor_scalar(row[k][:, a, 0:D], x1[k][:, a, :], mean_var[:, a, 0:1],
                                            rstd[:, a:a + 1], ALU.subtract, ALU.mult)
                ins.then_inc(xn_ready, 1)

            def low(b):
                for c in range(KC):
                    dve.wait_ge(xt_hi_ready, b * KC + c + 1)
                    dve.tensor_tensor(xt_lo[:, c, :], x_bank[c][:], xt_hi[:, c, :], ALU.subtract)\
                        .then_inc(xt_lo_ready, 1)

            def done(ins, b, n):
                ins.then_inc(gate_step, 1)
                dve.wait_ge(gate_step, b * STEPS + n)

            def by_expert(x):
                return x.rearrange("p (a e) -> p a e", e=EXPERTS)

            def shift(b):
                dve.wait_ge(logits_ready, b + 1)
                done(dve.tensor_reduce(score_max[:], by_expert(gate_bank[:, 0:TT * EXPERTS]), AX_X, ALU.max), b, 1)
                done(dve.tensor_tensor(logits[:], by_expert(gate_bank[:, 0:TT * EXPERTS]),
                                       score_max[:].unsqueeze(2).to_broadcast([P, TT, EXPERTS]), ALU.subtract), b, 2)

            def pick(b, k):
                dve.wait_ge(exp_ready, b + 1)
                dve.memset(hold[:], 0.0)
                for a in range(TT):
                    ins = dve.max(top[:, a, :], scores[:, a, :])
                done(ins, b, 3)
                dve.memset(hold[:], 0.0)
                for a in range(TT):
                    ins = dve.max_index(top_at[:, a, :], top[:, a, :], scores[:, a, :])
                done(ins, b, 4)
                dve.tensor_copy(top_f[:], top_at[:, :, 0:2])
                done(dve.tensor_tensor(top_sum[:], top[:, :, 0], top[:, :, 1], ALU.add), b, 5)
                shape = [P, TT, 2, EXPERTS]
                dve.tensor_tensor(picks[:], number[:, 0:EXPERTS].unsqueeze(1).unsqueeze(1).to_broadcast(shape),
                                  top_f[:].unsqueeze(3).to_broadcast(shape), ALU.is_equal)
                done(dve.reciprocal(top_inv[:], top_sum[:]), b, 6)
                done(dve.tensor_tensor(mask[:], picks[:, :, 0, :], picks[:, :, 1, :], ALU.add), b, 7)
                done(dve.tensor_tensor(weight[:], top[:, :, 0:2],
                                       top_inv[:].unsqueeze(2).to_broadcast([P, TT, 2]), ALU.mult), b, 8)
                dve.tensor_copy(row[k][:, :, D], weight[:, :, 1])
                dve.tensor_tensor(row[k][:, :, D + 1], weight[:, :, 0], weight[:, :, 1], ALU.subtract)
                dve.tensor_copy(row[k][:, :, D + 2], top_f[:, :, 0])
                done(dve.tensor_copy(row[k][:, :, D + 3], token[:]), b, 9)
                dve.tensor_scalar(token[:], token[:], float(TOK), None, ALU.add)

            def assign(b, k):
                dve.wait_ge(rank_ready, b + 1)
                done(dve.tensor_tensor(place[:], by_expert(rank_bank[:, 0:TT * EXPERTS]),
                                       taken[:, 0:EXPERTS].unsqueeze(1).to_broadcast([P, TT, EXPERTS]), ALU.add), b, 10)
                dve.tensor_tensor(taken[:, 0:EXPERTS], rank_bank[:, TT * EXPERTS:(TT + 1) * EXPERTS],
                                  taken[:, 0:EXPERTS], ALU.add)
                done(dve.tensor_tensor(picked[:], picks[:], place[:].unsqueeze(2).to_broadcast(
                    [P, TT, 2, EXPERTS]), ALU.mult), b, 11)
                done(dve.tensor_reduce(slot_f[:], picked[:], AX_X, ALU.add), b, 12)
                done(dve.tensor_copy(slot[k][:], slot_f[:].rearrange("p a n -> p (a n)")), b, 13)
                dve.sem_inc(slots_ready, 1)

            def add(b, k, u):
                dve.wait_ge(low_ready, b * HALF + u + 1)
                dve.tensor_tensor(w_sum[:, u, :], low_bank[u][:], w_in[k][:, u, :], ALU.add)\
                    .then_inc(sum_ready, 1)

            def step(b, i, k):
                if has(b, 1):
                    moments(b + 1, i + k, 1 - k)
                pick(b, k)
                add(b, k, 0)
                assign(b, k)
                for u in range(1, HALF):
                    add(b, k, u)
                if has(b, 1):
                    norm(b + 1, 1 - k)
                for u in range(HALF):
                    if u == HALF - 1 and has(b, 1):
                        low(b + 1)
                    dve.wait_ge(w_hi_ready, b * HALF + u + 1)
                    dve.tensor_tensor(w_out[k][:, 1, u, :], w_sum[:, u, :], w_out[k][:, 0, u, :],
                                      ALU.subtract).then_inc(w_lo_ready, 1)
                if has(b, 1):
                    shift(b + 1)

            moments(0, 0, 0)
            norm(0, 0)
            low(0)
            shift(0)
            steady(step)(dve)

            def table(ins, n):
                ins.then_inc(table_step, 1)
                dve.wait_ge(table_step, n)

            table(dve.tensor_tensor(count[:], taken[:, 0:EXPERTS], base[:, 0:EXPERTS], ALU.subtract), 1)
            table(dve.tensor_tensor(over[:], count[:].unsqueeze(2).to_broadcast([P, EXPERTS, PARTS - 1]),
                                    steps[:], ALU.is_gt), 2)
            table(dve.tensor_reduce(tiles[:], over[:], AX_X, ALU.add), 3)
            table(dve.tensor_scalar(tiles[:], tiles[:], 1.0, None, ALU.add), 4)
            shape = [P, EXPERTS + 1, EXPERTS]
            table(dve.tensor_tensor(earlier[:], number[:].unsqueeze(2).to_broadcast(shape),
                                    number[:, 0:EXPERTS].unsqueeze(1).to_broadcast(shape), ALU.is_gt), 5)
            table(dve.tensor_tensor(earlier[:], earlier[:], tiles[:].unsqueeze(1).to_broadcast(shape),
                                    ALU.mult), 6)
            table(dve.tensor_reduce(start_f[:], earlier[:], AX_X, ALU.add), 7)
            table(dve.tensor_scalar(skip[:], tiles[:], -float(TOK), float(REGION), ALU.mult, ALU.add), 8)
            shape = [P, MAX_TILES + 1, EXPERTS]
            table(dve.tensor_tensor(begun[:], tile_number[:].unsqueeze(2).to_broadcast(shape),
                                    start_f[:, 1:].unsqueeze(1).to_broadcast(shape), ALU.is_ge), 9)
            table(dve.tensor_tensor(begun[:], begun[:], skip[:].unsqueeze(1).to_broadcast(shape), ALU.mult), 10)
            table(dve.tensor_reduce(tile_row[:], begun[:], AX_X, ALU.add), 11)
            table(dve.scalar_tensor_tensor(out=tile_row[:], in0=tile_number[:], scalar=float(TOK),
                                           in1=tile_row[:], op0=ALU.mult, op1=ALU.add), 12)
            dve.tensor_copy(tables["tile_row"][:], tile_row[:]).then_inc(table_ready, 1)
            dve.tensor_copy(tables["tile_start"][:], start_f[:]).then_inc(table_ready, 1)
            dve.tensor_copy(tables["row_end"][:], taken[:]).then_inc(table_ready, 1)
            dve.wait_ge(table_ready, 3)


def experts(nc, dram, tables):
    with ExitStack() as ctx:
        sb = lambda n, s, d: ctx.enter_context(nc.sbuf_tensor(n, s, d))
        pb = lambda n, s, d: ctx.enter_context(nc.psum_tensor(n, s, d))
        sem = lambda n: ctx.enter_context(nc.semaphore(n))

        w = [sb(f"w{k}", [P, 2, UNITS * 512], BF16) for k in range(2)]
        b13 = [sb(f"b13_{k}", [P, 2, MC], F32) for k in range(2)]
        b2 = [sb(f"b2_{k}", [P, D], F32) for k in range(2)]
        rows = sb("rows", [P, TT, ROW], F32)
        meta = sb("meta", [P, TT, ROW - D], F32)
        xt_hi = sb("f_xt_hi", [P, KC, TOK], BF16)
        xt_lo = sb("f_xt_lo", [P, KC, TOK], BF16)
        silu = sb("silu", [P, 2, TOK], F32)
        act_f = sb("act_f", [P, 2, TOK], F32)
        act_hi = sb("act_hi", [P, MC, TOK], BF16)
        act_lo = sb("act_lo", [P, MC, TOK], BF16)
        y_sum = sb("y_sum", [P, TT, D], F32)
        y_out = sb("y_out", [P, TT, D], F32)
        first_pick = sb("first_pick", [P, TT], F32)
        gate = sb("gate", [P, TT], F32)
        token = sb("f_token", [P, TT], U32)
        number = sb("f_number", [P, EXPERTS], F32)
        hold = sb("f_hold", [P, TT + 1], F32)
        ident = sb("f_ident", [P, P], F32)
        ones = sb("f_ones", [P, P], F32)

        y_bank = [pb(f"y_bank{a}", [P, 512], F32) for a in range(TT)]
        h1_bank = [pb(f"h1_bank{k}", [P, TOK], F32) for k in range(2)]
        h3_bank = [pb(f"h3_bank{k}", [P, TOK], F32) for k in range(2)]
        x_bank = [h1_bank[0], h3_bank[0]]

        const = sem("f_const")
        w_loaded = [sem(f"w_loaded{k}") for k in range(2)]
        padded = sem("padded")
        expert_done = sem("expert_done")
        rows_loaded = sem("rows_loaded")
        rows_free = sem("rows_free")
        xt_ready = sem("f_xt_ready")
        xt_hi_ready = sem("f_xt_hi_ready")
        xt_lo_ready = sem("f_xt_lo_ready")
        h_ready = sem("h_ready")
        silu_ready = sem("silu_ready")
        g_ready = sem("g_ready")
        g_hi_ready = sem("g_hi_ready")
        g_lo_ready = sem("g_lo_ready")
        gate_ready = sem("gate_ready")
        y_ready = sem("y_ready")
        y_read = sem("y_read")
        y_scaled = sem("y_scaled")
        y_scattered = sem("y_scattered")
        tile_out = sem("tile_out")
        GATE_STEPS = 4
        LOADS = 4

        block = ctx.enter_context(nc.Block())

        def bounds(engine, e):
            return [engine.value_load(tables["tile_start"][0:1, bass.ds(e + n, 1)], min_val=0, max_val=MAX_TILES)
                    for n in range(2)]

        def every_tile(engine, start, tile, end=None):
            with engine.Fori(0, EXPERTS // 2) as i:
                for k in range(2):
                    e = i * 2 + k
                    first, last = bounds(engine, e)
                    start(e, i, k)
                    with engine.Fori(first, last) as T:
                        tile(T, e, i, k, first)
                    if end:
                        end(last)

        def nothing(e, i, k):
            pass

        @block.sync
        def _(sp):
            def pad(e):
                end = sp.value_load(tables["row_end"][0:1, bass.ds(e, 1)], min_val=0, max_val=EXPERTS * REGION)
                sp.dma_start(dram["rows"][bass.ds(end, TOK)].rearrange("(a p) d -> p a d", p=P),
                             tables["padding"][:]).then_inc(padded, 16)

            def load_rows(at):
                sp.dma_start(rows[:], dram["rows"][bass.ds(at, TOK)].rearrange("(a p) d -> p a d", p=P))\
                    .then_inc(rows_loaded, 16)

            def load_weights(e, i, k):
                sp.wait_ge(expert_done, e + 1)
                halves = [dram["experts"][e][:, h].rearrange("p u n -> p (u n)") for h in range(2)]
                sp.dma_start(w[k][:, 0], halves[0]).then_inc(w_loaded[k], 16)
                pad(e + 1)
                sp.dma_start(b13[k][:], dram["bias13"][e]).then_inc(w_loaded[k], 16)
                sp.dma_start(b2[k][:], dram["bias2"][e].partition_broadcast(P)).then_inc(w_loaded[k], 16)
                sp.wait_ge(padded, e * 16 + 32)
                sp.dma_start(w[k][:, 1], halves[1]).then_inc(w_loaded[k], 16)

            def next_rows(T, e, i, k, first):
                at = sp.value_load(tables["tile_row"][0:1, bass.ds(T + 1, 1)], min_val=0,
                                   max_val=EXPERTS * REGION)
                sp.wait_ge(rows_free, T + 2)
                load_rows(at)

            pad(0)
            sp.wait_ge(padded, 16)
            load_rows(0)
            every_tile(sp, load_weights, next_rows)

        @block.gpsimd
        def _(pool):
            pool.memset(ones[:], 1.0).then_inc(const, 1)
            pool.wait_ge(const, 1)
            pool.affine_select(out=ident[:], in_=ones[:], compare_op=ALU.is_equal, fill=0.0, base=0,
                               pattern=[[-1, P]], channel_multiplier=1).then_inc(const, 1)
            pool.iota(number[:], pattern=[[1, EXPERTS]], base=0, channel_multiplier=0,
                      allow_small_or_imprecise_dtypes=True).then_inc(const, 1)
            pool.sem_inc(g_lo_ready, 2)

            def tile(T, e, i, k, first):
                for m in range(MC):
                    pool.wait_ge(g_hi_ready, T * MC + m + 1)
                    pool.tensor_tensor(act_lo[:, m, :], act_f[:, m % 2, :], act_hi[:, m, :],
                                       ALU.subtract).then_inc(g_lo_ready, 1)
                for a in range(TT):
                    pool.wait_ge(y_scaled, T * TT + a + 1)
                    pool.tensor_tensor(hold[:, a:a + 1], ones[:, 0:1], ones[:, 0:1], ALU.subtract)
                    pool.indirect_dma_start(
                        out=dram["y"], out_offset=bass.IndirectOffsetOnAxis(ap=token[:, a:a + 1], axis=0),
                        in_=y_out[:, a, :], in_offset=None, compute_op=ALU.add).then_inc(y_scattered, 16)
                pool.wait_ge(y_scattered, T * (16 * TT) + 16 * TT)
                pool.tensor_tensor(hold[:, TT:TT + 1], ones[:, 0:1], ones[:, 0:1], ALU.subtract)\
                    .then_inc(tile_out, 1)

            every_tile(pool, nothing, tile)

        @block.tensor
        def _(pe):
            def turn(T):
                pe.wait_ge(rows_loaded, T * 16 + 16)
                for c in range(KC):
                    for a in range(TT):
                        ins = pe.transpose(x_bank[c][:, a * P:(a + 1) * P], rows[:, a, c * P:(c + 1) * P], ident[:])
                    ins.then_inc(xt_ready, 1)

            def tile(T, e, i, k, first):
                pe.wait_ge(w_loaded[k], (i + 1) * (16 * LOADS))
                pe.wait_ge(xt_lo_ready, T * KC + KC)
                for m in range(MC):
                    pe.wait_ge(g_ready, T * MC + m + 1)
                    for kind, out in ((0, h1_bank), (1, h3_bank)):
                        for c in range(KC):
                            at = (2 * kind + c) * 512 + m * P
                            ins = halves_matmul(pe, out[m % 2][:], (w[k][:, 0, at:at + P], w[k][:, 1, at:at + P]),
                                                (xt_hi[:, c, :], xt_lo[:, c, :]), c == 0, c == KC - 1)
                    ins.then_inc(h_ready, 1)
                pe.wait_ge(g_ready, T * MC + 5)
                turn(T + 1)
                for m in range(MC):
                    pe.wait_ge(g_lo_ready, T * MC + m + 3)
                    for a in range(TT):
                        if m == 0:
                            pe.wait_ge(y_read, T * TT + a + 1)
                        tok = slice(a * P, (a + 1) * P)
                        at = 4 * 512 + m * D
                        ins = halves_matmul(pe, y_bank[a][:, 0:D], (act_hi[:, m, tok], act_lo[:, m, tok]),
                                            (w[k][:, 0, at:at + D], w[k][:, 1, at:at + D]), m == 0, m == MC - 1)
                        if m == MC - 1:
                            ins.then_inc(y_ready, 1)

            pe.wait_ge(const, 3)
            turn(0)
            every_tile(pe, nothing, tile)

        @block.scalar
        def _(act):
            def high(T):
                for c in range(KC):
                    act.wait_ge(xt_ready, T * KC + c + 1)
                    act.copy(xt_hi[:, c, :], x_bank[c][:]).then_inc(xt_hi_ready, 1)

            def tile(T, e, i, k, first):
                for m in range(MC):
                    act.wait_ge(h_ready, T * MC + m + 1)
                    act.activation(silu[:, m % 2, :], h1_bank[m % 2][:], ACT.Silu,
                                   bias=b13[k][:, 0, m:m + 1]).then_inc(silu_ready, 1)
                    act.wait_ge(g_ready, T * MC + m + 3)
                    act.copy(act_hi[:, m, :], act_f[:, m % 2, :]).then_inc(g_hi_ready, 1)
                high(T + 1)
                act.wait_ge(gate_ready, T * GATE_STEPS + GATE_STEPS)
                for a in range(TT):
                    act.wait_ge(y_read, T * TT + TT + a + 1)
                    act.activation(y_out[:, a, :], y_sum[:, a, :], ACT.Copy,
                                   scale=gate[:, a:a + 1]).then_inc(y_scaled, 1)

            high(0)
            every_tile(act, nothing, tile)

        @block.vector
        def _(dve):
            def low(T):
                for c in range(KC):
                    dve.wait_ge(xt_hi_ready, T * KC + c + 1)
                    dve.tensor_tensor(xt_lo[:, c, :], x_bank[c][:], xt_hi[:, c, :], ALU.subtract)\
                        .then_inc(xt_lo_ready, 1)
                dve.tensor_copy(meta[:], rows[:, :, D:ROW]).then_inc(rows_free, 1)

            def tile(T, e, i, k, first):
                for m in range(MC):
                    dve.wait_ge(silu_ready, T * MC + m + 1)
                    dve.wait_ge(g_lo_ready, T * MC + m + 1)
                    dve.scalar_tensor_tensor(out=act_f[:, m % 2, :], in0=h3_bank[m % 2][:],
                                             scalar=b13[k][:, 1, m:m + 1], in1=silu[:, m % 2, :],
                                             op0=ALU.add, op1=ALU.mult).then_inc(g_ready, 1)
                dve.wait_ge(rows_free, T + 2)
                dve.wait_ge(tile_out, T + 1)
                dve.tensor_copy(token[:], meta[:, :, 3]).then_inc(gate_ready, 1)
                dve.tensor_scalar(first_pick[:], meta[:, :, 2], number[:, bass.ds(e, 1)], None,
                                  ALU.is_equal).then_inc(gate_ready, 1)
                dve.wait_ge(gate_ready, T * GATE_STEPS + 2)
                dve.tensor_tensor(first_pick[:], first_pick[:], meta[:, :, 1], ALU.mult).then_inc(gate_ready, 1)
                dve.wait_ge(gate_ready, T * GATE_STEPS + 3)
                dve.tensor_tensor(gate[:], first_pick[:], meta[:, :, 0], ALU.add).then_inc(gate_ready, 1)
                dve.wait_ge(gate_ready, T * GATE_STEPS + 4)
                low(T + 1)
                for a in range(TT):
                    dve.wait_ge(y_ready, T * TT + a + 1)
                    dve.tensor_tensor(y_sum[:, a, :], y_bank[a][:, 0:D], b2[k][:], ALU.add).then_inc(y_read, 1)

            def end(last):
                dve.wait_ge(y_read, last * TT + TT)
                dve.sem_inc(expert_done, 1)

            dve.sem_inc(expert_done, 2)
            dve.sem_inc(rows_free, 1)
            dve.sem_inc(tile_out, 1)
            dve.sem_inc(g_ready, 2)
            dve.sem_inc(y_read, TT)
            dve.wait_ge(const, 3)
            low(0)
            every_tile(dve, nothing, tile, end)


def build(nc, ins, out):
    NB = 16
    tokens = lambda a: a.rearrange("b s d -> (b s) d").rearrange("(q a p) d -> q p a d", a=TT, p=P)
    scratch = lambda n, s, d: nc.dram_tensor(n, s, d, kind="Internal").ap()
    dram = dict(ins)
    dram["x"] = tokens(ins["x"])
    dram["x1"] = tokens(out[0:TOKENS].rearrange("(b s) d -> b s d", b=2 * NB))
    dram["y"] = out
    dram["rows"] = scratch("expert_rows", [EXPERTS * REGION + TOK, ROW], F32)
    qk = scratch("qk_scratch", [2, 4, D, TOK], BF16)
    dram["qk"] = qk.rearrange("b s (c p) n -> b c p s n", p=P)
    dram["qk_by_row"] = qk.rearrange("b s (h j) n -> b s j h n", j=DH)
    dram["experts"] = scratch("experts_scratch", [EXPERTS, P, 2, UNITS, 512], BF16)
    with ExitStack() as ctx:
        width = 4 * KC * D
        wq_sb = {h: ctx.enter_context(nc.sbuf_tensor(f"proj_{h}", [P, width], BF16)) for h in ("hi", "lo")}
        split_projections(nc, dram, wq_sb)
        attention(nc, dram, wq_sb, NB)
    with ExitStack() as ctx:
        tables = {n: ctx.enter_context(nc.sbuf_tensor(n, [P, EXPERTS + 1], I32))
                  for n in ("row_end", "tile_start")}
        tables["tile_row"] = ctx.enter_context(nc.sbuf_tensor("tile_row", [P, MAX_TILES + 1], I32))
        tables["padding"] = ctx.enter_context(nc.sbuf_tensor("padding", [P, TT, ROW], F32))
        route(nc, dram, tables, NB)
        experts(nc, dram, tables)


def lay_out(inputs):
    import numpy as np

    def arr(name):
        return np.asarray(inputs[name])

    def rows(w):
        w = np.swapaxes(w, -1, -2)
        w = w.reshape(w.shape[:-2] + (w.shape[-2] // P, P, w.shape[-1]))
        return np.ascontiguousarray(np.swapaxes(w, -2, -3))

    a = {"x": arr("x")}
    a["ctx"] = np.ascontiguousarray(arr("ctx_1024").reshape(16, TOK, KC, P).transpose(0, 3, 2, 1))
    a["w_qkvo"] = np.concatenate([rows(arr(f"L0_xattn_w{n}")).reshape(P, KC * D) for n in "qkvo"], axis=1)
    a["bias_qk"] = np.ascontiguousarray(
        np.stack([arr("L0_xattn_bq"), arr("L0_xattn_bk")]).reshape(2, KC, P).transpose(2, 0, 1))
    a["bias_v"] = arr("L0_xattn_bv")
    a["bias_o"] = arr("L0_xattn_bo")
    a["wg"] = rows(arr("L0_ffn_Wg"))
    units = [rows(arr(f"L0_ffn_W{n}")).reshape(EXPERTS, P, 2, 512) for n in "132"]
    a["w_units"] = np.concatenate(units, axis=2)
    fa = {n: arr(f"L0_ffn_A{n}") for n in "132"}
    fb = {n: np.swapaxes(arr(f"L0_ffn_B{n}"), 1, 2) for n in "132"}
    a["lora"] = np.ascontiguousarray(np.stack([
        np.concatenate([fa["1"], fa["3"][:, :, :P], fb["1"], fb["3"]], axis=2),
        np.concatenate([fa["3"][:, :, P:], fa["2"], fb["3"], fb["2"]], axis=2)], axis=1))
    a["bias13"] = np.ascontiguousarray(
        np.stack([arr("L0_ffn_b1"), arr("L0_ffn_b3")]).reshape(2, EXPERTS, MC, P).transpose(1, 3, 0, 2))
    a["bias2"] = arr("L0_ffn_b2")
    return a


def kernel(**inputs):
    import concourse.bacc as bacc
    from concourse.bass_utils import run_bass_kernel_spmd

    nc = bacc.Bacc("TRN2", target_bir_lowering=False, num_devices=1)
    arrays = lay_out(inputs)
    ins = {n: nc.dram_tensor(f"in_{n}", a.shape, mybir.dt.from_np(a.dtype), kind="ExternalInput").ap()
           for n, a in arrays.items()}
    shape = tuple(inputs["x"].shape)
    out = nc.dram_tensor("out_y", [TOKENS + TOK, D], F32, kind="ExternalOutput").ap()
    build(nc, ins, out)
    r = run_bass_kernel_spmd(nc, [{f"in_{n}": a for n, a in arrays.items()}], core_ids=[0])
    return r.results[0]["out_y"][:TOKENS].reshape(shape)
```
